# Optimizing a Trainium2 kernel written in Bass

```python
import numpy as np
import jax
import jax.numpy as jnp

def _softmax(x, axis=-1):
    return jax.nn.softmax(x, axis=axis)

def _gelu(x):
    return jax.nn.gelu(x, approximate=True)

def _silu(x):
    return jax.nn.silu(x)

def _sigmoid(x):
    return jax.nn.sigmoid(x)

def _layernorm(x, axis=-1, eps=1e-05):
    m = jnp.mean(x, axis=axis, keepdims=True)
    v = jnp.var(x, axis=axis, keepdims=True)
    return (x - m) / jnp.sqrt(v + eps)

def _scatter_add(tgt, idx, src, axis=0):
    return tgt.at[idx].add(src)

def _segment_sum(src, seg, n):
    return jax.ops.segment_sum(src, seg, n)
kernel_name = 'mk_decoder_preln_d1_seqx_r2_cf3ec0'

def setup_inputs(seed: int=0):
    np.random.seed(seed)
    _w = jnp.asarray

    def _rec_inputs():
        import jax
        import jax.numpy as jnp
        _rk = jax.random.key(seed)
        x = -0.0002928 + 1 * jax.random.normal(jax.random.fold_in(_rk, 1), (16, 256, 512), jnp.float32)
        _lenS = 256 - jax.random.randint(jax.random.fold_in(_rk, 7), (16,), 0, max(1, 256 // 4) + 1, jnp.int32)
        _lenS2 = 256 - jax.random.randint(jax.random.fold_in(_rk, 8), (16,), 0, max(1, 256 // 4) + 1, jnp.int32)
        _ctx_1024P = jax.random.normal(jax.random.fold_in(_rk, 11), (16, 16, 512), jnp.float32)
        _ctx_1024c = jax.random.dirichlet(jax.random.fold_in(_rk, 511), 0.3 * jnp.ones((16,), jnp.float32), (16, 256))
        _ctx_1024t = jnp.einsum('bsk,bkd->bsd', _ctx_1024c, _ctx_1024P)
        _ctx_1024t = _ctx_1024t * jax.lax.rsqrt(jnp.mean(jnp.square(_ctx_1024t)) + 1e-12) * 0.953939
        ctx_1024 = -1.39393e-06 + 0.999914 * (_ctx_1024t + 0.3 * jax.random.normal(jax.random.fold_in(_rk, 611), (16, 256, 512), jnp.float32))
        _validS = jnp.arange(256)[None, :] < _lenS[:, None]
        _validS2 = jnp.arange(256)[None, :] < _lenS2[:, None]
        _causal = jnp.tril(jnp.ones((256, 256), dtype=bool))
        mask_Bx1x1024_ff1 = jnp.where(jnp.ones((16, 1, 512), dtype=bool), 1.0, 0.0).astype(jnp.float32)
        return (x, ctx_1024, mask_Bx1x1024_ff1)
    x, ctx_1024, mask_Bx1x1024_ff1 = _rec_inputs()

    def _L0_attn_setup():
        import jax, jax.numpy as jnp
        import numpy as np
        B, S, D = (4, 1024, 512)
        COMP_RATIO = 4
        TOP_K = 64
        key = jax.random.key(seed)
        ks = jax.random.split(key, 9)
        sd = 1.0 / np.sqrt(D)
        return {'x': jax.random.normal(ks[0], (B, S, D), dtype=jnp.float32), 'Wq': jax.random.normal(ks[1], (D, D), dtype=jnp.float32) * sd, 'bq': jnp.zeros((D,), dtype=jnp.float32), 'Wk': jax.random.normal(ks[2], (D, D), dtype=jnp.float32) * sd, 'bk': jnp.zeros((D,), dtype=jnp.float32), 'Wv': jax.random.normal(ks[3], (D, D), dtype=jnp.float32) * sd, 'bv': jnp.zeros((D,), dtype=jnp.float32), 'Wo': jax.random.normal(ks[4], (D, D), dtype=jnp.float32) * sd, 'bo': jnp.zeros((D,), dtype=jnp.float32)}
    _L0_attn_all = _L0_attn_setup()
    _L0_attn_in = {k: v for k, v in _L0_attn_all.items() if k in ('Wq', 'bq', 'Wk', 'bk', 'Wv', 'bv', 'Wo', 'bo')}
    del _L0_attn_all

    def _L0_xattn_setup():
        import jax, jax.numpy as jnp
        import numpy as np
        import math
        IN_CH = 256
        HEADS = 8
        HEAD_CH = IN_CH // HEADS
        WIN = 4
        B, S = (8, 512)

        def _pad_embed_matrix(embed, seq_len):
            rel_len = seq_len * 2 - 1
            pad = (rel_len - embed.shape[0]) // 2
            return jnp.pad(embed, ((pad, pad), (0, 0)))

        def _skew_relative_to_absolute(t):
            b, h, s, r = t.shape
            t = jnp.pad(t, ((0, 0), (0, 0), (0, 0), (0, 1))).reshape(b, h, s * (r + 1))
            left = r // 2 + 1
            right = -(left + s * (r + 1)) % r
            t = jnp.pad(t, ((0, 0), (0, 0), (left, right)))
            t = t.reshape(b, h, -1, r)
            return t[:, :, 1:s + 1, :s]

        def _skew_absolute_to_relative(t):
            b, h, s, _ = t.shape
            r = 2 * s - 1
            t = jnp.pad(t, ((0, 0), (0, 0), (0, 0), (r - s, 0))).reshape(b, h, s * r)
            right = -(s * r) % (r + 1)
            t = jnp.pad(t, ((0, 0), (0, 0), (0, right)))
            t = t.reshape(b, h, -1, r + 1)
            return t[:, :, :, :r]
        key = jax.random.key(seed)
        ks = jax.random.split(key, 16)
        xav = math.sqrt(6.0 / (IN_CH + IN_CH))
        rel_std = 1.0 / math.sqrt(HEAD_CH)
        return {'query': jax.random.normal(ks[0], (B, IN_CH, S), jnp.float32), 'key': jax.random.normal(ks[1], (B, IN_CH, S), jnp.float32), 'value': jax.random.normal(ks[2], (B, IN_CH, S), jnp.float32), 'mask': jnp.ones((B, 1, S), jnp.float32), 'wq': jax.random.uniform(ks[3], (IN_CH, IN_CH), jnp.float32, -xav, xav), 'bq': jnp.zeros((IN_CH,), jnp.float32), 'wk': jax.random.uniform(ks[4], (IN_CH, IN_CH), jnp.float32, -xav, xav), 'bk': jnp.zeros((IN_CH,), jnp.float32), 'wv': jax.random.uniform(ks[5], (IN_CH, IN_CH), jnp.float32, -xav, xav), 'bv': jnp.zeros((IN_CH,), jnp.float32), 'wo': jax.random.normal(ks[6], (IN_CH, IN_CH), jnp.float32) * 0.02, 'bo': jnp.zeros((IN_CH,), jnp.float32), 'rel_k': jax.random.normal(ks[7], (2 * WIN + 1, HEAD_CH), jnp.float32) * rel_std, 'rel_v': jax.random.normal(ks[8], (2 * WIN + 1, HEAD_CH), jnp.float32) * rel_std}
    _L0_xattn_all = _L0_xattn_setup()
    _L0_xattn_in = {k: v for k, v in _L0_xattn_all.items() if k in ('wq', 'bq', 'wk', 'bk', 'wv', 'bv', 'wo', 'bo', 'rel_k', 'rel_v')}
    del _L0_xattn_all

    def _L0_ffn_setup():
        import jax, jax.numpy as jnp
        import numpy as np
        from jax import lax
        B, N, DIM = (4, 1024, 512)
        HEADS = 8
        NUM_EXPERTS = 8192
        NUM_KEYS = 128
        DIM_KEY = DIM // 2
        DIM_INNER = 2 * DIM
        PK_TOPK = 16
        TOPK = 1
        key = jax.random.key(seed)
        ks = jax.random.split(key, 10)
        s = lambda k, shape, std=0.02: jax.random.normal(k, shape, dtype=jnp.float32) * std
        return {'x': jax.random.normal(ks[0], (B, N, DIM), dtype=jnp.float32), 'Wq': s(ks[1], (DIM_KEY * HEADS * 2, DIM)), 'keys': s(ks[2], (HEADS, NUM_KEYS, 2, DIM_KEY)), 'W_in': s(ks[3], (DIM_INNER, DIM)), 'W_out': s(ks[4], (DIM, DIM_INNER)), 'in_a': s(ks[5], (NUM_EXPERTS, DIM)), 'in_b': s(ks[6], (NUM_EXPERTS, DIM_INNER)), 'out_a': s(ks[7], (NUM_EXPERTS, DIM_INNER)), 'out_b': s(ks[8], (NUM_EXPERTS, DIM))}
    _L0_ffn_all = _L0_ffn_setup()
    _L0_ffn_in = {k: v for k, v in _L0_ffn_all.items() if k in ('Wq', 'keys', 'W_in', 'W_out', 'in_a', 'in_b', 'out_a', 'out_b')}
    del _L0_ffn_all
    return {'x': x, 'ctx_1024': ctx_1024, 'mask_Bx1x1024_ff1': mask_Bx1x1024_ff1, 'L0_attn_Wq': _L0_attn_in['Wq'], 'L0_attn_bq': _L0_attn_in['bq'], 'L0_attn_Wk': _L0_attn_in['Wk'], 'L0_attn_bk': _L0_attn_in['bk'], 'L0_attn_Wv': _L0_attn_in['Wv'], 'L0_attn_bv': _L0_attn_in['bv'], 'L0_attn_Wo': _L0_attn_in['Wo'], 'L0_attn_bo': _L0_attn_in['bo'], 'L0_xattn_wq': _L0_xattn_in['wq'], 'L0_xattn_bq': _L0_xattn_in['bq'], 'L0_xattn_wk': _L0_xattn_in['wk'], 'L0_xattn_bk': _L0_xattn_in['bk'], 'L0_xattn_wv': _L0_xattn_in['wv'], 'L0_xattn_bv': _L0_xattn_in['bv'], 'L0_xattn_wo': _L0_xattn_in['wo'], 'L0_xattn_bo': _L0_xattn_in['bo'], 'L0_xattn_rel_k': _L0_xattn_in['rel_k'], 'L0_xattn_rel_v': _L0_xattn_in['rel_v'], 'L0_ffn_Wq': _L0_ffn_in['Wq'], 'L0_ffn_keys': _L0_ffn_in['keys'], 'L0_ffn_W_in': _L0_ffn_in['W_in'], 'L0_ffn_W_out': _L0_ffn_in['W_out'], 'L0_ffn_in_a': _L0_ffn_in['in_a'], 'L0_ffn_in_b': _L0_ffn_in['in_b'], 'L0_ffn_out_a': _L0_ffn_in['out_a'], 'L0_ffn_out_b': _L0_ffn_in['out_b']}

def reference(x, ctx_1024, mask_Bx1x1024_ff1, L0_attn_Wq, L0_attn_bq, L0_attn_Wk, L0_attn_bk, L0_attn_Wv, L0_attn_bv, L0_attn_Wo, L0_attn_bo, L0_xattn_wq, L0_xattn_bq, L0_xattn_wk, L0_xattn_bk, L0_xattn_wv, L0_xattn_bv, L0_xattn_wo, L0_xattn_bo, L0_xattn_rel_k, L0_xattn_rel_v, L0_ffn_Wq, L0_ffn_keys, L0_ffn_W_in, L0_ffn_W_out, L0_ffn_in_a, L0_ffn_in_b, L0_ffn_out_a, L0_ffn_out_b):
    import jax
    import jax.numpy as jnp

    def _L0_attn_ref(x, Wq, bq, Wk, bk, Wv, bv, Wo, bo):
        import jax, jax.numpy as jnp
        import numpy as np
        B, S, D = (4, 1024, 512)
        COMP_RATIO = 4
        TOP_K = 64
        b, s, d = x.shape
        scale = 1.0 / jnp.sqrt(jnp.asarray(d, x.dtype))
        Q = x @ Wq + bq
        K = x @ Wk + bk
        V = x @ Wv + bv
        raw = jnp.einsum('bqd,bkd->bqk', Q, K) * scale
        causal = jnp.triu(jnp.ones((s, s), dtype=bool), k=1)
        w_scores = jnp.where(causal, jnp.asarray(-jnp.inf, raw.dtype), raw)
        w_attn = jax.nn.softmax(w_scores, axis=-1) @ V
        sc = s // COMP_RATIO
        Kc = K.reshape(b, sc, COMP_RATIO, d).mean(axis=2)
        Vc = V.reshape(b, sc, COMP_RATIO, d).mean(axis=2)
        c_scores = jnp.einsum('bqd,bkd->bqk', Q, Kc) * scale
        c_attn = jax.nn.softmax(c_scores, axis=-1) @ Vc
        top_vals, top_idx = jax.lax.top_k(raw, TOP_K)
        bi = jnp.arange(b)[:, None, None]
        si = jnp.arange(s)[None, :, None]
        sparse = jnp.zeros_like(raw).at[bi, si, top_idx].set(top_vals)
        s_attn = jax.nn.softmax(sparse, axis=-1) @ V
        out = (w_attn + c_attn + s_attn) / 3.0
        return out @ Wo + bo

    def _L0_xattn_ref(query, key, value, mask, wq, bq, wk, bk, wv, bv, wo, bo, rel_k, rel_v):
        import jax, jax.numpy as jnp
        import numpy as np
        import math
        IN_CH = 256
        HEADS = 8
        HEAD_CH = IN_CH // HEADS
        WIN = 4
        B, S = (8, 512)

        def _pad_embed_matrix(embed, seq_len):
            rel_len = seq_len * 2 - 1
            pad = (rel_len - embed.shape[0]) // 2
            return jnp.pad(embed, ((pad, pad), (0, 0)))

        def _skew_relative_to_absolute(t):
            b, h, s, r = t.shape
            t = jnp.pad(t, ((0, 0), (0, 0), (0, 0), (0, 1))).reshape(b, h, s * (r + 1))
            left = r // 2 + 1
            right = -(left + s * (r + 1)) % r
            t = jnp.pad(t, ((0, 0), (0, 0), (left, right)))
            t = t.reshape(b, h, -1, r)
            return t[:, :, 1:s + 1, :s]

        def _skew_absolute_to_relative(t):
            b, h, s, _ = t.shape
            r = 2 * s - 1
            t = jnp.pad(t, ((0, 0), (0, 0), (0, 0), (r - s, 0))).reshape(b, h, s * r)
            right = -(s * r) % (r + 1)
            t = jnp.pad(t, ((0, 0), (0, 0), (0, right)))
            t = t.reshape(b, h, -1, r + 1)
            return t[:, :, :, :r]
        b, c, s = query.shape
        h, hc = (HEADS, HEAD_CH)
        scale = 1.0 / math.sqrt(hc)
        q = jnp.einsum('oi,bis->bos', wq, query) + bq[:, None]
        k = jnp.einsum('oi,bis->bos', wk, key) + bk[:, None]
        v = jnp.einsum('oi,bis->bos', wv, value) + bv[:, None]
        q = q.reshape(b, h, hc, s).transpose(0, 1, 3, 2)
        k = k.reshape(b, h, hc, s).transpose(0, 1, 3, 2)
        v = v.reshape(b, h, hc, s).transpose(0, 1, 3, 2)
        scores = jnp.einsum('bhqd,bhkd->bhqk', q, k) * scale
        emb_k = _pad_embed_matrix(rel_k, s)
        rel_scores = jnp.einsum('bhqd,rd->bhqr', q, emb_k) * scale
        scores = scores + _skew_relative_to_absolute(rel_scores)
        scores = jnp.where(mask[:, None, :, :] == 0.0, -jnp.inf, scores)
        weights = jax.nn.softmax(scores, axis=-1)
        context = jnp.einsum('bhqk,bhkd->bhqd', weights, v)
        emb_v = _pad_embed_matrix(rel_v, s)
        rel_weights = _skew_absolute_to_relative(weights)
        context = context + jnp.einsum('bhqr,rd->bhqd', rel_weights, emb_v)
        context = context.transpose(0, 1, 3, 2).reshape(b, c, s)
        return jnp.einsum('oi,bis->bos', wo, context) + bo[:, None]

    def _L0_ffn_ref(x, Wq, keys, W_in, W_out, in_a, in_b, out_a, out_b):
        import jax, jax.numpy as jnp
        import numpy as np
        from jax import lax
        B, N, DIM = (4, 1024, 512)
        HEADS = 8
        NUM_EXPERTS = 8192
        NUM_KEYS = 128
        DIM_KEY = DIM // 2
        DIM_INNER = 2 * DIM
        PK_TOPK = 16
        TOPK = 1
        b, n, d = x.shape
        q = (x @ Wq.T).reshape(b, n, 2, HEADS, DIM_KEY).transpose(2, 0, 1, 3, 4)
        sim = jnp.einsum('pbnhd,hkpd->pbnhk', q, keys)
        sx, ix = lax.top_k(sim[0], PK_TOPK)
        sy, iy = lax.top_k(sim[1], PK_TOPK)
        all_scores = (sx[..., :, None] + sy[..., None, :]).reshape(b, n, HEADS, PK_TOPK * PK_TOPK)
        all_indices = (ix[..., :, None] * NUM_KEYS + iy[..., None, :]).reshape(b, n, HEADS, PK_TOPK * PK_TOPK)
        scores, pk = lax.top_k(all_scores, TOPK)
        indices = jnp.take_along_axis(all_indices, pk, axis=-1)
        A_in = in_a[indices]
        B_in = in_b[indices]
        A_out = out_a[indices]
        B_out = out_b[indices]
        gate = jax.nn.relu(scores)
        hidden = x @ W_in.T
        lin = jnp.einsum('bnd,bnhkd->bnhk', x, A_in) * gate
        hidden = hidden + jnp.einsum('bnhk,bnhkd->bnd', lin, B_in)
        hidden = jax.nn.gelu(hidden, approximate=False)
        out = hidden @ W_out.T
        lout = jnp.einsum('bnd,bnhkd->bnhk', hidden, A_out) * gate
        out = out + jnp.einsum('bnhk,bnhkd->bnd', lout, B_out)
        return out
    x = x + _L0_attn_ref(_layernorm(x, axis=-1), L0_attn_Wq, L0_attn_bq, L0_attn_Wk, L0_attn_bk, L0_attn_Wv, L0_attn_bv, L0_attn_Wo, L0_attn_bo)
    x = x + _L0_xattn_ref(_layernorm(x, axis=-1), ctx_1024, ctx_1024, mask_Bx1x1024_ff1, L0_xattn_wq, L0_xattn_bq, L0_xattn_wk, L0_xattn_bk, L0_xattn_wv, L0_xattn_bv, L0_xattn_wo, L0_xattn_bo, L0_xattn_rel_k, L0_xattn_rel_v)
    x = x + _L0_ffn_ref(_layernorm(x, axis=-1), L0_ffn_Wq, L0_ffn_keys, L0_ffn_W_in, L0_ffn_W_out, L0_ffn_in_a, L0_ffn_in_b, L0_ffn_out_a, L0_ffn_out_b)
    return x

_drawn_inputs = setup_inputs


def setup_inputs(seed=0):
    import zlib

    import numpy as np

    out = dict(_drawn_inputs(seed))
    spreads = {'L0_attn_bq': (0.0, 0.8),
     'L0_attn_bk': (0.0, 0.8),
     'L0_attn_bv': (0.0, 0.1),
     'L0_attn_bo': (0.0, 0.1),
     'L0_xattn_bq': (0.0, 0.773),
     'L0_xattn_bk': (0.0, 2.0),
     'L0_xattn_bv': (0.0, 0.8),
     'L0_xattn_bo': (0.0, 0.8)}
    factors = {'L0_xattn_rel_k': 8.0,
     'L0_xattn_rel_v': 8.0,
     'L0_ffn_Wq': 6.445,
     'L0_ffn_keys': 6.375,
     'L0_ffn_in_a': 4.668,
     'L0_ffn_in_b': 4.425,
     'L0_ffn_out_a': 4.974,
     'L0_ffn_out_b': 4.713,
     'L0_ffn_W_out': 2.876}
    for name, (base, spread) in spreads.items():
        noise = np.random.default_rng([zlib.crc32(name.encode()), seed]).standard_normal(out[name].shape)
        drawn = base * np.exp(spread * noise) if base else spread * noise
        out[name] = jnp.asarray(drawn.astype(out[name].dtype))
    for name, factor in factors.items():
        out[name] = (out[name] * factor).astype(out[name].dtype)
    return out
```

```python
from contextlib import ExitStack

import concourse.bass as bass
from concourse import mybir

F32 = mybir.dt.float32
BF16 = mybir.dt.bfloat16
U32 = mybir.dt.uint32
ALU = mybir.AluOpType
ACT = mybir.ActivationFunctionType
AX = mybir.AxisListType

P = 128
BANK = 512
NEG = -1.0e30
EPS = 1e-5
QUAD = 32


def self_wait(eng):
    eng.drain()


def layer_norm_stats(nc, dve, rows, stats, moments, tiles, var_ready):
    for t in range(tiles):
        nc.vector.bn_stats(stats[:, t, :], rows[:, t, :])
    self_wait(dve)
    for t in range(tiles):
        nc.vector.bn_aggr(moments[:, t, :], stats[:, t, :])
    self_wait(dve)
    nc.vector.tensor_scalar(moments[:, 0:tiles, 1:2], moments[:, 0:tiles, 1:2], EPS, None,
                            ALU.add).then_inc(var_ready, 1)


def attention_pass(nc, w, x2_dram, x3_dram):
    B, S, D = w["x"].shape
    TT = S // P
    KD = D // P
    COMP = 4
    TOPK = 64
    SCALE = float(D) ** -0.5
    C, L = S, D
    REL, HC = w["rel_k"].shape
    H = C // HC
    CT = C // P
    HPT = P // HC
    QT_N = L // P
    WIN = REL // 2
    BAND = QUAD + 2 * WIN
    SPAN = P + 2 * WIN
    STEPS = H * QT_N
    ROW = STEPS * BAND
    XSCALE = float(HC) ** -0.5
    PROW = L + 2 * WIN
    PSLOTS = 2 * QT_N

    T_XN, T_Q, T_K, T_V, T_RAW = 0, 2, 4, 6, 8
    T_CK, T_CV, T_WT, T_OT, T_CQ, T_REL, T_PT = 10, 12, 14, 16, 18, 20, 21
    T_PB = T_PT + STEPS
    T_CTX = T_PB + 1
    T_JOBS = T_CTX + CT
    S_ATT, S_SCORE = 0, TT
    S_OUT = S_SCORE + STEPS
    S_JOBS = S_OUT + CT
    assert T_JOBS % 2 == 0 and S_JOBS % 2 == 0

    rel_scratch = nc.dram_tensor("rel_scratch", [(P + 1) * ROW], F32, kind="Internal").ap()
    prob_scratch = nc.dram_tensor("prob_scratch", [(P + 1) * ROW], F32, kind="Internal").ap()

    with ExitStack() as ctx:
        def sb(name, shape, dt=F32):
            return ctx.enter_context(nc.sbuf_tensor(name, shape, dt))

        def sem(name):
            return ctx.enter_context(nc.semaphore(name))

        ident = sb("ident", [P, P])
        zeros = sb("zeros", [1, BANK], BF16)
        w_q, w_k, w_v, w_o = (sb(f"w_{n}", [P, KD, D]) for n in "qkvo")
        b_q, b_k, b_v = (sb(f"b_{n}", [P, KD]) for n in "qkv")
        b_o = sb("b_o", [P, D])
        cw_q, cw_k, cw_v, cw_o = (sb(f"cw_{n}", [P, CT, C]) for n in "qkvo")
        cb_q, cb_k, cb_v, cb_o = (sb(f"cb_{n}", [P, CT]) for n in "qkvo")
        cb_qs = sb("cb_qs", [P, CT])
        rel_k4 = sb("rel_k4", [P, HPT * REL])
        rel_v8 = sb("rel_v8", [H * REL, C])
        half = sb("half", [P, TT])
        shares = sb("shares", [P, 3])

        x_in = sb("x_in", [P, TT, D])
        x_bo = sb("x_bo", [P, TT, D])
        c_in = sb("c_in", [P, CT, L])
        mask_in = sb("mask_in", [P, L])
        mask_add = sb("mask_add", [P, L])
        stats = sb("stats", [P, TT, 6])
        mom = sb("mom", [P, TT, 2])
        rstd = sb("rstd", [P, TT])
        xn = sb("xn", [P, TT, D])
        xn_t = sb("xn_t", [P, KD, S])
        q_t = sb("q_t", [P, KD, S])
        k_t = sb("k_t", [P, KD, S])
        v = sb("v", [P, TT, D])
        raw = sb("raw", [P, TT, S])
        causal = sb("causal", [P, TT, S])
        csum = sb("csum", [P, TT, S // COMP])
        left = sb("left", [P, TT, S])
        best = sb("best", [P, TT, 8])
        sparse = sb("sparse", [P, TT, S])
        nmax = sb("nmax", [P, TT, 3])
        sums = sb("sums", [P, TT, 3])
        rsum = sb("rsum", [P, TT, 3])
        e_w = sb("e_w", [P, TT, S])
        e_c = sb("e_c", [P, TT, S // COMP])
        e_s = sb("e_s", [P, TT, S])
        mix = sb("mix", [P, TT, S])
        mix_t = sb("mix_t", [P, TT, S])
        o_t = sb("o_t", [P, KD, S])
        x1 = sb("x1", [P, TT, D])
        x3 = sb("x3", [P, CT, L])
        stats3 = sb("stats3", [P, TT, 6])
        mom3 = sb("mom3", [P, TT, 2])
        rstd3 = sb("rstd3", [P, TT])
        stats2 = sb("stats2", [P, TT, 6])
        mom2 = sb("mom2", [P, TT, 2])
        rstd2 = sb("rstd2", [P, TT])
        qn = sb("qn", [P, CT, L])
        cq = sb("cq", [P, CT, L])
        ck = sb("ck", [P, CT, L])
        cv = sb("cv", [P, QT_N, C])
        rel_pad = sb("rel_pad", [P, STEPS, BAND])
        band = sb("band", [P, 2, QT_N, SPAN])
        scores = sb("scores", [P, 2, L])
        nmx = sb("nmx", [P, STEPS])
        lsum = sb("lsum", [P, STEPS])
        linv = sb("linv", [P, STEPS])
        PSTEP = PROW + P
        probs = sb("probs", [P, PSLOTS * PROW + QT_N * P + QUAD * QT_N])
        prob_t = sb("prob_t", [P, 2, L])
        near = sb("near", [P, STEPS, BAND])
        near_c = sb("near_c", [P, QT_N, H, REL])
        near_t = sb("near_t", [H * REL, L])
        cn = sb("cn", [P, QT_N, C])
        cn_t = sb("cn_t", [P, CT, L])
        x2 = sb("x2", [P, CT, L])

        t_bank = [ctx.enter_context(nc.psum_tensor(f"t_bank{i}", [P, BANK], F32)) for i in range(2)]
        s_bank = [ctx.enter_context(nc.psum_tensor(f"s_bank{i}", [P, BANK], F32)) for i in range(2)]
        acc = ctx.enter_context(nc.psum_tensor("acc", [P, QT_N, C], F32))

        weights_in = sem("weights_in")
        consts = sem("consts")
        bias_scaled = sem("bias_scaled")
        x_loaded = sem("x_loaded")
        c_loaded = sem("c_loaded")
        ckv_done = sem("ckv_done")
        mask_loaded = sem("mask_loaded")
        x_used = sem("x_used")
        mask_used = sem("mask_used")
        var_ready = sem("var_ready")
        rstd_ready = sem("rstd_ready")
        xn_ready = sem("xn_ready")
        xbo_ready = sem("xbo_ready")
        causal_ready = sem("causal_ready")
        nmax_ready = sem("nmax_ready")
        sparse_ready = sem("sparse_ready")
        exps_ready = sem("exps_ready")
        mix_ready = sem("mix_ready")
        qn_ready = sem("qn_ready")
        t_filled = sem("t_filled")
        t_emptied = sem("t_emptied")
        s_filled = sem("s_filled")
        s_emptied = sem("s_emptied")
        rel_written = sem("rel_written")
        band_loaded = [sem(f"band_loaded{i}") for i in range(2)]
        exp_done = sem("exp_done")
        near_written = [sem(f"near_written{i}") for i in range(2)]
        near_loaded = sem("near_loaded")
        near_packed = sem("near_packed")
        acc_done = sem("acc_done")
        acc_emptied = sem("acc_emptied")
        cn_ready = sem("cn_ready")
        x2_ready = sem("x2_ready")
        x2_stored = sem("x2_stored")
        x3_ready = sem("x3_ready")
        x3_stored = sem("x3_stored")
        gate = sem("gate")

        weights = [(w_q, w["attn_Wq"]), (w_k, w["attn_Wk"]), (w_v, w["attn_Wv"]), (w_o, w["attn_Wo"]),
                   (cw_q, w["xattn_wqT"]), (cw_k, w["xattn_wkT"]), (cw_v, w["xattn_wvT"]),
                   (cw_o, w["xattn_woT"])]
        columns = [(b_q, w["attn_bq"]), (b_k, w["attn_bk"]), (b_v, w["attn_bv"]),
                   (cb_q, w["xattn_bq"]), (cb_k, w["xattn_bk"]), (cb_v, w["xattn_bv"]),
                   (cb_o, w["xattn_bo"])]
        N_WEIGHT_DMAS = len(weights) + len(columns) + 1 + HPT + H
        N_CONSTS = 8

        def prob_tile(slot):
            return probs[:, slot * PROW + WIN:slot * PROW + WIN + L]

        block = ctx.enter_context(nc.Block())

        @block.sync
        def _(sp):
            for tile, src in weights:
                sp.dma_start(tile[:], src.rearrange("(k p) n -> p k n", p=P)).then_inc(weights_in, 16)
            for tile, src in columns:
                sp.dma_start(tile[:], src).then_inc(weights_in, 16)
            sp.dma_start(b_o[:], w["attn_bo"].partition_broadcast(P)).then_inc(weights_in, 16)
            sp.wait_ge(consts, N_CONSTS)
            for h in range(HPT):
                sp.dma_start(rel_k4[h * HC:(h + 1) * HC, h * REL:(h + 1) * REL],
                             w["rel_kT"]).then_inc(weights_in, 16)
            for h in range(H):
                sp.dma_start(rel_v8[h * REL:(h + 1) * REL, h * HC:(h + 1) * HC],
                             w["rel_v"]).then_inc(weights_in, 16)

            with sp.Fori(0, B) as b:
                sp.wait_ge(t_emptied, b * T_JOBS + T_REL + 1)
                sp.wait_ge(band_loaded[0], b * (H // 2) * 64)
                sp.wait_ge(band_loaded[1], b * (H // 2) * 64)
                sp.dma_start(rel_scratch[0:P * ROW].rearrange("(p n) -> p n", p=P),
                             rel_pad[:].rearrange("p s w -> p (s w)")).then_inc(rel_written, 16)
                sp.wait_ge(rel_written, b * 16 + 16)
                sp.sem_inc(gate, 1)

                def load_band(h):
                    for g in range(P // QUAD):
                        base = g * QUAD * ROW + h * QT_N * BAND
                        src = rel_scratch[base:base + QUAD * (ROW - 1)].rearrange("(r c) -> r c", c=ROW - 1)
                        src = src[:, 0:QT_N * BAND].rearrange("r (t w) -> r t w", w=BAND)
                        sp.dma_start(band[g * QUAD:(g + 1) * QUAD, h % 2, :, g * QUAD:g * QUAD + BAND],
                                     src).then_inc(band_loaded[h % 2], 16)

                sp.wait_ge(s_filled, b * S_JOBS)
                load_band(0)
                load_band(1)
                sp.wait_ge(near_loaded, b * 64)
                for h in range(H):
                    sp.wait_ge(exp_done, b * STEPS + (h + 1) * QT_N)
                    for g in range(P // QUAD):
                        at = (h % 2) * QT_N * PROW + g * QUAD
                        src = probs[g * QUAD:(g + 1) * QUAD, at:at + QT_N * PSTEP]
                        src = src.rearrange("r (t c) -> r t c", c=PSTEP)[:, :, 0:BAND]
                        dst = prob_scratch[g * QUAD * ROW:(g + 1) * QUAD * ROW]
                        dst = dst.rearrange("(r s w) -> r s w", r=QUAD, w=BAND)[:, h * QT_N:(h + 1) * QT_N, :]
                        sp.dma_start(dst, src).then_inc(near_written[h % 2], 16)
                    if h + 2 < H:
                        sp.wait_ge(s_filled, b * S_JOBS + S_SCORE + (h + 1) * QT_N)
                        load_band(h + 2)
                sp.wait_ge(near_written[0], (b + 1) * (H // 2) * 64)
                sp.wait_ge(near_written[1], (b + 1) * (H // 2) * 64)
                for g in range(P // QUAD):
                    base = g * QUAD * ROW
                    src = prob_scratch[base:base + QUAD * (ROW + 1)].rearrange("(r c) -> r c", c=ROW + 1)
                    n = ROW - QUAD + 1
                    sp.dma_start(near[g * QUAD:(g + 1) * QUAD, :, :].rearrange("r s w -> r (s w)")[:, 0:n],
                                 src[:, 0:n]).then_inc(near_loaded, 16)
                sp.wait_ge(x2_ready, b + 1)
                sp.sem_inc(gate, 1)
                sp.dma_start(x2_dram[bass.ds(b * S, S), :].rearrange("(t p) n -> p t n", p=P),
                             x2[:]).then_inc(x2_stored, 16)
                sp.wait_ge(x3_ready, b + 1)
                sp.sem_inc(gate, 1)
                sp.dma_start(x3_dram[bass.ds(b * S, S), :].rearrange("(t p) n -> p t n", p=P),
                             x3[:]).then_inc(x3_stored, 16)
            sp.wait_ge(x2_stored, B * 16)
            sp.wait_ge(x3_stored, B * 16)

        @block.gpsimd
        def _(pool):
            def after(ins):
                ins.then_inc(consts, 1)
            nc.gpsimd.memset(ident[:], 0.0)
            nc.gpsimd.drain()
            after(nc.gpsimd.affine_select(out=ident[:], in_=ident[:], compare_op=ALU.not_equal, fill=1.0,
                                          base=0, pattern=[[-1, P]], channel_multiplier=1))
            after(nc.gpsimd.memset(rel_k4[:], 0.0))
            after(nc.gpsimd.memset(rel_v8[:], 0.0))
            after(nc.gpsimd.memset(half[:], -0.5))
            after(nc.gpsimd.memset(zeros[:], 0.0))
            after(nc.gpsimd.memset(rel_pad[:], 0.0))
            after(nc.gpsimd.memset(band[:], 0.0))
            after(nc.gpsimd.memset(probs[:], 0.0))

            pool.wait_ge(weights_in, 16 * N_WEIGHT_DMAS)

            def load(b):
                pool.wait_ge(x_used, b)
                nc.gpsimd.sem_inc(gate, 1)
                pool.dma_start(x_in[:], w["x"][b].rearrange("(t p) n -> p t n", p=P)).then_inc(x_loaded, 16)
                pool.wait_ge(mask_used, b)
                nc.gpsimd.sem_inc(gate, 1)
                pool.dma_start(mask_in[:], w["mask"][b].partition_broadcast(P)).then_inc(mask_loaded, 16)
                pool.wait_ge(ckv_done, b)
                nc.gpsimd.sem_inc(gate, 1)
                pool.dma_start(c_in[:], w["ctx"][b].rearrange("(t p) n -> p t n", p=P)).then_inc(c_loaded, 16)

            def prepare(b, last):
                pool.wait_ge(var_ready, 3 * b + 1)
                nc.gpsimd.tensor_tensor(rstd[:], mom[:, :, 1], half[:], ALU.pow).then_inc(rstd_ready, 1)
                pool.wait_ge(x_loaded, 16 * b + 16)
                pool.wait_ge(s_emptied, b * S_JOBS)
                for t in range(TT):
                    ins = nc.gpsimd.tensor_tensor(x_bo[:, t, :], x_in[:, t, :], b_o[:], ALU.add)
                ins.then_inc(xbo_ready, 1)
                for t in range(TT):
                    pool.wait_ge(t_emptied, b * T_JOBS + T_RAW + t + 1)
                    nc.gpsimd.sem_inc(gate, 1)
                    nc.gpsimd.affine_select(out=causal[:, t, :], in_=raw[:, t, :], compare_op=ALU.is_ge,
                                            fill=NEG, base=t * P, pattern=[[-1, S]],
                                            channel_multiplier=1).then_inc(causal_ready, 1)
                pool.wait_ge(var_ready, 3 * b + 2)
                nc.gpsimd.tensor_tensor(rstd2[:], mom2[:, :, 1], half[:], ALU.pow).then_inc(rstd_ready, 1)
                if not last:
                    load(b + 1)
                pool.wait_ge(var_ready, 3 * b + 3)
                nc.gpsimd.tensor_tensor(rstd3[:], mom3[:, :, 1], half[:], ALU.pow).then_inc(rstd_ready, 1)

            load(0)
            with pool.Fori(0, B - 1) as b:
                prepare(b, last=False)
            prepare(B - 1, last=True)

        @block.tensor
        def _(pe):
            pe.wait_ge(consts, N_CONSTS)
            pe.wait_ge(weights_in, 16 * N_WEIGHT_DMAS)
            with pe.Fori(0, B) as b:
                def t_open(n):
                    pe.wait_ge(t_emptied, b * T_JOBS + max(n - 1, 0))
                    return t_bank[n % 2]

                def s_open(n):
                    pe.wait_ge(s_emptied, b * S_JOBS + max(n - 1, 0))
                    return s_bank[n % 2]

                def t_evacuated(n):
                    pe.wait_ge(t_emptied, b * T_JOBS + n + 1)

                def product(out, lhs, rhs, k_tiles):
                    for k in range(k_tiles):
                        ins = nc.tensor.matmul(out, lhs(k), rhs(k), start=(k == 0), stop=(k == k_tiles - 1))
                    return ins

                for t in range(TT):
                    bank = t_open(T_XN + t)
                    pe.wait_ge(xn_ready, b * TT + t + 1)
                    for k in range(KD):
                        ins = nc.tensor.transpose(bank[:, k * P:(k + 1) * P], xn[:, t, k * P:(k + 1) * P], ident[:])
                    ins.then_inc(t_filled, 1)
                t_evacuated(T_XN + TT - 1)
                for job, wt in ((T_Q, w_q), (T_K, w_k)):
                    for m2 in range(KD // 2):
                        bank = t_open(job + m2)
                        for j in range(2):
                            m = 2 * m2 + j
                            ins = product(bank[:, j * S:(j + 1) * S], lambda k: wt[:, k, m * P:(m + 1) * P],
                                          lambda k: xn_t[:, k, :], KD)
                        ins.then_inc(t_filled, 1)
                for t in range(TT):
                    bank = t_open(T_V + t)
                    product(bank[:, 0:D], lambda k: xn_t[:, k, t * P:(t + 1) * P], lambda k: w_v[:, k, :],
                            KD).then_inc(t_filled, 1)
                for t in range(TT):
                    bank = t_open(T_RAW + t)
                    t_evacuated(T_K + KD // 2 - 1)
                    product(bank[:, 0:S], lambda k: q_t[:, k, t * P:(t + 1) * P], lambda k: k_t[:, k, :],
                            KD).then_inc(t_filled, 1)
                pe.wait_ge(c_loaded, 16 * b + 16)
                for o in range(CT):
                    bank = t_open(T_CK + o)
                    product(bank[:, 0:L], lambda k: cw_k[:, k, o * P:(o + 1) * P], lambda k: c_in[:, k, :],
                            CT).then_inc(t_filled, 1)
                for s2 in range(QT_N // 2):
                    bank = t_open(T_CV + s2)
                    for j in range(2):
                        s = 2 * s2 + j
                        ins = product(bank[:, j * C:(j + 1) * C], lambda k: c_in[:, k, s * P:(s + 1) * P],
                                      lambda k: cw_v[:, k, :], CT)
                    ins.then_inc(t_filled, 1)
                t_evacuated(T_CV + QT_N // 2 - 1)
                pe.sem_inc(ckv_done, 1)
                for t in range(TT):
                    bank = t_open(T_WT + t)
                    pe.wait_ge(mix_ready, b * TT + t + 1)
                    for k in range(TT):
                        ins = nc.tensor.transpose(bank[:, k * P:(k + 1) * P], mix[:, t, k * P:(k + 1) * P], ident[:])
                    ins.then_inc(t_filled, 1)
                t_evacuated(T_WT + TT - 1)
                for m2 in range(KD // 2):
                    bank = t_open(T_OT + m2)
                    for j in range(2):
                        m = 2 * m2 + j
                        ins = product(bank[:, j * S:(j + 1) * S], lambda k: v[:, k, m * P:(m + 1) * P],
                                      lambda k: mix_t[:, k, :], TT)
                    ins.then_inc(t_filled, 1)
                t_evacuated(T_OT + KD // 2 - 1)
                for t in range(TT):
                    bank = s_open(S_ATT + t)
                    product(bank[:, 0:D], lambda k: o_t[:, k, t * P:(t + 1) * P], lambda k: w_o[:, k, :],
                            KD).then_inc(s_filled, 1)

                pe.wait_ge(qn_ready, b + 1)
                for o in range(CT):
                    bank = t_open(T_CQ + o)
                    product(bank[:, 0:L], lambda k: cw_q[:, k, o * P:(o + 1) * P], lambda k: qn[:, k, :],
                            CT).then_inc(t_filled, 1)
                t_evacuated(T_CQ + CT - 1)
                bank = t_open(T_REL)
                n = HPT * REL
                for t in range(QT_N):
                    for o in range(CT):
                        at = (t * CT + o) * n
                        ins = nc.tensor.matmul(bank[:, at:at + n], cq[:, o, t * P:(t + 1) * P], rel_k4[:],
                                               start=True, stop=True)
                ins.then_inc(t_filled, 1)
                pe.wait_ge(acc_emptied, b)
                for j in range(QT_N // 2):
                    nc.tensor.matmul(acc[:, 2 * j:2 * j + 2, :].rearrange("p t c -> p (t c)"),
                                     zeros[:, 0:P], zeros[:], start=True, stop=False, skip_group_check=True)

                def score(n):
                    h, t = divmod(n, QT_N)
                    o, r = divmod(h, HPT)
                    bank = s_open(S_SCORE + n)
                    nc.tensor.matmul(bank[:, 0:L], cq[r * HC:(r + 1) * HC, o, t * P:(t + 1) * P],
                                     ck[r * HC:(r + 1) * HC, o, :], start=True, stop=False,
                                     skip_group_check=True)
                    if t == 0:
                        pe.wait_ge(band_loaded[h % 2], (b * (H // 2) + h // 2 + 1) * 64)
                    lo = max(t * P - WIN, 0)
                    hi = min(t * P + P + WIN, L)
                    off = lo - (t * P - WIN)
                    nc.tensor.matmul(bank[:, lo:hi], ident[:], band[:, h % 2, t, off:off + hi - lo],
                                     start=False, stop=True, skip_group_check=True).then_inc(s_filled, 1)

                def turn(n):
                    bank = t_open(T_PT + n)
                    pe.wait_ge(exp_done, b * STEPS + n + 1)
                    src = prob_tile(n % PSLOTS)
                    for k in range(QT_N):
                        ins = nc.tensor.transpose(bank[:, k * P:(k + 1) * P], src[:, k * P:(k + 1) * P], ident[:])
                    ins.then_inc(t_filled, 1)

                def weigh(n):
                    h, t = divmod(n, QT_N)
                    t_evacuated(T_PT + n)
                    for k in range(QT_N):
                        nc.tensor.matmul(acc[:, t, h * HC:(h + 1) * HC], prob_t[:, n % 2, k * P:(k + 1) * P],
                                         cv[:, k, h * HC:(h + 1) * HC], start=False, stop=False,
                                         skip_group_check=True)

                for s in range(STEPS + 3):
                    if s < STEPS:
                        score(s)
                    if 2 <= s < STEPS + 2:
                        turn(s - 2)
                    if s >= 3:
                        weigh(s - 3)
                bank = t_open(T_PB)
                pe.wait_ge(near_packed, b + 1)
                for t in range(QT_N):
                    ins = nc.tensor.transpose(bank[0:H * REL, t * P:(t + 1) * P],
                                              near_c[:, t, :, :].rearrange("p h j -> p (h j)"), ident[:])
                ins.then_inc(t_filled, 1)
                t_evacuated(T_PB)
                for t in range(QT_N):
                    ins = nc.tensor.matmul(acc[:, t, :], near_t[:, t * P:(t + 1) * P], rel_v8[:],
                                           start=False, stop=(t % 2 == 1), skip_group_check=True)
                ins.then_inc(acc_done, 1)
                pe.wait_ge(cn_ready, b + 1)
                for o in range(CT):
                    bank = t_open(T_CTX + o)
                    for t in range(QT_N):
                        ins = nc.tensor.transpose(bank[:, t * P:(t + 1) * P], cn[:, t, o * P:(o + 1) * P], ident[:])
                    ins.then_inc(t_filled, 1)
                t_evacuated(T_CTX + CT - 1)
                for o in range(CT):
                    bank = s_open(S_OUT + o)
                    product(bank[:, 0:L], lambda k: cw_o[:, k, o * P:(o + 1) * P], lambda k: cn_t[:, k, :],
                            CT).then_inc(s_filled, 1)

        @block.scalar
        def _(act):
            act.wait_ge(weights_in, 16 * N_WEIGHT_DMAS)
            act.wait_ge(consts, N_CONSTS)
            nc.scalar.mul(cb_qs[:], cb_q[:], XSCALE)
            self_wait(act)
            with act.Fori(0, B) as b:
                def t_full(n):
                    act.wait_ge(t_filled, b * T_JOBS + n + 1)
                    return t_bank[n % 2]

                for t in range(TT):
                    bank = t_full(T_XN + t)
                    nc.scalar.copy(xn_t[:, :, t * P:(t + 1) * P],
                                   bank[:].rearrange("p (k n) -> p k n", k=KD)).then_inc(t_emptied, 1)
                for job, dst, bias in ((T_Q, q_t, b_q), (T_K, k_t, b_k)):
                    for m2 in range(KD // 2):
                        bank = t_full(job + m2)
                        for j in range(2):
                            m = 2 * m2 + j
                            ins = nc.scalar.activation(dst[:, m, :], bank[:, j * S:(j + 1) * S], ACT.Identity,
                                                       bias=bias[:, m:m + 1])
                        ins.then_inc(t_emptied, 1)
                for t in range(TT):
                    bank = t_full(T_V + t)
                    nc.scalar.copy(v[:, t, :], bank[:, 0:D]).then_inc(t_emptied, 1)
                for t in range(TT):
                    bank = t_full(T_RAW + t)
                    nc.scalar.mul(raw[:, t, :], bank[:, 0:S], SCALE).then_inc(t_emptied, 1)
                for o in range(CT):
                    bank = t_full(T_CK + o)
                    nc.scalar.activation(ck[:, o, :], bank[:, 0:L], ACT.Identity,
                                         bias=cb_k[:, o:o + 1]).then_inc(t_emptied, 1)
                for s2 in range(QT_N // 2):
                    bank = t_full(T_CV + s2)
                    nc.scalar.copy(cv[:, 2 * s2:2 * s2 + 2, :],
                                   bank[:].rearrange("p (s c) -> p s c", s=2)).then_inc(t_emptied, 1)
                for t in range(TT):
                    act.wait_ge(nmax_ready, b * TT + t + 1)
                    nc.scalar.activation(e_w[:, t, :], causal[:, t, :], ACT.Exp, bias=nmax[:, t, 0:1],
                                         accum_out=sums[:, t, 0:1])
                    nc.scalar.activation(e_c[:, t, :], csum[:, t, :], ACT.Exp, bias=nmax[:, t, 1:2],
                                         scale=1.0 / COMP, accum_out=sums[:, t, 1:2])
                    act.wait_ge(sparse_ready, b * TT + t + 1)
                    nc.scalar.activation(e_s[:, t, :], sparse[:, t, :], ACT.Exp, bias=nmax[:, t, 2:3],
                                         accum_out=sums[:, t, 2:3]).then_inc(exps_ready, 1)
                for t in range(TT):
                    bank = t_full(T_WT + t)
                    nc.scalar.copy(mix_t[:, :, t * P:(t + 1) * P],
                                   bank[:, 0:S].rearrange("p (k n) -> p k n", k=TT)).then_inc(t_emptied, 1)
                for m2 in range(KD // 2):
                    bank = t_full(T_OT + m2)
                    for j in range(2):
                        m = 2 * m2 + j
                        ins = nc.scalar.activation(o_t[:, m, :], bank[:, j * S:(j + 1) * S], ACT.Identity,
                                                   bias=b_v[:, m:m + 1])
                    ins.then_inc(t_emptied, 1)
                for o in range(CT):
                    bank = t_full(T_CQ + o)
                    nc.scalar.activation(cq[:, o, :], bank[:, 0:L], ACT.Identity, bias=cb_qs[:, o:o + 1],
                                         scale=XSCALE).then_inc(t_emptied, 1)
                bank = t_full(T_REL)
                act.wait_ge(rel_written, b * 16)
                ins = nc.scalar.copy(
                    rel_pad[:].rearrange("p (h t) w -> p h t w", t=QT_N)[:, :, :, 0:REL],
                    bank[:, 0:QT_N * H * REL].rearrange("p (t h j) -> p h t j", t=QT_N, j=REL))
                ins.then_inc(t_emptied, 1)
                for n in range(STEPS + 1):
                    if n < STEPS:
                        h = n // QT_N
                        act.wait_ge(s_emptied, b * S_JOBS + S_SCORE + n + 1)
                        if n % QT_N == 0:
                            act.wait_ge(near_written[h % 2], (b * (H // 2) + h // 2) * 64)
                        nc.scalar.activation(prob_tile(n % PSLOTS), scores[:, n % 2, :], ACT.Exp,
                                             bias=nmx[:, n:n + 1], scale=-1.0,
                                             accum_out=lsum[:, n:n + 1]).then_inc(exp_done, 1)
                    if n >= 1:
                        bank = t_full(T_PT + n - 1)
                        nc.scalar.copy(prob_t[:, (n - 1) % 2, :], bank[:]).then_inc(t_emptied, 1)
                bank = t_full(T_PB)
                nc.scalar.copy(near_t[:], bank[0:H * REL, :]).then_inc(t_emptied, 1)
                for o in range(CT):
                    bank = t_full(T_CTX + o)
                    nc.scalar.activation(cn_t[:, o, :], bank[:, 0:L], ACT.Identity,
                                         bias=cb_v[:, o:o + 1]).then_inc(t_emptied, 1)

        @block.vector
        def _(dve):
            for j, share in enumerate((3.0, 3.0 * COMP, 3.0)):
                nc.vector.memset(shares[:, j:j + 1], share)
            dve.wait_ge(weights_in, 16 * N_WEIGHT_DMAS)
            self_wait(dve)
            with dve.Fori(0, B) as b:
                def normalise(dst, src, moments, rs, ready, each):
                    for t in range(TT):
                        ins = nc.vector.tensor_scalar(dst[:, t, :], src[:, t, :], moments[:, t, 0:1],
                                                      rs[:, t:t + 1], ALU.subtract, ALU.mult)
                        if each or t == TT - 1:
                            ins.then_inc(ready, 1)

                dve.wait_ge(x_loaded, 16 * b + 16)
                layer_norm_stats(nc, dve, x_in, stats, mom, TT, var_ready)
                dve.wait_ge(rstd_ready, 3 * b + 1)
                normalise(xn, x_in, mom, rstd, xn_ready, True)
                dve.wait_ge(mask_loaded, 16 * b + 16)
                nc.vector.tensor_scalar(mask_add[:], mask_in[:], 0.0, NEG, ALU.is_equal,
                                        ALU.mult).then_inc(mask_used, 1)
                dve.wait_ge(xbo_ready, b + 1)
                dve.sem_inc(x_used, 1)

                for t in range(TT):
                    dve.wait_ge(t_emptied, b * T_JOBS + T_RAW + t + 1)
                    nc.vector.tensor_reduce(csum[:, t, :], raw[:, t, :].rearrange("p (s c) -> p s c", c=COMP),
                                            AX.X, ALU.add)
                    self_wait(dve)
                    nc.vector.tensor_reduce(nmax[:, t, 1:2], csum[:, t, :], AX.X, ALU.max, negate=True)
                    self_wait(dve)
                    nc.vector.tensor_scalar(nmax[:, t, 1:2], nmax[:, t, 1:2], 1.0 / COMP, None, ALU.mult)
                    dve.wait_ge(causal_ready, b * TT + t + 1)
                    nc.vector.tensor_reduce(nmax[:, t, 0:1], causal[:, t, :], AX.X, ALU.max,
                                            negate=True).then_inc(nmax_ready, 1)
                    for r in range(TOPK // 8):
                        src = raw if r == 0 else left
                        nc.vector.max(best[:, t, :], src[:, t, :])
                        self_wait(dve)
                        if r == 0:
                            nc.vector.tensor_scalar(nmax[:, t, 2:3], best[:, t, 0:1], 0.0, -1.0, ALU.max,
                                                    ALU.mult)
                        nc.vector.match_replace(left[:, t, :], best[:, t, :], src[:, t, :], NEG)
                        self_wait(dve)
                    nc.vector.scalar_tensor_tensor(out=sparse[:, t, :], in0=left[:, t, :], scalar=NEG,
                                                   in1=raw[:, t, :], op0=ALU.is_equal,
                                                   op1=ALU.mult).then_inc(sparse_ready, 1)
                for t in range(TT):
                    dve.wait_ge(exps_ready, b * TT + t + 1)
                    nc.vector.tensor_tensor(rsum[:, t, :], sums[:, t, :], shares[:], ALU.mult)
                    self_wait(dve)
                    nc.vector.reciprocal(rsum[:, t, :], rsum[:, t, :])
                    self_wait(dve)
                    nc.vector.tensor_scalar(mix[:, t, :], e_w[:, t, :], rsum[:, t, 0:1], None, ALU.mult)
                    self_wait(dve)
                    nc.vector.scalar_tensor_tensor(out=mix[:, t, :], in0=e_s[:, t, :], scalar=rsum[:, t, 2:3],
                                                   in1=mix[:, t, :], op0=ALU.mult, op1=ALU.add)
                    self_wait(dve)
                    groups = mix[:, t, :].rearrange("p (s c) -> p s c", c=COMP)
                    nc.vector.scalar_tensor_tensor(
                        out=groups, in0=e_c[:, t, :].unsqueeze(2).to_broadcast([P, S // COMP, COMP]),
                        scalar=rsum[:, t, 1:2], in1=groups, op0=ALU.mult, op1=ALU.add).then_inc(mix_ready, 1)
                for t in range(TT):
                    dve.wait_ge(s_filled, b * S_JOBS + S_ATT + t + 1)
                    nc.vector.tensor_tensor(x1[:, t, :], s_bank[(S_ATT + t) % 2][:, 0:D], x_bo[:, t, :],
                                            ALU.add).then_inc(s_emptied, 1)
                self_wait(dve)
                layer_norm_stats(nc, dve, x1, stats2, mom2, TT, var_ready)
                dve.wait_ge(rstd_ready, 3 * b + 2)
                normalise(qn, x1, mom2, rstd2, qn_ready, False)

                for n in range(STEPS):
                    dve.wait_ge(s_filled, b * S_JOBS + S_SCORE + n + 1)
                    dve.wait_ge(exp_done, b * STEPS + max(n - 1, 0))
                    dve.sem_inc(gate, 1)
                    nc.vector.tensor_tensor_reduce(out=scores[:, n % 2, :], in0=s_bank[(S_SCORE + n) % 2][:, 0:L],
                                                   in1=mask_add[:], scale=-1.0, scalar=-NEG, op0=ALU.add,
                                                   op1=ALU.min, accum_out=nmx[:, n:n + 1]).then_inc(s_emptied, 1)
                dve.wait_ge(exp_done, (b + 1) * STEPS)
                nc.vector.reciprocal(linv[:], lsum[:])
                dve.wait_ge(near_loaded, b * 64 + 64)
                nc.vector.tensor_copy(near_c[:].rearrange("p t h j -> p h t j"),
                                      near[:].rearrange("p (h t) w -> p h t w", t=QT_N)[:, :, :, 0:REL]
                                      ).then_inc(near_packed, 1)
                self_wait(dve)
                dve.wait_ge(acc_done, b + 1)
                for t in range(QT_N):
                    li = linv[:].rearrange("p (h t) -> p h t", t=QT_N)[:, :, t:t + 1].to_broadcast([P, H, HC])
                    ins = nc.vector.tensor_tensor(cn[:, t, :].rearrange("p (h c) -> p h c", h=H),
                                                  acc[:, t, :].rearrange("p (h c) -> p h c", h=H), li, ALU.mult)
                ins.then_inc(cn_ready, 1)
                dve.wait_ge(cn_ready, b + 1)
                dve.sem_inc(acc_emptied, 1)
                for o in range(CT):
                    dve.wait_ge(s_filled, b * S_JOBS + S_OUT + o + 1)
                    dve.wait_ge(x2_stored, 16 * b)
                    nc.vector.scalar_tensor_tensor(out=x2[:, o, :], in0=s_bank[(S_OUT + o) % 2][:, 0:L],
                                                   scalar=cb_o[:, o:o + 1], in1=x1[:, o, :], op0=ALU.add,
                                                   op1=ALU.add).then_inc(s_emptied, 1)
                dve.wait_ge(s_emptied, (b + 1) * S_JOBS)
                dve.sem_inc(x2_ready, 1)
                layer_norm_stats(nc, dve, x2, stats3, mom3, TT, var_ready)
                dve.wait_ge(rstd_ready, 3 * b + 3)
                dve.wait_ge(x3_stored, 16 * b)
                normalise(x3, x2, mom3, rstd3, x3_ready, False)


def expert_pass(nc, w, x2_dram, x3_dram, out):
    N, D = x2_dram.shape
    ROUNDS = N // P
    KD = D // P
    HEADS, KEYS = 8, P
    PH = 2 * HEADS
    DK = w["ffn_Wq"].shape[0] // PH
    KT = DK // P
    E = w["in_a"].shape[0]
    F = w["ffn_W_inT"].shape[1]
    KF = F // P
    SIMS = PH * KEYS
    CHUNKS = SIMS // BANK
    PER = BANK // KEYS
    HALVES = F // BANK
    AB = 4
    assert KEYS * KEYS >= E and HEADS % AB == 0 and DK % P == 0

    with ExitStack() as ctx:
        def sb(name, shape, dt=F32):
            return ctx.enter_context(nc.sbuf_tensor(name, shape, dt))

        def pb(name, shape):
            return ctx.enter_context(nc.psum_tensor(name, shape, F32))

        def sem(name):
            return ctx.enter_context(nc.semaphore(name))

        ident = sb("ident_f", [P, P])
        fold = sb("fold", [P, KD, SIMS])
        w_in = sb("w_in", [P, KD, F])
        w_out = sb("w_out", [P, KF, D])
        wq_in = sb("wq_in", [P, 2, KT, D])
        keys_in = sb("keys_in", [P, 2, KT, KEYS])
        xn_pe = sb("xn_pe", [P, D])
        xn_ve = sb("xn_ve", [P, D])
        x_res = sb("x_res", [P, D])
        xn_t = sb("xn_tf", [P, KD, P])
        sims = sb("sims", [P, SIMS])
        top = sb("top", [P, PH, 8])
        place = sb("place", [P, PH, 8], U32)
        row_f = sb("row_f", [P, HEADS])
        rows = sb("rows", [P, HEADS], U32)
        rows_now = sb("rows_now", [P, HEADS], U32)
        score = sb("score", [P, HEADS])
        gates = sb("gates", [P, HEADS])
        lin = sb("lin", [P, HEADS])
        lout = sb("lout", [P, HEADS])
        in_a = sb("in_a_rows", [P, HEADS, D])
        in_b = sb("in_b_rows", [P, AB, F])
        out_a = sb("out_a_rows", [P, AB, F])
        out_b = sb("out_b_rows", [P, HEADS, D])
        hid = sb("hid", [P, F])
        hid_t = sb("hid_t", [P, KF, P])
        res = sb("res", [P, D])

        x_bank = pb("x_bank", [P, BANK])
        l_bank = [pb(f"l_bank{i}", [P, BANK]) for i in range(2)]
        h_bank = [pb(f"h_bank{i}", [P, BANK]) for i in range(KF * P // BANK)]
        hid_ps = pb("hid_ps", [P, F])
        out_ps = pb("out_ps", [P, D])

        ident_ready = sem("ident_ready")
        ident_zeroed = sem("ident_zeroed")
        w_loaded = sem("w_loaded")
        wq_loaded = [sem(f"wq_loaded{i}") for i in range(2)]
        fold_filled = sem("fold_filled")
        fold_emptied = sem("fold_emptied")
        xpe_loaded = sem("xpe_loaded")
        xve_loaded = sem("xve_loaded")
        xres_loaded = sem("xres_loaded")
        xt_filled = sem("xt_filled")
        xt_emptied = sem("xt_emptied")
        sims_filled = sem("sims_filled")
        sims_emptied = sem("sims_emptied")
        picked = sem("picked")
        rows_taken = sem("rows_taken")
        in_a_loaded = [sem(f"in_a_loaded{i}") for i in range(HEADS)]
        in_b_loaded = [sem(f"in_b_loaded{i}") for i in range(AB)]
        out_a_loaded = [sem(f"out_a_loaded{i}") for i in range(AB)]
        out_b_loaded = [sem(f"out_b_loaded{i}") for i in range(HEADS)]
        in_a_used = sem("in_a_used")
        in_b_used = sem("in_b_used")
        out_a_used = sem("out_a_used")
        out_b_used = sem("out_b_used")
        hid_filled = sem("hid_filled")
        hid_summed = sem("hid_summed")
        gelu_done = sem("gelu_done")
        ht_filled = sem("ht_filled")
        ht_emptied = sem("ht_emptied")
        out_filled = sem("out_filled")
        res_ready = sem("res_ready")
        res_stored = sem("res_stored")
        gate = sem("gate_f")

        def wait(eng, what, value):
            if not (isinstance(value, int) and value <= 0):
                eng.wait_ge(what, value)

        def rounds(eng, front, back):
            front(0)
            with eng.Fori(1, ROUNDS) as r:
                back(r - 1, lambda: front(r))
            back(ROUNDS - 1, lambda: None)

        block = ctx.enter_context(nc.Block())

        @block.sync
        def _(sp):
            wq_v = w["ffn_Wq"].rearrange("(g k p) n -> g p k n", k=KT, p=P)
            keys_v = w["ffn_keysT"].rearrange("(g k p) n -> g p k n", k=KT, p=P)
            for g in range(PH):
                wait(sp, fold_filled, g - 1)
                sp.dma_start(wq_in[:, g % 2, :, :], wq_v[g]).then_inc(wq_loaded[g % 2], 16)
                sp.dma_start(keys_in[:, g % 2, :, :], keys_v[g]).then_inc(wq_loaded[g % 2], 16)
            sp.dma_start(w_in[:], w["ffn_W_inT"].rearrange("(k p) n -> p k n", p=P)).then_inc(w_loaded, 16)
            sp.dma_start(w_out[:], w["ffn_W_outT"].rearrange("(k p) n -> p k n", p=P)).then_inc(w_loaded, 16)

            def tokens(dram, r):
                return dram[bass.ds(r * P, P), :]

            def front(r):
                wait(sp, xt_filled, r)
                sp.sem_inc(gate, 1)
                sp.dma_start(xn_pe[:], tokens(x3_dram, r)).then_inc(xpe_loaded, 16)
                wait(sp, in_a_used, r * HEADS)
                sp.sem_inc(gate, 1)
                sp.dma_start(xn_ve[:], tokens(x3_dram, r)).then_inc(xve_loaded, 16)
                wait(sp, res_ready, r)
                sp.sem_inc(gate, 1)
                sp.dma_start(x_res[:], tokens(x2_dram, r)).then_inc(xres_loaded, 16)

            def back(r, next_front):
                next_front()
                sp.wait_ge(res_ready, r + 1)
                sp.sem_inc(gate, 1)
                sp.dma_start(tokens(out, r), res[:]).then_inc(res_stored, 16)

            rounds(sp, front, back)
            sp.wait_ge(res_stored, 16 * ROUNDS)

        @block.gpsimd
        def _(pool):
            nc.gpsimd.memset(ident[:], 0.0).then_inc(ident_zeroed, 1)
            pool.wait_ge(ident_zeroed, 1)
            nc.gpsimd.affine_select(out=ident[:], in_=ident[:], compare_op=ALU.not_equal, fill=1.0,
                                    base=0, pattern=[[-1, P]], channel_multiplier=1).then_inc(ident_ready, 1)

            def gather(dst, table, h, loaded):
                nc.gpsimd.indirect_dma_start(dst, None, table,
                                             bass.IndirectOffsetOnAxis(rows_now[:, h:h + 1], 0)).then_inc(loaded, 16)

            def gathers(r):
                pool.wait_ge(picked, r + 1)
                for loaded in out_a_loaded:
                    wait(pool, loaded, 16 * (HEADS // AB) * r)
                for loaded in out_b_loaded:
                    wait(pool, loaded, 16 * r)
                nc.gpsimd.sem_inc(gate, 1)
                nc.gpsimd.tensor_copy(rows_now[:], rows[:]).then_inc(rows_taken, 1)
                pool.wait_ge(rows_taken, r + 1)
                nc.gpsimd.sem_inc(gate, 1)
                for table, dst, slots, loaded, used in (
                        ("in_a", in_a, HEADS, in_a_loaded, in_a_used), ("in_b", in_b, AB, in_b_loaded, in_b_used),
                        ("out_a", out_a, AB, out_a_loaded, out_a_used),
                        ("out_b", out_b, HEADS, out_b_loaded, out_b_used)):
                    for h in range(HEADS):
                        wait(pool, used, r * HEADS + h + 1 - slots)
                        nc.gpsimd.sem_inc(gate, 1)
                        gather(dst[:, h % slots, :], w[table], h, loaded[h % slots])

            gathers(0)
            with pool.Fori(1, ROUNDS) as r:
                gathers(r)

        @block.tensor
        def _(pe):
            pe.wait_ge(ident_ready, 1)
            for g in range(PH):
                pe.wait_ge(wq_loaded[g % 2], 32 * (g // 2 + 1))
                wait(pe, fold_emptied, g - 1)
                for i in range(KD):
                    for k in range(KT):
                        ins = nc.tensor.matmul(l_bank[g % 2][:, i * P:(i + 1) * P],
                                               wq_in[:, g % 2, k, i * P:(i + 1) * P], keys_in[:, g % 2, k, :],
                                               start=(k == 0), stop=(k == KT - 1))
                ins.then_inc(fold_filled, 1)
            pe.wait_ge(fold_emptied, PH)
            pe.wait_ge(w_loaded, 32)

            def front(r):
                pe.wait_ge(xpe_loaded, 16 * r + 16)
                wait(pe, xt_emptied, r)
                for k in range(KD):
                    ins = nc.tensor.transpose(x_bank[:, k * P:(k + 1) * P], xn_pe[:, k * P:(k + 1) * P], ident[:])
                ins.then_inc(xt_filled, 1)
                pe.wait_ge(xt_emptied, r + 1)
                for c in range(CHUNKS):
                    wait(pe, sims_emptied, CHUNKS * r + c - 1)
                    for k in range(KD):
                        ins = nc.tensor.matmul(l_bank[c % 2][:], xn_t[:, k, :], fold[:, k, c * BANK:(c + 1) * BANK],
                                               start=(k == 0), stop=(k == KD - 1))
                    ins.then_inc(sims_filled, 1)

            def back(r, next_front):
                wait(pe, gelu_done, r)
                for n in range(HALVES):
                    for k in range(KD):
                        ins = nc.tensor.matmul(hid_ps[:, n * BANK:(n + 1) * BANK], xn_t[:, k, :],
                                               w_in[:, k, n * BANK:(n + 1) * BANK],
                                               start=(k == 0), stop=(k == KD - 1))
                ins.then_inc(hid_filled, 1)
                next_front()
                pe.wait_ge(gelu_done, r + 1)
                for j, bank in enumerate(h_bank):
                    wait(pe, ht_emptied, len(h_bank) * r)
                    for k in range(PER):
                        at = (j * PER + k) * P
                        ins = nc.tensor.transpose(bank[:, k * P:(k + 1) * P], hid[:, at:at + P], ident[:])
                    ins.then_inc(ht_filled, 1)
                pe.wait_ge(ht_emptied, len(h_bank) * (r + 1))
                wait(pe, res_ready, r)
                for k in range(KF):
                    ins = nc.tensor.matmul(out_ps[:], hid_t[:, k, :], w_out[:, k, :], start=(k == 0),
                                           stop=(k == KF - 1))
                ins.then_inc(out_filled, 1)

            rounds(pe, front, back)

        @block.scalar
        def _(act):
            for g in range(PH):
                act.wait_ge(fold_filled, g + 1)
                nc.scalar.copy(fold[:, :, g * KEYS:(g + 1) * KEYS],
                               l_bank[g % 2][:].rearrange("p (i n) -> p i n", i=KD)).then_inc(fold_emptied, 1)

            def front(r):
                act.wait_ge(xt_filled, r + 1)
                nc.scalar.copy(xn_t[:].rearrange("p k n -> p (k n)"), x_bank[:]).then_inc(xt_emptied, 1)
                wait(act, picked, r)
                for c in range(CHUNKS):
                    act.wait_ge(sims_filled, CHUNKS * r + c + 1)
                    nc.scalar.copy(sims[:, c * BANK:(c + 1) * BANK], l_bank[c % 2][:]).then_inc(sims_emptied, 1)

            def back(r, next_front):
                next_front()
                wait(act, out_a_used, r * HEADS)
                act.wait_ge(hid_summed, r + 1)
                nc.scalar.activation(hid[:], hid_ps[:], ACT.Gelu).then_inc(gelu_done, 1)
                for j, bank in enumerate(h_bank):
                    act.wait_ge(ht_filled, len(h_bank) * r + j + 1)
                    nc.scalar.copy(hid_t[:, j * PER:(j + 1) * PER, :].rearrange("p k n -> p (k n)"),
                                   bank[:]).then_inc(ht_emptied, 1)

            rounds(act, front, back)

        @block.vector
        def _(dve):
            def front(r):
                for c in range(CHUNKS):
                    dve.wait_ge(sims_emptied, CHUNKS * r + c + 1)
                    dve.sem_inc(gate, 1)
                    pairs = range(c * PER, (c + 1) * PER)
                    for g in pairs:
                        nc.vector.max(top[:, g, :], sims[:, g * KEYS:(g + 1) * KEYS])
                    self_wait(dve)
                    for g in pairs:
                        nc.vector.max_index(place[:, g, :], top[:, g, :], sims[:, g * KEYS:(g + 1) * KEYS])
                self_wait(dve)
                nc.vector.scalar_tensor_tensor(out=row_f[:], in0=place[:, 0:HEADS, 0], scalar=float(KEYS),
                                               in1=place[:, HEADS:PH, 0], op0=ALU.mult, op1=ALU.add)
                nc.vector.tensor_tensor(score[:], top[:, 0:HEADS, 0], top[:, HEADS:PH, 0], ALU.add)
                self_wait(dve)
                wait(dve, rows_taken, r)
                nc.vector.tensor_scalar(rows[:], row_f[:], float(E - 1), None, ALU.min).then_inc(picked, 1)

            def back(r, next_front):
                nc.vector.tensor_scalar(gates[:], score[:], 0.0, None, ALU.max)
                dve.wait_ge(xve_loaded, 16 * r + 16)
                for h in range(HEADS):
                    dve.wait_ge(in_a_loaded[h], 16 * r + 16)
                    nc.vector.tensor_tensor_reduce(out=in_a[:, h, :], in0=in_a[:, h, :], in1=xn_ve[:], scale=1.0,
                                                   scalar=0.0, op0=ALU.mult, op1=ALU.add,
                                                   accum_out=lin[:, h:h + 1]).then_inc(in_a_used, 1)
                self_wait(dve)
                nc.vector.tensor_tensor(lin[:], lin[:], gates[:], ALU.mult)
                self_wait(dve)
                dve.wait_ge(hid_filled, r + 1)
                for h in range(HEADS):
                    dve.wait_ge(in_b_loaded[h % AB], 16 * (HEADS // AB) * r + 16 * (h // AB + 1))
                    ins = nc.vector.scalar_tensor_tensor(out=hid_ps[:], in0=in_b[:, h % AB, :],
                                                         scalar=lin[:, h:h + 1], in1=hid_ps[:], op0=ALU.mult,
                                                         op1=ALU.add)
                    ins.then_inc(in_b_used, 1)
                    self_wait(dve)
                dve.sem_inc(hid_summed, 1)
                next_front()
                dve.wait_ge(gelu_done, r + 1)
                for h in range(HEADS):
                    dve.wait_ge(out_a_loaded[h % AB], 16 * (HEADS // AB) * r + 16 * (h // AB + 1))
                    nc.vector.tensor_tensor_reduce(out=out_a[:, h % AB, :], in0=out_a[:, h % AB, :], in1=hid[:], scale=1.0,
                                                   scalar=0.0, op0=ALU.mult, op1=ALU.add,
                                                   accum_out=lout[:, h:h + 1]).then_inc(out_a_used, 1)
                self_wait(dve)
                nc.vector.tensor_tensor(lout[:], lout[:], gates[:], ALU.mult)
                self_wait(dve)
                dve.wait_ge(out_filled, r + 1)
                for h in range(HEADS):
                    dve.wait_ge(out_b_loaded[h], 16 * r + 16)
                    nc.vector.scalar_tensor_tensor(out=out_ps[:], in0=out_b[:, h, :], scalar=lout[:, h:h + 1],
                                                   in1=out_ps[:], op0=ALU.mult, op1=ALU.add).then_inc(out_b_used, 1)
                    self_wait(dve)
                dve.wait_ge(xres_loaded, 16 * r + 16)
                wait(dve, res_stored, 16 * r)
                nc.vector.tensor_tensor(res[:], out_ps[:], x_res[:], ALU.add).then_inc(res_ready, 1)

            rounds(dve, front, back)


def decoder_layer(nc, w, out):
    B, S, D = w["x"].shape
    x2_dram = nc.dram_tensor("x2_scratch", [B * S, D], F32, kind="Internal").ap()
    x3_dram = nc.dram_tensor("x3_scratch", [B * S, D], F32, kind="Internal").ap()
    attention_pass(nc, w, x2_dram, x3_dram)
    expert_pass(nc, w, x2_dram, x3_dram, out.rearrange("b s d -> (b s) d"))


def kernel(**inputs):
    import numpy as np
    import concourse.bacc as bacc
    from concourse.bass_utils import run_bass_kernel_spmd

    def columns(name):
        return inputs[name].reshape(-1, 128).T

    arrays = {"x": inputs["x"], "ctx": inputs["ctx_1024"],
              "mask": inputs["mask_Bx1x1024_ff1"].reshape(inputs["x"].shape[0], -1),
              "attn_bo": inputs["L0_attn_bo"], "rel_k": inputs["L0_xattn_rel_k"],
              "rel_kT": inputs["L0_xattn_rel_k"].T, "rel_v": inputs["L0_xattn_rel_v"],
              "ffn_Wq": inputs["L0_ffn_Wq"],
              "ffn_keysT": np.asarray(inputs["L0_ffn_keys"]).transpose(2, 0, 3, 1).reshape(
                  inputs["L0_ffn_Wq"].shape[0], -1),
              "ffn_W_inT": inputs["L0_ffn_W_in"].T, "ffn_W_outT": inputs["L0_ffn_W_out"].T,
              "in_a": inputs["L0_ffn_in_a"], "in_b": inputs["L0_ffn_in_b"],
              "out_a": inputs["L0_ffn_out_a"], "out_b": inputs["L0_ffn_out_b"]}
    for c in "qkvo":
        arrays[f"attn_W{c}"] = inputs[f"L0_attn_W{c}"]
        arrays[f"xattn_w{c}T"] = inputs[f"L0_xattn_w{c}"].T
        arrays[f"xattn_b{c}"] = columns(f"L0_xattn_b{c}")
        if c != "o":
            arrays[f"attn_b{c}"] = columns(f"L0_attn_b{c}")
    arrays = {f"in_{k}_dram": np.ascontiguousarray(a) for k, a in arrays.items()}

    nc = bacc.Bacc("TRN2", target_bir_lowering=False, num_devices=1)
    w = {k[3:-5]: nc.dram_tensor(k, a.shape, mybir.dt.from_np(a.dtype), kind="ExternalInput").ap()
         for k, a in arrays.items()}
    shape = inputs["x"].shape
    out = nc.dram_tensor("out_0_dram", shape, F32, kind="ExternalOutput").ap()
    decoder_layer(nc, w, out)
    return run_bass_kernel_spmd(nc, [arrays], core_ids=[0]).results[0]["out_0_dram"]
```

```python
from contextlib import ExitStack

import concourse.bass as bass
from concourse import mybir

F32 = mybir.dt.float32
BF16 = mybir.dt.bfloat16
U32 = mybir.dt.uint32
ALU = mybir.AluOpType
ACT = mybir.ActivationFunctionType
AX = mybir.AxisListType

P = 128
BANK = 512
NEG = -1.0e30
EPS = 1e-5
QUAD = 32


def self_wait(eng):
    eng.drain()


def wait(eng, what, value):
    if not (isinstance(value, int) and value <= 0):
        eng.wait_ge(what, value)


def layer_norm_stats(nc, dve, rows, stats, moments, tiles, var_ready):
    for t in range(tiles):
        nc.vector.bn_stats(stats[:, t, :], rows[:, t, :])
    self_wait(dve)
    for t in range(tiles):
        nc.vector.bn_aggr(moments[:, t, :], stats[:, t, :])
    self_wait(dve)
    nc.vector.tensor_scalar(moments[:, 0:tiles, 1:2], moments[:, 0:tiles, 1:2], EPS, None,
                            ALU.add).then_inc(var_ready, 1)


def attention_pass(nc, w, x2_dram, x3_dram):
    B, S, D = w["x"].shape
    TT = S // P
    KD = D // P
    COMP = 4
    TOPK = 64
    SCALE = float(D) ** -0.5
    C, L = S, D
    REL, HC = w["rel_k"].shape
    H = C // HC
    CT = C // P
    HPT = P // HC
    QT_N = L // P
    WIN = REL // 2
    BAND = QUAD + 2 * WIN
    SPAN = P + 2 * WIN
    STEPS = H * QT_N
    ROW = STEPS * BAND
    XSCALE = float(HC) ** -0.5
    PROW = L + 2 * WIN
    PSLOTS = 2 * QT_N

    A_XN, A_Q, A_K, A_V, A_RAW, A_WT, A_OT, A_JOBS = 0, 2, 4, 6, 8, 10, 12, 14
    S_SCORE, S_OUT, S_JOBS = 0, STEPS, STEPS + CT
    T_FIRST = {"CK": 0, "CV": 2, "CQ": 4, "REL": 6}
    T_MID = {"PT": 0, "CK": STEPS, "CV": STEPS + 2, "CQ": STEPS + 4, "REL": STEPS + 6, "PB": STEPS + 7,
             "CTX": STEPS + 8}
    T_LAST = {"PT": 0, "PB": STEPS, "CTX": STEPS + 1}
    N_FIRST, N_MID = T_FIRST["REL"] + 1, T_MID["CTX"] + CT
    assert A_JOBS % 2 == 0 and S_JOBS % 2 == 0 and N_MID % 2 == 0
    assert TT == CT == 2 and KD == QT_N == 4

    def t_job(b, kind, n=0):
        if isinstance(b, int) and b == 0:
            return T_FIRST[kind] % 2 ^ n % 2, T_FIRST[kind] + n
        place = (T_LAST if isinstance(b, int) and b == B else T_MID)[kind] + n
        return (N_FIRST + place) % 2, (b - 1) * N_MID + (N_FIRST + place)

    AT_LN, AT_XN, AT_QKV, AT_RAW, AT_MAX = 0, 3, 5, 11, 12
    AT_TOP = AT_MAX + 1
    AT_SPARSE = AT_TOP + TOPK // 8
    AT_MIX = AT_SPARSE + 2
    AT_WT = AT_MIX + 2
    AT_OT = AT_WT + 1
    AT_ATT = AT_OT + 3
    AT_LN2 = AT_ATT + 1

    rel_scratch = nc.dram_tensor("rel_scratch", [(P + 1) * ROW], F32, kind="Internal").ap()
    prob_scratch = nc.dram_tensor("prob_scratch", [(P + 1) * ROW], F32, kind="Internal").ap()

    with ExitStack() as ctx:
        def sb(name, shape, dt=F32):
            return ctx.enter_context(nc.sbuf_tensor(name, shape, dt))

        def sem(name):
            return ctx.enter_context(nc.semaphore(name))

        ident = sb("ident", [P, P])
        zeros = sb("zeros", [1, BANK], BF16)
        w_q, w_k, w_v, w_o = (sb(f"w_{n}", [P, KD, D]) for n in "qkvo")
        b_q, b_k, b_v = (sb(f"b_{n}", [P, KD]) for n in "qkv")
        b_o = sb("b_o", [P, D])
        cw_q, cw_k, cw_v, cw_o = (sb(f"cw_{n}", [P, CT, C]) for n in "qkvo")
        cb_q, cb_k, cb_v, cb_o = (sb(f"cb_{n}", [P, CT]) for n in "qkvo")
        cb_qs = sb("cb_qs", [P, CT])
        rel_k4 = sb("rel_k4", [P, HPT * REL])
        rel_v8 = sb("rel_v8", [H * REL, C])
        half = sb("half", [P, TT])
        shares = sb("shares", [P, 3])

        x_in = sb("x_in", [P, TT, D])
        x_bo = sb("x_bo", [P, TT, D])
        c_in = sb("c_in", [P, CT, L])
        mask_in = sb("mask_in", [P, L])
        mask_add = sb("mask_add", [P, L])
        stats = sb("stats", [P, TT, 6])
        mom = sb("mom", [P, TT, 2])
        rstd = sb("rstd", [P, TT])
        xn = sb("xn", [P, TT, D])
        xn_t = sb("xn_t", [P, KD, S])
        q_t = sb("q_t", [P, KD, S])
        k_t = sb("k_t", [P, KD, S])
        v = sb("v", [P, TT, D])
        raw = sb("raw", [P, TT, S])
        causal = sb("causal", [P, TT, S])
        csum = sb("csum", [P, TT, S // COMP])
        left = sb("left", [P, TT, S])
        best = sb("best", [P, TT, 8])
        sparse = sb("sparse", [P, TT, S])
        nmax = sb("nmax", [P, TT, 3])
        sums = sb("sums", [P, TT, 3])
        rsum = sb("rsum", [P, TT, 3])
        e_w = sb("e_w", [P, TT, S])
        e_c = sb("e_c", [P, TT, S // COMP])
        e_s = sb("e_s", [P, TT, S])
        mix = sb("mix", [P, TT, S])
        mix_t = sb("mix_t", [P, TT, S])
        o_t = sb("o_t", [P, KD, S])
        x1 = sb("x1", [P, TT, D])
        x1_prev = sb("x1_prev", [P, TT, D])
        x3 = sb("x3", [P, CT, L])
        stats3 = sb("stats3", [P, TT, 6])
        mom3 = sb("mom3", [P, TT, 2])
        rstd3 = sb("rstd3", [P, TT])
        stats2 = sb("stats2", [P, TT, 6])
        mom2 = sb("mom2", [P, TT, 2])
        rstd2 = sb("rstd2", [P, TT])
        qn = sb("qn", [P, CT, L])
        cq = sb("cq", [P, CT, L])
        ck = sb("ck", [P, CT, L])
        cv = sb("cv", [P, QT_N, C])
        rel_pad = sb("rel_pad", [P, STEPS, BAND])
        band = sb("band", [P, 2, QT_N, SPAN])
        scores = sb("scores", [P, 2, L])
        nmx = sb("nmx", [P, STEPS])
        lsum = sb("lsum", [P, STEPS])
        linv = sb("linv", [P, STEPS])
        PSTEP = PROW + P
        probs = sb("probs", [P, PSLOTS * PROW + QT_N * P + QUAD * QT_N])
        prob_t = sb("prob_t", [P, 2, L])
        near = sb("near", [P, STEPS, BAND])
        near_c = sb("near_c", [P, QT_N, H, REL])
        near_t = sb("near_t", [H * REL, L])
        cn = sb("cn", [P, QT_N, C])
        cn_t = sb("cn_t", [P, CT, L])
        x2 = sb("x2", [P, CT, L])

        a_bank = [ctx.enter_context(nc.psum_tensor(f"a_bank{i}", [P, BANK], F32)) for i in range(2)]
        t_bank = [ctx.enter_context(nc.psum_tensor(f"t_bank{i}", [P, BANK], F32)) for i in range(2)]
        s_bank = [ctx.enter_context(nc.psum_tensor(f"s_bank{i}", [P, BANK], F32)) for i in range(2)]
        acc = ctx.enter_context(nc.psum_tensor("acc", [P, QT_N, C], F32))

        weights_in = sem("weights_in")
        consts = sem("consts")
        bias_scaled = sem("bias_scaled")
        x_loaded = sem("x_loaded")
        c_loaded = sem("c_loaded")
        ckv_done = sem("ckv_done")
        mask_loaded = sem("mask_loaded")
        x_used = sem("x_used")
        mask_used = sem("mask_used")
        var_ready = [sem(f"var_ready{i}") for i in range(3)]
        rstd_ready = [sem(f"rstd_ready{i}") for i in range(3)]
        xn_ready = sem("xn_ready")
        xbo_ready = sem("xbo_ready")
        causal_ready = sem("causal_ready")
        nmax_ready = sem("nmax_ready")
        sparse_ready = sem("sparse_ready")
        exps_ready = sem("exps_ready")
        mix_ready = sem("mix_ready")
        qn_ready = sem("qn_ready")
        a_filled = sem("a_filled")
        a_emptied = sem("a_emptied")
        att_filled = sem("att_filled")
        att_emptied = sem("att_emptied")
        t_filled = sem("t_filled")
        t_emptied = sem("t_emptied")
        s_filled = sem("s_filled")
        s_emptied = sem("s_emptied")
        rel_written = sem("rel_written")
        band_loaded = [sem(f"band_loaded{i}") for i in range(2)]
        exp_done = sem("exp_done")
        near_written = [sem(f"near_written{i}") for i in range(2)]
        near_loaded = sem("near_loaded")
        near_packed = sem("near_packed")
        acc_done = sem("acc_done")
        acc_emptied = sem("acc_emptied")
        cn_ready = sem("cn_ready")
        x2_ready = sem("x2_ready")
        x2_stored = sem("x2_stored")
        x3_ready = sem("x3_ready")
        x3_stored = sem("x3_stored")
        gate = sem("gate")

        weights = [(w_q, w["attn_Wq"]), (w_k, w["attn_Wk"]), (w_v, w["attn_Wv"]), (w_o, w["attn_Wo"]),
                   (cw_q, w["xattn_wqT"]), (cw_k, w["xattn_wkT"]), (cw_v, w["xattn_wvT"]),
                   (cw_o, w["xattn_woT"])]
        columns = [(b_q, w["attn_bq"]), (b_k, w["attn_bk"]), (b_v, w["attn_bv"]),
                   (cb_q, w["xattn_bq"]), (cb_k, w["xattn_bk"]), (cb_v, w["xattn_bv"]),
                   (cb_o, w["xattn_bo"])]
        N_WEIGHT_DMAS = len(weights) + len(columns) + 1 + HPT + H
        N_CONSTS = 8

        def prob_tile(slot):
            return probs[:, slot * PROW + WIN:slot * PROW + WIN + L]

        block = ctx.enter_context(nc.Block())

        @block.sync
        def _(sp):
            for tile, src in weights:
                sp.dma_start(tile[:], src.rearrange("(k p) n -> p k n", p=P)).then_inc(weights_in, 16)
            for tile, src in columns:
                sp.dma_start(tile[:], src).then_inc(weights_in, 16)
            sp.dma_start(b_o[:], w["attn_bo"].partition_broadcast(P)).then_inc(weights_in, 16)
            sp.wait_ge(consts, N_CONSTS)
            for h in range(HPT):
                sp.dma_start(rel_k4[h * HC:(h + 1) * HC, h * REL:(h + 1) * REL],
                             w["rel_kT"]).then_inc(weights_in, 16)
            for h in range(H):
                sp.dma_start(rel_v8[h * REL:(h + 1) * REL, h * HC:(h + 1) * HC],
                             w["rel_v"]).then_inc(weights_in, 16)

            def load_band(h):
                for g in range(P // QUAD):
                    base = g * QUAD * ROW + h * QT_N * BAND
                    src = rel_scratch[base:base + QUAD * (ROW - 1)].rearrange("(r c) -> r c", c=ROW - 1)
                    src = src[:, 0:QT_N * BAND].rearrange("r (t w) -> r t w", w=BAND)
                    sp.dma_start(band[g * QUAD:(g + 1) * QUAD, h % 2, :, g * QUAD:g * QUAD + BAND],
                                 src).then_inc(band_loaded[h % 2], 16)

            def windows(r):
                wait(sp, near_loaded, r * 64)
                for h in range(H):
                    sp.wait_ge(exp_done, r * STEPS + (h + 1) * QT_N)
                    for g in range(P // QUAD):
                        at = (h % 2) * QT_N * PROW + g * QUAD
                        src = probs[g * QUAD:(g + 1) * QUAD, at:at + QT_N * PSTEP]
                        src = src.rearrange("r (t c) -> r t c", c=PSTEP)[:, :, 0:BAND]
                        dst = prob_scratch[g * QUAD * ROW:(g + 1) * QUAD * ROW]
                        dst = dst.rearrange("(r s w) -> r s w", r=QUAD, w=BAND)[:, h * QT_N:(h + 1) * QT_N, :]
                        sp.dma_start(dst, src).then_inc(near_written[h % 2], 16)
                    if h + 2 < H:
                        sp.wait_ge(s_filled, r * S_JOBS + S_SCORE + (h + 1) * QT_N)
                        load_band(h + 2)

            def near_back(r):
                sp.wait_ge(near_written[0], (r + 1) * (H // 2) * 64)
                sp.wait_ge(near_written[1], (r + 1) * (H // 2) * 64)
                for g in range(P // QUAD):
                    base = g * QUAD * ROW
                    src = prob_scratch[base:base + QUAD * (ROW + 1)].rearrange("(r c) -> r c", c=ROW + 1)
                    n = ROW - QUAD + 1
                    sp.dma_start(near[g * QUAD:(g + 1) * QUAD, :, :].rearrange("r s w -> r (s w)")[:, 0:n],
                                 src[:, 0:n]).then_inc(near_loaded, 16)

            def relative(b):
                sp.wait_ge(t_emptied, t_job(b, "REL")[1] + 1)
                wait(sp, band_loaded[0], b * (H // 2) * 64)
                wait(sp, band_loaded[1], b * (H // 2) * 64)
                sp.dma_start(rel_scratch[0:P * ROW].rearrange("(p n) -> p n", p=P),
                             rel_pad[:].rearrange("p s w -> p (s w)")).then_inc(rel_written, 16)
                sp.wait_ge(rel_written, b * 16 + 16)
                sp.sem_inc(gate, 1)
                load_band(0)
                load_band(1)

            def store(r):
                rows = bass.ds(r * S, S)
                sp.wait_ge(x2_ready, r + 1)
                sp.sem_inc(gate, 1)
                sp.dma_start(x2_dram[rows, :].rearrange("(t p) n -> p t n", p=P), x2[:]).then_inc(x2_stored, 16)
                sp.wait_ge(x3_ready, r + 1)
                sp.sem_inc(gate, 1)
                sp.dma_start(x3_dram[rows, :].rearrange("(t p) n -> p t n", p=P), x3[:]).then_inc(x3_stored, 16)

            def round_(b):
                windows(b - 1)
                near_back(b - 1)
                if not (isinstance(b, int) and b == B):
                    relative(b)
                store(b - 1)

            relative(0)
            with sp.Fori(1, B) as b:
                round_(b)
            round_(B)
            sp.wait_ge(x2_stored, B * 16)
            sp.wait_ge(x3_stored, B * 16)

        @block.gpsimd
        def _(pool):
            def after(ins):
                ins.then_inc(consts, 1)
            nc.gpsimd.memset(ident[:], 0.0)
            nc.gpsimd.drain()
            after(nc.gpsimd.affine_select(out=ident[:], in_=ident[:], compare_op=ALU.not_equal, fill=1.0,
                                          base=0, pattern=[[-1, P]], channel_multiplier=1))
            after(nc.gpsimd.memset(rel_k4[:], 0.0))
            after(nc.gpsimd.memset(rel_v8[:], 0.0))
            after(nc.gpsimd.memset(half[:], -0.5))
            after(nc.gpsimd.memset(zeros[:], 0.0))
            after(nc.gpsimd.memset(rel_pad[:], 0.0))
            after(nc.gpsimd.memset(band[:], 0.0))
            after(nc.gpsimd.memset(probs[:], 0.0))

            pool.wait_ge(weights_in, 16 * N_WEIGHT_DMAS)

            def power(moments, rs, which, b):
                pool.wait_ge(var_ready[which], b + 1)
                nc.gpsimd.tensor_tensor(rs[:], moments[:, :, 1], half[:], ALU.pow).then_inc(rstd_ready[which], 1)

            def load_x(b):
                wait(pool, x_used, b)
                nc.gpsimd.sem_inc(gate, 1)
                pool.dma_start(x_in[:], w["x"][b].rearrange("(t p) n -> p t n", p=P)).then_inc(x_loaded, 16)

            def load_c(b):
                wait(pool, mask_used, b)
                nc.gpsimd.sem_inc(gate, 1)
                pool.dma_start(mask_in[:], w["mask"][b].partition_broadcast(P)).then_inc(mask_loaded, 16)
                wait(pool, ckv_done, b)
                nc.gpsimd.sem_inc(gate, 1)
                pool.dma_start(c_in[:], w["ctx"][b].rearrange("(t p) n -> p t n", p=P)).then_inc(c_loaded, 16)

            def attend(b, last):
                power(mom, rstd, 0, b)
                wait(pool, att_emptied, b * TT)
                nc.gpsimd.sem_inc(gate, 1)
                for t in range(TT):
                    ins = nc.gpsimd.tensor_tensor(x_bo[:, t, :], x_in[:, t, :], b_o[:], ALU.add)
                ins.then_inc(xbo_ready, 1)
                if not last:
                    load_x(b + 1)
                wait(pool, exps_ready, b * TT)
                for t in range(TT):
                    pool.wait_ge(a_emptied, b * A_JOBS + A_RAW + t + 1)
                    nc.gpsimd.sem_inc(gate, 1)
                    nc.gpsimd.affine_select(out=causal[:, t, :], in_=raw[:, t, :], compare_op=ALU.is_ge,
                                            fill=NEG, base=t * P, pattern=[[-1, S]],
                                            channel_multiplier=1).then_inc(causal_ready, 1)
                power(mom2, rstd2, 1, b)

            load_x(0)
            load_c(0)
            attend(0, last=False)
            load_c(1)
            with pool.Fori(1, B - 1) as b:
                attend(b, last=False)
                power(mom3, rstd3, 2, b - 1)
                load_c(b + 1)
            attend(B - 1, last=True)
            power(mom3, rstd3, 2, B - 2)
            power(mom3, rstd3, 2, B - 1)

        @block.tensor
        def _(pe):
            pe.wait_ge(consts, N_CONSTS)
            pe.wait_ge(weights_in, 16 * N_WEIGHT_DMAS)
            def product(out, lhs, rhs, k_tiles):
                for k in range(k_tiles):
                    ins = nc.tensor.matmul(out, lhs(k), rhs(k), start=(k == 0), stop=(k == k_tiles - 1))
                return ins

            def t_open(b, kind, n=0):
                bank, before = t_job(b, kind, n)
                wait(pe, t_emptied, before - 1)
                return t_bank[bank]

            def t_evacuated(b, kind, n):
                pe.wait_ge(t_emptied, t_job(b, kind, n)[1] + 1)

            def attend(b, s):
                def a_open(n):
                    wait(pe, a_emptied, b * A_JOBS + max(n - 1, 0))
                    return a_bank[n % 2]

                def a_evacuated(n):
                    pe.wait_ge(a_emptied, b * A_JOBS + n + 1)

                if s == AT_XN:
                    wait(pe, att_emptied, b * TT)
                    for t in range(TT):
                        bank = a_open(A_XN + t)
                        pe.wait_ge(xn_ready, b * TT + t + 1)
                        for k in range(KD):
                            ins = nc.tensor.transpose(bank[:, k * P:(k + 1) * P], xn[:, t, k * P:(k + 1) * P],
                                                      ident[:])
                        ins.then_inc(a_filled, 1)
                for i, (job, wt) in enumerate(((A_Q, w_q), (A_K, w_k))):
                    if 0 <= s - AT_QKV - 2 * i < 2:
                        m2 = s - AT_QKV - 2 * i
                        a_evacuated(A_XN + TT - 1)
                        bank = a_open(job + m2)
                        for j in range(2):
                            m = 2 * m2 + j
                            ins = product(bank[:, j * S:(j + 1) * S], lambda k: wt[:, k, m * P:(m + 1) * P],
                                          lambda k: xn_t[:, k, :], KD)
                        ins.then_inc(a_filled, 1)
                if 0 <= s - AT_QKV - 4 < TT:
                    t = s - AT_QKV - 4
                    bank = a_open(A_V + t)
                    product(bank[:, 0:D], lambda k: xn_t[:, k, t * P:(t + 1) * P], lambda k: w_v[:, k, :],
                            KD).then_inc(a_filled, 1)
                if s == AT_RAW:
                    a_evacuated(A_K + KD // 2 - 1)
                    for t in range(TT):
                        bank = a_open(A_RAW + t)
                        product(bank[:, 0:S], lambda k: q_t[:, k, t * P:(t + 1) * P], lambda k: k_t[:, k, :],
                                KD).then_inc(a_filled, 1)
                if s == AT_WT:
                    for t in range(TT):
                        bank = a_open(A_WT + t)
                        pe.wait_ge(mix_ready, b * TT + t + 1)
                        for k in range(TT):
                            ins = nc.tensor.transpose(bank[:, k * P:(k + 1) * P], mix[:, t, k * P:(k + 1) * P],
                                                      ident[:])
                        ins.then_inc(a_filled, 1)
                if 0 <= s - AT_OT < 2:
                    m2 = s - AT_OT
                    a_evacuated(A_WT + TT - 1)
                    bank = a_open(A_OT + m2)
                    for j in range(2):
                        m = 2 * m2 + j
                        ins = product(bank[:, j * S:(j + 1) * S], lambda k: v[:, k, m * P:(m + 1) * P],
                                      lambda k: mix_t[:, k, :], TT)
                    ins.then_inc(a_filled, 1)
                if s == AT_ATT:
                    a_evacuated(A_JOBS - 1)
                    for t in range(TT):
                        product(a_bank[t][:, 0:D], lambda k: o_t[:, k, t * P:(t + 1) * P],
                                lambda k: w_o[:, k, :], KD).then_inc(att_filled, 1)

            def score(r, n):
                h, t = divmod(n, QT_N)
                o, g = divmod(h, HPT)
                wait(pe, s_emptied, r * S_JOBS + max(n - 1, 0))
                bank = s_bank[n % 2]
                nc.tensor.matmul(bank[:, 0:L], cq[g * HC:(g + 1) * HC, o, t * P:(t + 1) * P],
                                 ck[g * HC:(g + 1) * HC, o, :], start=True, stop=False, skip_group_check=True)
                if t == 0:
                    pe.wait_ge(band_loaded[h % 2], (r * (H // 2) + h // 2 + 1) * 64)
                lo = max(t * P - WIN, 0)
                hi = min(t * P + P + WIN, L)
                off = lo - (t * P - WIN)
                nc.tensor.matmul(bank[:, lo:hi], ident[:], band[:, h % 2, t, off:off + hi - lo],
                                 start=False, stop=True, skip_group_check=True).then_inc(s_filled, 1)

            def turn(r, n):
                bank = t_open(r + 1, "PT", n)
                pe.wait_ge(exp_done, r * STEPS + n + 1)
                src = prob_tile(n % PSLOTS)
                for k in range(QT_N):
                    ins = nc.tensor.transpose(bank[:, k * P:(k + 1) * P], src[:, k * P:(k + 1) * P], ident[:])
                ins.then_inc(t_filled, 1)

            def weigh(r, n):
                h, t = divmod(n, QT_N)
                t_evacuated(r + 1, "PT", n)
                for k in range(QT_N):
                    nc.tensor.matmul(acc[:, t, h * HC:(h + 1) * HC], prob_t[:, n % 2, k * P:(k + 1) * P],
                                     cv[:, k, h * HC:(h + 1) * HC], start=False, stop=False,
                                     skip_group_check=True)

            def steps(b, beside):
                r = b - 1
                wait(pe, acc_emptied, r)
                for j in range(QT_N // 2):
                    nc.tensor.matmul(acc[:, 2 * j:2 * j + 2, :].rearrange("p t c -> p (t c)"),
                                     zeros[:, 0:P], zeros[:], start=True, stop=False, skip_group_check=True)
                for s in range(STEPS + 3):
                    if s < STEPS:
                        score(r, s)
                    if 2 <= s < STEPS + 2:
                        turn(r, s - 2)
                    if s >= 3:
                        weigh(r, s - 3)
                    beside(s)

            def project(b):
                pe.wait_ge(c_loaded, 16 * b + 16)
                for o in range(CT):
                    bank = t_open(b, "CK", o)
                    product(bank[:, 0:L], lambda k: cw_k[:, k, o * P:(o + 1) * P], lambda k: c_in[:, k, :],
                            CT).then_inc(t_filled, 1)
                for s2 in range(QT_N // 2):
                    bank = t_open(b, "CV", s2)
                    for j in range(2):
                        s = 2 * s2 + j
                        ins = product(bank[:, j * C:(j + 1) * C], lambda k: c_in[:, k, s * P:(s + 1) * P],
                                      lambda k: cw_v[:, k, :], CT)
                    ins.then_inc(t_filled, 1)
                pe.wait_ge(qn_ready, b + 1)
                for o in range(CT):
                    bank = t_open(b, "CQ", o)
                    product(bank[:, 0:L], lambda k: cw_q[:, k, o * P:(o + 1) * P], lambda k: qn[:, k, :],
                            CT).then_inc(t_filled, 1)
                t_evacuated(b, "CQ", CT - 1)
                pe.sem_inc(ckv_done, 1)
                bank = t_open(b, "REL")
                n = HPT * REL
                for t in range(QT_N):
                    for o in range(CT):
                        at = (t * CT + o) * n
                        ins = nc.tensor.matmul(bank[:, at:at + n], cq[:, o, t * P:(t + 1) * P], rel_k4[:],
                                               start=True, stop=True)
                ins.then_inc(t_filled, 1)

            def finish(b):
                r = b - 1
                bank = t_open(b, "PB")
                pe.wait_ge(near_packed, r + 1)
                for t in range(QT_N):
                    ins = nc.tensor.transpose(bank[0:H * REL, t * P:(t + 1) * P],
                                              near_c[:, t, :, :].rearrange("p h j -> p (h j)"), ident[:])
                ins.then_inc(t_filled, 1)
                t_evacuated(b, "PB", 0)
                for t in range(QT_N):
                    ins = nc.tensor.matmul(acc[:, t, :], near_t[:, t * P:(t + 1) * P], rel_v8[:],
                                           start=False, stop=(t % 2 == 1), skip_group_check=True)
                ins.then_inc(acc_done, 1)
                pe.wait_ge(cn_ready, r + 1)
                for o in range(CT):
                    bank = t_open(b, "CTX", o)
                    for t in range(QT_N):
                        ins = nc.tensor.transpose(bank[:, t * P:(t + 1) * P], cn[:, t, o * P:(o + 1) * P], ident[:])
                    ins.then_inc(t_filled, 1)
                t_evacuated(b, "CTX", CT - 1)
                for o in range(CT):
                    wait(pe, s_emptied, r * S_JOBS + S_OUT + o - 1)
                    product(s_bank[(S_OUT + o) % 2][:, 0:L], lambda k: cw_o[:, k, o * P:(o + 1) * P],
                            lambda k: cn_t[:, k, :], CT).then_inc(s_filled, 1)

            for s in range(STEPS + 3):
                attend(0, s)
            project(0)
            with pe.Fori(1, B) as b:
                steps(b, lambda s: attend(b, s))
                project(b)
                finish(b)
            steps(B, lambda s: None)
            finish(B)

        @block.scalar
        def _(act):
            act.wait_ge(weights_in, 16 * N_WEIGHT_DMAS)
            act.wait_ge(consts, N_CONSTS)
            nc.scalar.mul(cb_qs[:], cb_q[:], XSCALE)
            self_wait(act)
            def t_full(b, kind, n=0):
                bank, before = t_job(b, kind, n)
                act.wait_ge(t_filled, before + 1)
                return t_bank[bank]

            def attend(b, s):
                def a_full(n):
                    act.wait_ge(a_filled, b * A_JOBS + n + 1)
                    return a_bank[n % 2]

                if s == AT_XN:
                    for t in range(TT):
                        bank = a_full(A_XN + t)
                        nc.scalar.copy(xn_t[:, :, t * P:(t + 1) * P],
                                       bank[:].rearrange("p (k n) -> p k n", k=KD)).then_inc(a_emptied, 1)
                for i, (job, dst, bias) in enumerate(((A_Q, q_t, b_q), (A_K, k_t, b_k))):
                    if 0 <= s - AT_QKV - 2 * i < 2:
                        m2 = s - AT_QKV - 2 * i
                        bank = a_full(job + m2)
                        for j in range(2):
                            m = 2 * m2 + j
                            ins = nc.scalar.activation(dst[:, m, :], bank[:, j * S:(j + 1) * S], ACT.Identity,
                                                       bias=bias[:, m:m + 1])
                        ins.then_inc(a_emptied, 1)
                if 0 <= s - AT_QKV - 4 < TT:
                    t = s - AT_QKV - 4
                    bank = a_full(A_V + t)
                    nc.scalar.copy(v[:, t, :], bank[:, 0:D]).then_inc(a_emptied, 1)
                if s == AT_RAW:
                    for t in range(TT):
                        bank = a_full(A_RAW + t)
                        nc.scalar.mul(raw[:, t, :], bank[:, 0:S], SCALE).then_inc(a_emptied, 1)
                if s == AT_TOP + 1:
                    for t in range(TT):
                        act.wait_ge(nmax_ready, b * TT + t + 1)
                        nc.scalar.activation(e_w[:, t, :], causal[:, t, :], ACT.Exp, bias=nmax[:, t, 0:1],
                                             accum_out=sums[:, t, 0:1])
                        nc.scalar.activation(e_c[:, t, :], csum[:, t, :], ACT.Exp, bias=nmax[:, t, 1:2],
                                             scale=1.0 / COMP, accum_out=sums[:, t, 1:2])
                if s == AT_SPARSE + 1:
                    for t in range(TT):
                        act.wait_ge(sparse_ready, b * TT + t + 1)
                        nc.scalar.activation(e_s[:, t, :], sparse[:, t, :], ACT.Exp, bias=nmax[:, t, 2:3],
                                             accum_out=sums[:, t, 2:3]).then_inc(exps_ready, 1)
                if s == AT_WT:
                    for t in range(TT):
                        bank = a_full(A_WT + t)
                        nc.scalar.copy(mix_t[:, :, t * P:(t + 1) * P],
                                       bank[:, 0:S].rearrange("p (k n) -> p k n", k=TT)).then_inc(a_emptied, 1)
                if 0 <= s - AT_OT < 2:
                    m2 = s - AT_OT
                    bank = a_full(A_OT + m2)
                    for j in range(2):
                        m = 2 * m2 + j
                        ins = nc.scalar.activation(o_t[:, m, :], bank[:, j * S:(j + 1) * S], ACT.Identity,
                                                   bias=b_v[:, m:m + 1])
                    ins.then_inc(a_emptied, 1)

            def steps(b, beside):
                r = b - 1
                for s in range(STEPS + 3):
                    if s < STEPS:
                        h = s // QT_N
                        act.wait_ge(s_emptied, r * S_JOBS + S_SCORE + s + 1)
                        if s % QT_N == 0:
                            wait(act, near_written[h % 2], (r * (H // 2) + h // 2) * 64)
                        nc.scalar.activation(prob_tile(s % PSLOTS), scores[:, s % 2, :], ACT.Exp,
                                             bias=nmx[:, s:s + 1], scale=-1.0,
                                             accum_out=lsum[:, s:s + 1]).then_inc(exp_done, 1)
                    if 1 <= s <= STEPS:
                        bank = t_full(b, "PT", s - 1)
                        nc.scalar.copy(prob_t[:, (s - 1) % 2, :], bank[:]).then_inc(t_emptied, 1)
                    beside(s)

            def project(b):
                for o in range(CT):
                    bank = t_full(b, "CK", o)
                    nc.scalar.activation(ck[:, o, :], bank[:, 0:L], ACT.Identity,
                                         bias=cb_k[:, o:o + 1]).then_inc(t_emptied, 1)
                for s2 in range(QT_N // 2):
                    bank = t_full(b, "CV", s2)
                    nc.scalar.copy(cv[:, 2 * s2:2 * s2 + 2, :],
                                   bank[:].rearrange("p (s c) -> p s c", s=2)).then_inc(t_emptied, 1)
                for o in range(CT):
                    bank = t_full(b, "CQ", o)
                    nc.scalar.activation(cq[:, o, :], bank[:, 0:L], ACT.Identity, bias=cb_qs[:, o:o + 1],
                                         scale=XSCALE).then_inc(t_emptied, 1)
                bank = t_full(b, "REL")
                wait(act, rel_written, b * 16)
                nc.scalar.copy(
                    rel_pad[:].rearrange("p (h t) w -> p h t w", t=QT_N)[:, :, :, 0:REL],
                    bank[:, 0:QT_N * H * REL].rearrange("p (t h j) -> p h t j", t=QT_N, j=REL)
                ).then_inc(t_emptied, 1)

            def finish(b):
                bank = t_full(b, "PB")
                nc.scalar.copy(near_t[:], bank[0:H * REL, :]).then_inc(t_emptied, 1)
                for o in range(CT):
                    bank = t_full(b, "CTX", o)
                    nc.scalar.activation(cn_t[:, o, :], bank[:, 0:L], ACT.Identity,
                                         bias=cb_v[:, o:o + 1]).then_inc(t_emptied, 1)

            for s in range(STEPS + 3):
                attend(0, s)
            project(0)
            with act.Fori(1, B) as b:
                steps(b, lambda s: attend(b, s))
                project(b)
                finish(b)
            steps(B, lambda s: None)
            finish(B)

        @block.vector
        def _(dve):
            for j, share in enumerate((3.0, 3.0 * COMP, 3.0)):
                nc.vector.memset(shares[:, j:j + 1], share)
            dve.wait_ge(weights_in, 16 * N_WEIGHT_DMAS)
            self_wait(dve)
            def normalise(dst, src, moments, rs, ready, each):
                for t in range(TT):
                    ins = nc.vector.tensor_scalar(dst[:, t, :], src[:, t, :], moments[:, t, 0:1],
                                                  rs[:, t:t + 1], ALU.subtract, ALU.mult)
                    if each or t == TT - 1:
                        ins.then_inc(ready, 1)

            def attend(b, s):
                if s == AT_LN:
                    dve.wait_ge(x_loaded, 16 * b + 16)
                    layer_norm_stats(nc, dve, x_in, stats, mom, TT, var_ready[0])
                if s == AT_LN + 1:
                    dve.wait_ge(rstd_ready[0], b + 1)
                    normalise(xn, x_in, mom, rstd, xn_ready, True)
                if s == AT_XN:
                    dve.wait_ge(xbo_ready, b + 1)
                    dve.wait_ge(xn_ready, (b + 1) * TT)
                    dve.sem_inc(x_used, 1)
                if s == AT_MAX:
                    for t in range(TT):
                        dve.wait_ge(a_emptied, b * A_JOBS + A_RAW + t + 1)
                        nc.vector.tensor_reduce(csum[:, t, :], raw[:, t, :].rearrange("p (s c) -> p s c", c=COMP),
                                                AX.X, ALU.add)
                    self_wait(dve)
                    for t in range(TT):
                        nc.vector.tensor_reduce(nmax[:, t, 1:2], csum[:, t, :], AX.X, ALU.max, negate=True)
                    self_wait(dve)
                    for t in range(TT):
                        nc.vector.tensor_scalar(nmax[:, t, 1:2], nmax[:, t, 1:2], 1.0 / COMP, None, ALU.mult)
                        dve.wait_ge(causal_ready, b * TT + t + 1)
                        nc.vector.tensor_reduce(nmax[:, t, 0:1], causal[:, t, :], AX.X, ALU.max,
                                                negate=True).then_inc(nmax_ready, 1)
                if AT_TOP <= s < AT_SPARSE:
                    src = raw if s == AT_TOP else left
                    for t in range(TT):
                        nc.vector.max(best[:, t, :], src[:, t, :])
                    self_wait(dve)
                    for t in range(TT):
                        if s == AT_TOP:
                            nc.vector.tensor_scalar(nmax[:, t, 2:3], best[:, t, 0:1], 0.0, -1.0, ALU.max,
                                                    ALU.mult)
                        nc.vector.match_replace(left[:, t, :], best[:, t, :], src[:, t, :], NEG)
                    self_wait(dve)
                if s == AT_SPARSE:
                    for t in range(TT):
                        nc.vector.scalar_tensor_tensor(out=sparse[:, t, :], in0=left[:, t, :], scalar=NEG,
                                                       in1=raw[:, t, :], op0=ALU.is_equal,
                                                       op1=ALU.mult).then_inc(sparse_ready, 1)
                if s == AT_MIX:
                    for t in range(TT):
                        dve.wait_ge(exps_ready, b * TT + t + 1)
                        nc.vector.tensor_tensor(rsum[:, t, :], sums[:, t, :], shares[:], ALU.mult)
                    self_wait(dve)
                    for t in range(TT):
                        nc.vector.reciprocal(rsum[:, t, :], rsum[:, t, :])
                    self_wait(dve)
                    for t in range(TT):
                        nc.vector.tensor_scalar(mix[:, t, :], e_w[:, t, :], rsum[:, t, 0:1], None, ALU.mult)
                    self_wait(dve)
                    for t in range(TT):
                        nc.vector.scalar_tensor_tensor(out=mix[:, t, :], in0=e_s[:, t, :],
                                                       scalar=rsum[:, t, 2:3], in1=mix[:, t, :],
                                                       op0=ALU.mult, op1=ALU.add)
                    self_wait(dve)
                    for t in range(TT):
                        groups = mix[:, t, :].rearrange("p (s c) -> p s c", c=COMP)
                        nc.vector.scalar_tensor_tensor(
                            out=groups, in0=e_c[:, t, :].unsqueeze(2).to_broadcast([P, S // COMP, COMP]),
                            scalar=rsum[:, t, 1:2], in1=groups, op0=ALU.mult,
                            op1=ALU.add).then_inc(mix_ready, 1)
                if s == AT_LN2:
                    dve.wait_ge(xbo_ready, b + 1)
                    for t in range(TT):
                        dve.wait_ge(att_filled, b * TT + t + 1)
                        nc.vector.tensor_tensor(x1[:, t, :], a_bank[t][:, 0:D], x_bo[:, t, :],
                                                ALU.add).then_inc(att_emptied, 1)
                    self_wait(dve)
                    layer_norm_stats(nc, dve, x1, stats2, mom2, TT, var_ready[1])
                if s == AT_LN2 + 1:
                    dve.wait_ge(rstd_ready[1], b + 1)
                    normalise(qn, x1, mom2, rstd2, qn_ready, False)

            def steps(b, beside):
                r = b - 1
                for s in range(STEPS + 3):
                    if s < STEPS:
                        dve.wait_ge(s_filled, r * S_JOBS + S_SCORE + s + 1)
                        wait(dve, exp_done, r * STEPS + max(s - 1, 0))
                        dve.sem_inc(gate, 1)
                        nc.vector.tensor_tensor_reduce(
                            out=scores[:, s % 2, :], in0=s_bank[(S_SCORE + s) % 2][:, 0:L], in1=mask_add[:],
                            scale=-1.0, scalar=-NEG, op0=ALU.add, op1=ALU.min,
                            accum_out=nmx[:, s:s + 1]).then_inc(s_emptied, 1)
                    beside(s)

            def masks(b):
                self_wait(dve)
                dve.wait_ge(mask_loaded, 16 * b + 16)
                nc.vector.tensor_scalar(mask_add[:], mask_in[:], 0.0, NEG, ALU.is_equal,
                                        ALU.mult).then_inc(mask_used, 1)

            def keep_x1():
                for t in range(TT):
                    nc.vector.tensor_copy(x1_prev[:, t, :], x1[:, t, :])
                self_wait(dve)

            def finish(b):
                r = b - 1
                dve.wait_ge(exp_done, (r + 1) * STEPS)
                nc.vector.reciprocal(linv[:], lsum[:])
                dve.wait_ge(near_loaded, r * 64 + 64)
                nc.vector.tensor_copy(near_c[:].rearrange("p t h j -> p h t j"),
                                      near[:].rearrange("p (h t) w -> p h t w", t=QT_N)[:, :, :, 0:REL]
                                      ).then_inc(near_packed, 1)
                self_wait(dve)
                dve.wait_ge(acc_done, r + 1)
                for t in range(QT_N):
                    li = linv[:].rearrange("p (h t) -> p h t", t=QT_N)[:, :, t:t + 1].to_broadcast([P, H, HC])
                    ins = nc.vector.tensor_tensor(cn[:, t, :].rearrange("p (h c) -> p h c", h=H),
                                                  acc[:, t, :].rearrange("p (h c) -> p h c", h=H), li, ALU.mult)
                ins.then_inc(cn_ready, 1)
                dve.wait_ge(cn_ready, r + 1)
                dve.sem_inc(acc_emptied, 1)
                wait(dve, x2_stored, 16 * r)
                for o in range(CT):
                    dve.wait_ge(s_filled, r * S_JOBS + S_OUT + o + 1)
                    nc.vector.scalar_tensor_tensor(out=x2[:, o, :], in0=s_bank[(S_OUT + o) % 2][:, 0:L],
                                                   scalar=cb_o[:, o:o + 1], in1=x1_prev[:, o, :], op0=ALU.add,
                                                   op1=ALU.add).then_inc(s_emptied, 1)
                dve.wait_ge(s_emptied, (r + 1) * S_JOBS)
                dve.sem_inc(x2_ready, 1)
                layer_norm_stats(nc, dve, x2, stats3, mom3, TT, var_ready[2])
                dve.wait_ge(rstd_ready[2], r + 1)
                wait(dve, x3_stored, 16 * r)
                normalise(x3, x2, mom3, rstd3, x3_ready, False)

            for s in range(STEPS + 3):
                attend(0, s)
            masks(0)
            keep_x1()
            with dve.Fori(1, B) as b:
                steps(b, lambda s: attend(b, s))
                masks(b)
                finish(b)
                keep_x1()
            steps(B, lambda s: None)
            finish(B)


def expert_pass(nc, w, x2_dram, x3_dram, out):
    N, D = x2_dram.shape
    ROUNDS = N // P
    KD = D // P
    HEADS, KEYS = 8, P
    PH = 2 * HEADS
    DK = w["ffn_Wq"].shape[0] // PH
    KT = DK // P
    E = w["in_a"].shape[0]
    F = w["ffn_W_inT"].shape[1]
    KF = F // P
    SIMS = PH * KEYS
    CHUNKS = SIMS // BANK
    PER = BANK // KEYS
    HALVES = F // BANK
    AB = 4
    assert KEYS * KEYS >= E and HEADS % AB == 0 and DK % P == 0

    with ExitStack() as ctx:
        def sb(name, shape, dt=F32):
            return ctx.enter_context(nc.sbuf_tensor(name, shape, dt))

        def pb(name, shape):
            return ctx.enter_context(nc.psum_tensor(name, shape, F32))

        def sem(name):
            return ctx.enter_context(nc.semaphore(name))

        ident = sb("ident_f", [P, P])
        fold = sb("fold", [P, KD, SIMS])
        w_in = sb("w_in", [P, KD, F])
        w_out = sb("w_out", [P, KF, D])
        wq_in = sb("wq_in", [P, 2, KT, D])
        keys_in = sb("keys_in", [P, 2, KT, KEYS])
        xn_pe = sb("xn_pe", [P, D])
        xn_ve = sb("xn_ve", [P, D])
        x_res = sb("x_res", [P, D])
        xn_t = sb("xn_tf", [P, KD, P])
        sims = sb("sims", [P, SIMS])
        top = sb("top", [P, PH, 8])
        place = sb("place", [P, PH, 8], U32)
        row_f = sb("row_f", [P, HEADS])
        rows = sb("rows", [P, HEADS], U32)
        rows_now = sb("rows_now", [P, HEADS], U32)
        score = sb("score", [P, HEADS])
        gates = sb("gates", [P, HEADS])
        lin = sb("lin", [P, HEADS])
        lout = sb("lout", [P, HEADS])
        in_a = sb("in_a_rows", [P, HEADS, D])
        in_b = sb("in_b_rows", [P, AB, F])
        out_a = sb("out_a_rows", [P, AB, F])
        out_b = sb("out_b_rows", [P, HEADS, D])
        hid = sb("hid", [P, F])
        hid_t = sb("hid_t", [P, KF, P])
        res = sb("res", [P, D])

        x_bank = pb("x_bank", [P, BANK])
        l_bank = [pb(f"l_bank{i}", [P, BANK]) for i in range(2)]
        h_bank = [pb(f"h_bank{i}", [P, BANK]) for i in range(KF * P // BANK)]
        hid_ps = pb("hid_ps", [P, F])
        out_ps = pb("out_ps", [P, D])

        ident_ready = sem("ident_ready")
        ident_zeroed = sem("ident_zeroed")
        w_loaded = sem("w_loaded")
        wq_loaded = [sem(f"wq_loaded{i}") for i in range(2)]
        fold_filled = sem("fold_filled")
        fold_emptied = sem("fold_emptied")
        xpe_loaded = sem("xpe_loaded")
        xve_loaded = sem("xve_loaded")
        xres_loaded = sem("xres_loaded")
        xt_filled = sem("xt_filled")
        xt_emptied = sem("xt_emptied")
        sims_filled = sem("sims_filled")
        sims_emptied = sem("sims_emptied")
        picked = sem("picked")
        rows_taken = sem("rows_taken")
        in_a_loaded = [sem(f"in_a_loaded{i}") for i in range(HEADS)]
        in_b_loaded = [sem(f"in_b_loaded{i}") for i in range(AB)]
        out_a_loaded = [sem(f"out_a_loaded{i}") for i in range(AB)]
        out_b_loaded = [sem(f"out_b_loaded{i}") for i in range(HEADS)]
        in_a_used = sem("in_a_used")
        in_b_used = sem("in_b_used")
        out_a_used = sem("out_a_used")
        out_b_used = sem("out_b_used")
        hid_filled = sem("hid_filled")
        hid_summed = sem("hid_summed")
        gelu_done = sem("gelu_done")
        ht_filled = sem("ht_filled")
        ht_emptied = sem("ht_emptied")
        out_filled = sem("out_filled")
        res_ready = sem("res_ready")
        res_stored = sem("res_stored")
        gate = sem("gate_f")

        def wait(eng, what, value):
            if not (isinstance(value, int) and value <= 0):
                eng.wait_ge(what, value)

        def rounds(eng, front, back):
            front(0)
            with eng.Fori(1, ROUNDS) as r:
                back(r - 1, lambda: front(r))
            back(ROUNDS - 1, lambda: None)

        block = ctx.enter_context(nc.Block())

        @block.sync
        def _(sp):
            wq_v = w["ffn_Wq"].rearrange("(g k p) n -> g p k n", k=KT, p=P)
            keys_v = w["ffn_keysT"].rearrange("(g k p) n -> g p k n", k=KT, p=P)
            for g in range(PH):
                wait(sp, fold_filled, g - 1)
                sp.dma_start(wq_in[:, g % 2, :, :], wq_v[g]).then_inc(wq_loaded[g % 2], 16)
                sp.dma_start(keys_in[:, g % 2, :, :], keys_v[g]).then_inc(wq_loaded[g % 2], 16)
            sp.dma_start(w_in[:], w["ffn_W_inT"].rearrange("(k p) n -> p k n", p=P)).then_inc(w_loaded, 16)
            sp.dma_start(w_out[:], w["ffn_W_outT"].rearrange("(k p) n -> p k n", p=P)).then_inc(w_loaded, 16)

            def tokens(dram, r):
                return dram[bass.ds(r * P, P), :]

            def front(r):
                wait(sp, xt_filled, r)
                sp.sem_inc(gate, 1)
                sp.dma_start(xn_pe[:], tokens(x3_dram, r)).then_inc(xpe_loaded, 16)
                wait(sp, in_a_used, r * HEADS)
                sp.sem_inc(gate, 1)
                sp.dma_start(xn_ve[:], tokens(x3_dram, r)).then_inc(xve_loaded, 16)
                wait(sp, res_ready, r)
                sp.sem_inc(gate, 1)
                sp.dma_start(x_res[:], tokens(x2_dram, r)).then_inc(xres_loaded, 16)

            def back(r, next_front):
                next_front()
                sp.wait_ge(res_ready, r + 1)
                sp.sem_inc(gate, 1)
                sp.dma_start(tokens(out, r), res[:]).then_inc(res_stored, 16)

            rounds(sp, front, back)
            sp.wait_ge(res_stored, 16 * ROUNDS)

        @block.gpsimd
        def _(pool):
            nc.gpsimd.memset(ident[:], 0.0).then_inc(ident_zeroed, 1)
            pool.wait_ge(ident_zeroed, 1)
            nc.gpsimd.affine_select(out=ident[:], in_=ident[:], compare_op=ALU.not_equal, fill=1.0,
                                    base=0, pattern=[[-1, P]], channel_multiplier=1).then_inc(ident_ready, 1)

            def gather(dst, table, h, loaded):
                nc.gpsimd.indirect_dma_start(dst, None, table,
                                             bass.IndirectOffsetOnAxis(rows_now[:, h:h + 1], 0)).then_inc(loaded, 16)

            def gathers(r):
                pool.wait_ge(picked, r + 1)
                for loaded in out_a_loaded:
                    wait(pool, loaded, 16 * (HEADS // AB) * r)
                for loaded in out_b_loaded:
                    wait(pool, loaded, 16 * r)
                nc.gpsimd.sem_inc(gate, 1)
                nc.gpsimd.tensor_copy(rows_now[:], rows[:]).then_inc(rows_taken, 1)
                pool.wait_ge(rows_taken, r + 1)
                nc.gpsimd.sem_inc(gate, 1)
                for table, dst, slots, loaded, used in (
                        ("in_a", in_a, HEADS, in_a_loaded, in_a_used), ("in_b", in_b, AB, in_b_loaded, in_b_used),
                        ("out_a", out_a, AB, out_a_loaded, out_a_used),
                        ("out_b", out_b, HEADS, out_b_loaded, out_b_used)):
                    for h in range(HEADS):
                        wait(pool, used, r * HEADS + h + 1 - slots)
                        nc.gpsimd.sem_inc(gate, 1)
                        gather(dst[:, h % slots, :], w[table], h, loaded[h % slots])

            gathers(0)
            with pool.Fori(1, ROUNDS) as r:
                gathers(r)

        @block.tensor
        def _(pe):
            pe.wait_ge(ident_ready, 1)
            for g in range(PH):
                pe.wait_ge(wq_loaded[g % 2], 32 * (g // 2 + 1))
                wait(pe, fold_emptied, g - 1)
                for i in range(KD):
                    for k in range(KT):
                        ins = nc.tensor.matmul(l_bank[g % 2][:, i * P:(i + 1) * P],
                                               wq_in[:, g % 2, k, i * P:(i + 1) * P], keys_in[:, g % 2, k, :],
                                               start=(k == 0), stop=(k == KT - 1))
                ins.then_inc(fold_filled, 1)
            pe.wait_ge(fold_emptied, PH)
            pe.wait_ge(w_loaded, 32)

            def front(r):
                pe.wait_ge(xpe_loaded, 16 * r + 16)
                wait(pe, xt_emptied, r)
                for k in range(KD):
                    ins = nc.tensor.transpose(x_bank[:, k * P:(k + 1) * P], xn_pe[:, k * P:(k + 1) * P], ident[:])
                ins.then_inc(xt_filled, 1)
                pe.wait_ge(xt_emptied, r + 1)
                for c in range(CHUNKS):
                    wait(pe, sims_emptied, CHUNKS * r + c - 1)
                    for k in range(KD):
                        ins = nc.tensor.matmul(l_bank[c % 2][:], xn_t[:, k, :], fold[:, k, c * BANK:(c + 1) * BANK],
                                               start=(k == 0), stop=(k == KD - 1))
                    ins.then_inc(sims_filled, 1)

            def back(r, next_front):
                wait(pe, gelu_done, r)
                for n in range(HALVES):
                    for k in range(KD):
                        ins = nc.tensor.matmul(hid_ps[:, n * BANK:(n + 1) * BANK], xn_t[:, k, :],
                                               w_in[:, k, n * BANK:(n + 1) * BANK],
                                               start=(k == 0), stop=(k == KD - 1))
                ins.then_inc(hid_filled, 1)
                next_front()
                pe.wait_ge(gelu_done, r + 1)
                for j, bank in enumerate(h_bank):
                    wait(pe, ht_emptied, len(h_bank) * r)
                    for k in range(PER):
                        at = (j * PER + k) * P
                        ins = nc.tensor.transpose(bank[:, k * P:(k + 1) * P], hid[:, at:at + P], ident[:])
                    ins.then_inc(ht_filled, 1)
                pe.wait_ge(ht_emptied, len(h_bank) * (r + 1))
                wait(pe, res_ready, r)
                for k in range(KF):
                    ins = nc.tensor.matmul(out_ps[:], hid_t[:, k, :], w_out[:, k, :], start=(k == 0),
                                           stop=(k == KF - 1))
                ins.then_inc(out_filled, 1)

            rounds(pe, front, back)

        @block.scalar
        def _(act):
            for g in range(PH):
                act.wait_ge(fold_filled, g + 1)
                nc.scalar.copy(fold[:, :, g * KEYS:(g + 1) * KEYS],
                               l_bank[g % 2][:].rearrange("p (i n) -> p i n", i=KD)).then_inc(fold_emptied, 1)

            def front(r):
                act.wait_ge(xt_filled, r + 1)
                nc.scalar.copy(xn_t[:].rearrange("p k n -> p (k n)"), x_bank[:]).then_inc(xt_emptied, 1)
                wait(act, picked, r)
                for c in range(CHUNKS):
                    act.wait_ge(sims_filled, CHUNKS * r + c + 1)
                    nc.scalar.copy(sims[:, c * BANK:(c + 1) * BANK], l_bank[c % 2][:]).then_inc(sims_emptied, 1)

            def back(r, next_front):
                next_front()
                wait(act, out_a_used, r * HEADS)
                act.wait_ge(hid_summed, r + 1)
                nc.scalar.activation(hid[:], hid_ps[:], ACT.Gelu).then_inc(gelu_done, 1)
                for j, bank in enumerate(h_bank):
                    act.wait_ge(ht_filled, len(h_bank) * r + j + 1)
                    nc.scalar.copy(hid_t[:, j * PER:(j + 1) * PER, :].rearrange("p k n -> p (k n)"),
                                   bank[:]).then_inc(ht_emptied, 1)

            rounds(act, front, back)

        @block.vector
        def _(dve):
            def front(r):
                for c in range(CHUNKS):
                    dve.wait_ge(sims_emptied, CHUNKS * r + c + 1)
                    dve.sem_inc(gate, 1)
                    pairs = range(c * PER, (c + 1) * PER)
                    for g in pairs:
                        nc.vector.max(top[:, g, :], sims[:, g * KEYS:(g + 1) * KEYS])
                    self_wait(dve)
                    for g in pairs:
                        nc.vector.max_index(place[:, g, :], top[:, g, :], sims[:, g * KEYS:(g + 1) * KEYS])
                self_wait(dve)
                nc.vector.scalar_tensor_tensor(out=row_f[:], in0=place[:, 0:HEADS, 0], scalar=float(KEYS),
                                               in1=place[:, HEADS:PH, 0], op0=ALU.mult, op1=ALU.add)
                nc.vector.tensor_tensor(score[:], top[:, 0:HEADS, 0], top[:, HEADS:PH, 0], ALU.add)
                self_wait(dve)
                wait(dve, rows_taken, r)
                nc.vector.tensor_scalar(rows[:], row_f[:], float(E - 1), None, ALU.min).then_inc(picked, 1)

            def back(r, next_front):
                nc.vector.tensor_scalar(gates[:], score[:], 0.0, None, ALU.max)
                dve.wait_ge(xve_loaded, 16 * r + 16)
                for h in range(HEADS):
                    dve.wait_ge(in_a_loaded[h], 16 * r + 16)
                    nc.vector.tensor_tensor_reduce(out=in_a[:, h, :], in0=in_a[:, h, :], in1=xn_ve[:], scale=1.0,
                                                   scalar=0.0, op0=ALU.mult, op1=ALU.add,
                                                   accum_out=lin[:, h:h + 1]).then_inc(in_a_used, 1)
                self_wait(dve)
                nc.vector.tensor_tensor(lin[:], lin[:], gates[:], ALU.mult)
                self_wait(dve)
                dve.wait_ge(hid_filled, r + 1)
                for h in range(HEADS):
                    dve.wait_ge(in_b_loaded[h % AB], 16 * (HEADS // AB) * r + 16 * (h // AB + 1))
                    ins = nc.vector.scalar_tensor_tensor(out=hid_ps[:], in0=in_b[:, h % AB, :],
                                                         scalar=lin[:, h:h + 1], in1=hid_ps[:], op0=ALU.mult,
                                                         op1=ALU.add)
                    ins.then_inc(in_b_used, 1)
                    self_wait(dve)
                dve.sem_inc(hid_summed, 1)
                next_front()
                dve.wait_ge(gelu_done, r + 1)
                for h in range(HEADS):
                    dve.wait_ge(out_a_loaded[h % AB], 16 * (HEADS // AB) * r + 16 * (h // AB + 1))
                    nc.vector.tensor_tensor_reduce(out=out_a[:, h % AB, :], in0=out_a[:, h % AB, :], in1=hid[:], scale=1.0,
                                                   scalar=0.0, op0=ALU.mult, op1=ALU.add,
                                                   accum_out=lout[:, h:h + 1]).then_inc(out_a_used, 1)
                self_wait(dve)
                nc.vector.tensor_tensor(lout[:], lout[:], gates[:], ALU.mult)
                self_wait(dve)
                dve.wait_ge(out_filled, r + 1)
                for h in range(HEADS):
                    dve.wait_ge(out_b_loaded[h], 16 * r + 16)
                    nc.vector.scalar_tensor_tensor(out=out_ps[:], in0=out_b[:, h, :], scalar=lout[:, h:h + 1],
                                                   in1=out_ps[:], op0=ALU.mult, op1=ALU.add).then_inc(out_b_used, 1)
                    self_wait(dve)
                dve.wait_ge(xres_loaded, 16 * r + 16)
                wait(dve, res_stored, 16 * r)
                nc.vector.tensor_tensor(res[:], out_ps[:], x_res[:], ALU.add).then_inc(res_ready, 1)

            rounds(dve, front, back)


def decoder_layer(nc, w, out):
    B, S, D = w["x"].shape
    x2_dram = nc.dram_tensor("x2_scratch", [B * S, D], F32, kind="Internal").ap()
    x3_dram = nc.dram_tensor("x3_scratch", [B * S, D], F32, kind="Internal").ap()
    attention_pass(nc, w, x2_dram, x3_dram)
    expert_pass(nc, w, x2_dram, x3_dram, out.rearrange("b s d -> (b s) d"))


def kernel(**inputs):
    import numpy as np
    import concourse.bacc as bacc
    from concourse.bass_utils import run_bass_kernel_spmd

    def columns(name):
        return inputs[name].reshape(-1, 128).T

    arrays = {"x": inputs["x"], "ctx": inputs["ctx_1024"],
              "mask": inputs["mask_Bx1x1024_ff1"].reshape(inputs["x"].shape[0], -1),
              "attn_bo": inputs["L0_attn_bo"], "rel_k": inputs["L0_xattn_rel_k"],
              "rel_kT": inputs["L0_xattn_rel_k"].T, "rel_v": inputs["L0_xattn_rel_v"],
              "ffn_Wq": inputs["L0_ffn_Wq"],
              "ffn_keysT": np.asarray(inputs["L0_ffn_keys"]).transpose(2, 0, 3, 1).reshape(
                  inputs["L0_ffn_Wq"].shape[0], -1),
              "ffn_W_inT": inputs["L0_ffn_W_in"].T, "ffn_W_outT": inputs["L0_ffn_W_out"].T,
              "in_a": inputs["L0_ffn_in_a"], "in_b": inputs["L0_ffn_in_b"],
              "out_a": inputs["L0_ffn_out_a"], "out_b": inputs["L0_ffn_out_b"]}
    for c in "qkvo":
        arrays[f"attn_W{c}"] = inputs[f"L0_attn_W{c}"]
        arrays[f"xattn_w{c}T"] = inputs[f"L0_xattn_w{c}"].T
        arrays[f"xattn_b{c}"] = columns(f"L0_xattn_b{c}")
        if c != "o":
            arrays[f"attn_b{c}"] = columns(f"L0_attn_b{c}")
    arrays = {f"in_{k}_dram": np.ascontiguousarray(a) for k, a in arrays.items()}

    nc = bacc.Bacc("TRN2", target_bir_lowering=False, num_devices=1)
    w = {k[3:-5]: nc.dram_tensor(k, a.shape, mybir.dt.from_np(a.dtype), kind="ExternalInput").ap()
         for k, a in arrays.items()}
    shape = inputs["x"].shape
    out = nc.dram_tensor("out_0_dram", shape, F32, kind="ExternalOutput").ap()
    decoder_layer(nc, w, out)
    return run_bass_kernel_spmd(nc, [arrays], core_ids=[0]).results[0]["out_0_dram"]
```

```python
from contextlib import ExitStack

import concourse.bass as bass
from concourse import mybir

F32 = mybir.dt.float32
BF16 = mybir.dt.bfloat16
U32 = mybir.dt.uint32
ALU = mybir.AluOpType
ACT = mybir.ActivationFunctionType
AX = mybir.AxisListType

P = 128
BANK = 512
NEG = -1.0e30
EPS = 1e-5
QUAD = 32


def self_wait(eng):
    eng.drain()


def wait(eng, what, value):
    if not (isinstance(value, int) and value <= 0):
        eng.wait_ge(what, value)


def layer_norm_stats(nc, dve, rows, stats, moments, tiles, var_ready, only=None):
    for t in range(tiles) if only is None else [only]:
        nc.vector.bn_stats(stats[:, t, :], rows[:, t, :])
    if only is None or only == tiles - 1:
        self_wait(dve)
        for t in range(tiles):
            nc.vector.bn_aggr(moments[:, t, :], stats[:, t, :])
        self_wait(dve)
        nc.vector.tensor_scalar(moments[:, 0:tiles, 1:2], moments[:, 0:tiles, 1:2], EPS, None,
                                ALU.add).then_inc(var_ready, 1)


def attention_pass(nc, w, x2_dram, x3_dram):
    B, S, D = w["x"].shape
    TT = S // P
    KD = D // P
    COMP = 4
    TOPK = 64
    SCALE = float(D) ** -0.5
    C, L = S, D
    REL, HC = w["rel_k"].shape
    H = C // HC
    CT = C // P
    HPT = P // HC
    QT_N = L // P
    WIN = REL // 2
    BAND = QUAD + 2 * WIN
    SPAN = P + 2 * WIN
    STEPS = H * QT_N
    ROW = STEPS * BAND
    XSCALE = float(HC) ** -0.5
    PROW = L + 2 * WIN
    GROUPS = CT * QT_N
    PSLOTS = 2 * HPT

    A_START = {"XN": 0, "Q": 2, "K": 4, "RAW": 6, "V": 8}
    A_MID = {"XN": 0, "Q": 2, "K": 4, "RAW": 6, "WT": 8, "OT": 10, "V": 12}
    A_LAST = {"WT": 0, "OT": 2}
    N_A_START, N_A_MID = 2 * len(A_START), 2 * len(A_MID)

    def a_job(b, kind, n=0):
        if kind in ("WT", "OT"):
            last = isinstance(b, int) and b == B - 1
            return b * N_A_MID + (N_A_START + (A_LAST if last else A_MID)[kind] + n)
        if isinstance(b, int) and b == 0:
            return A_START[kind] + n
        return (b - 1) * N_A_MID + (N_A_START + A_MID[kind] + n)

    S_SCORE, S_OUT, S_JOBS = 0, STEPS, STEPS + CT
    AT_LN, AT_XN, AT_Q, AT_K, AT_RAW, AT_MAX, AT_V = 1, 6, 8, 13, 18, 22, 30
    AT_TOP = 0
    AT_CK = (3, 5)
    AT_SPARSE = AT_TOP + 2 * TOPK // 8
    AT_MIX = AT_SPARSE + 2
    AT_WT = AT_MIX + 4
    AT_OT = AT_WT + 1
    AT_ATT = AT_OT + 3
    AT_LN2 = AT_ATT + 1
    AT_LN3 = 9
    assert AT_LN2 + 3 <= STEPS and AT_SPARSE + 1 <= AT_RAW and AT_OT < AT_V

    AT_CQ = (STEPS, STEPS + 1)
    ahead = {("CK", 0): AT_CK[0], ("CK", 1): AT_CK[1], ("CQ", 0): AT_CQ[0], ("CQ", 1): AT_CQ[1]}
    behind = [("CV", 0), ("REL", 0), ("CV", 1)]
    middle = []
    for s in range(STEPS):
        middle.append(("PT", s))
        middle += [job for job, at in ahead.items() if at == s + 3]
    t_order = {"first": [*ahead, *behind], "middle": middle + behind + [("PB", 0)],
               "last": [("PT", s) for s in range(STEPS)] + [("PB", 0)]}
    T_PLACE = {which: {job: place for place, job in enumerate(jobs)} for which, jobs in t_order.items()}
    N_FIRST, N_MID = len(t_order["first"]), len(t_order["middle"])
    assert S_JOBS % 2 == 0 and N_MID % 2 == 0
    assert TT == CT == 2 and KD == QT_N == HPT == 4

    def t_job(b, kind, n=0):
        if isinstance(b, int) and b == 0:
            place = T_PLACE["first"][kind, n]
            return place % 2, place
        place = T_PLACE["last" if isinstance(b, int) and b == B else "middle"][kind, n]
        return (N_FIRST + place) % 2, (b - 1) * N_MID + (N_FIRST + place)

    rel_scratch = nc.dram_tensor("rel_scratch", [(P + 1) * ROW], F32, kind="Internal").ap()
    prob_scratch = nc.dram_tensor("prob_scratch", [(P + 1) * ROW], F32, kind="Internal").ap()

    with ExitStack() as ctx:
        def sb(name, shape, dt=F32):
            return ctx.enter_context(nc.sbuf_tensor(name, shape, dt))

        def sem(name):
            return ctx.enter_context(nc.semaphore(name))

        ident = sb("ident", [P, P])
        zeros = sb("zeros", [1, BANK], BF16)
        w_q, w_k, w_v, w_o = (sb(f"w_{n}", [P, KD, D]) for n in "qkvo")
        b_q, b_k, b_v = (sb(f"b_{n}", [P, KD]) for n in "qkv")
        b_o = sb("b_o", [P, D])
        cw_q, cw_k, cw_v, cw_o = (sb(f"cw_{n}", [P, CT, C]) for n in "qkvo")
        cb_q, cb_k, cb_v, cb_o = (sb(f"cb_{n}", [P, CT]) for n in "qkvo")
        cb_qs = sb("cb_qs", [P, CT])
        rel_k4 = sb("rel_k4", [P, HPT * REL])
        rel_v8 = sb("rel_v8", [H * REL, C])
        half = sb("half", [P, TT])
        shares = sb("shares", [P, 3])

        x_in = sb("x_in", [P, TT, D])
        x_bo = sb("x_bo", [P, TT, D])
        c_in = sb("c_in", [P, CT, L])
        mask_in = sb("mask_in", [P, L])
        mask_add = sb("mask_add", [P, L])
        added = sb("added", [P, 2, L])
        stats = sb("stats", [P, TT, 6])
        mom = sb("mom", [P, TT, 2])
        rstd = sb("rstd", [P, TT])
        xn = sb("xn", [P, TT, D])
        xn_t = sb("xn_t", [P, KD, S])
        q_t = sb("q_t", [P, KD, S])
        k_t = sb("k_t", [P, KD, S])
        v = sb("v", [P, TT, D])
        raw = sb("raw", [P, TT, S])
        causal = sb("causal", [P, TT, S])
        csum = sb("csum", [P, TT, S // COMP])
        left = sb("left", [P, TT, S])
        best = sb("best", [P, TT, 8])
        nmax = sb("nmax", [P, TT, 3])
        sums = sb("sums", [P, TT, 3])
        rsum = sb("rsum", [P, TT, 3])
        e_w = sb("e_w", [P, TT, S])
        e_c = sb("e_c", [P, TT, S // COMP])
        e_s = sb("e_s", [P, TT, S])
        mix = sb("mix", [P, TT, S])
        mix_t = sb("mix_t", [P, TT, S])
        o_t = sb("o_t", [P, KD, S])
        x1 = sb("x1", [P, TT, D])
        x1_prev = sb("x1_prev", [P, TT, D])
        x3 = sb("x3", [P, CT, L])
        stats3 = sb("stats3", [P, TT, 6])
        mom3 = sb("mom3", [P, TT, 2])
        rstd3 = sb("rstd3", [P, TT])
        stats2 = sb("stats2", [P, TT, 6])
        mom2 = sb("mom2", [P, TT, 2])
        rstd2 = sb("rstd2", [P, TT])
        qn = sb("qn", [P, CT, L])
        cq = sb("cq", [P, CT, L])
        ck_next = sb("ck_next", [P, CT, L])
        ck = sb("ck", [P, CT, L])
        cv = sb("cv", [P, QT_N, C])
        rel_pad = sb("rel_pad", [P, STEPS, BAND])
        band = sb("band", [P, 2, QT_N, SPAN])
        scores = sb("scores", [P, 2, L])
        nmx = sb("nmx", [P, STEPS])
        lsum = sb("lsum", [P, STEPS])
        linv = sb("linv", [P, STEPS])
        probs = sb("probs", [P, PSLOTS * PROW])
        prob_t = sb("prob_t", [P, 2, HPT, QT_N, P])
        near = sb("near", [P, STEPS, BAND])
        near_c = sb("near_c", [P, QT_N, H, REL])
        near_t = sb("near_t", [H * REL, L])
        cn_t = sb("cn_t", [P, CT, L])
        x2 = sb("x2", [P, CT, L])

        a_bank = [ctx.enter_context(nc.psum_tensor(f"a_bank{i}", [P, BANK], F32)) for i in range(2)]
        t_bank = [ctx.enter_context(nc.psum_tensor(f"t_bank{i}", [P, BANK], F32)) for i in range(2)]
        s_bank = [ctx.enter_context(nc.psum_tensor(f"s_bank{i}", [P, BANK], F32)) for i in range(2)]
        acc = ctx.enter_context(nc.psum_tensor("acc", [P, CT, L], F32))

        first_in = sem("first_in")
        rest_in = sem("rest_in")
        consts = sem("consts")
        bias_scaled = sem("bias_scaled")
        x_loaded = sem("x_loaded")
        c_loaded = sem("c_loaded")
        ckv_done = sem("ckv_done")
        mask_loaded = sem("mask_loaded")
        mask_used = sem("mask_used")
        var_ready = [sem(f"var_ready{i}") for i in range(3)]
        rstd_ready = [sem(f"rstd_ready{i}") for i in range(3)]
        xn_ready = sem("xn_ready")
        xbo_ready = sem("xbo_ready")
        causal_ready = sem("causal_ready")
        nmax_ready = sem("nmax_ready")
        sparse_ready = sem("sparse_ready")
        exps_ready = sem("exps_ready")
        mix_ready = sem("mix_ready")
        qn_ready = sem("qn_ready")
        a_filled = sem("a_filled")
        a_emptied = sem("a_emptied")
        att_filled = sem("att_filled")
        att_emptied = sem("att_emptied")
        t_filled = sem("t_filled")
        t_emptied = sem("t_emptied")
        s_filled = sem("s_filled")
        s_emptied = sem("s_emptied")
        rel_written = sem("rel_written")
        band_loaded = [sem(f"band_loaded{i}") for i in range(2)]
        added_ready = sem("added_ready")
        exp_done = sem("exp_done")
        probs_ready = sem("probs_ready")
        near_written = [sem(f"near_written{i}") for i in range(2)]
        near_loaded = sem("near_loaded")
        near_packed = sem("near_packed")
        acc_done = sem("acc_done")
        acc_emptied = sem("acc_emptied")
        ck_kept = sem("ck_kept")
        x1_kept = sem("x1_kept")
        x2_ready = sem("x2_ready")
        x2_stored = sem("x2_stored")
        x3_ready = sem("x3_ready")
        x3_stored = sem("x3_stored")
        gate = sem("gate")

        weights = [(w_q, w["attn_Wq"]), (w_k, w["attn_Wk"]), (w_v, w["attn_Wv"]), (w_o, w["attn_Wo"]),
                   (cw_q, w["xattn_wqT"]), (cw_k, w["xattn_wkT"]), (cw_v, w["xattn_wvT"]),
                   (cw_o, w["xattn_woT"])]
        columns = [(b_q, w["attn_bq"]), (b_k, w["attn_bk"]), (b_v, w["attn_bv"]),
                   (cb_q, w["xattn_bq"]), (cb_k, w["xattn_bk"]), (cb_v, w["xattn_bv"]),
                   (cb_o, w["xattn_bo"])]
        N_EARLY = 2
        N_FIRST_DMAS = N_EARLY + len(columns)
        N_REST_DMAS = len(weights) - N_EARLY + 1 + HPT + H
        N_CONSTS = 8

        def prob_tile(slot):
            return probs[:, slot * PROW + WIN:slot * PROW + WIN + L]

        def band_on_pe(b):
            return isinstance(b, int) and b >= B - 1

        def window(group):
            first = group % QT_N * P - WIN
            return max(first, 0), min(first + SPAN, L), first

        block = ctx.enter_context(nc.Block())

        @block.sync
        def _(sp):
            for tile, src in columns:
                sp.dma_start(tile[:], src).then_inc(first_in, 16)
            for n, (tile, src) in enumerate(weights):
                sp.dma_start(tile[:], src.rearrange("(k p) n -> p k n", p=P)).then_inc(
                    first_in if n < N_EARLY else rest_in, 16)
            sp.dma_start(b_o[:], w["attn_bo"].partition_broadcast(P)).then_inc(rest_in, 16)
            sp.wait_ge(consts, N_CONSTS)
            for h in range(HPT):
                sp.dma_start(rel_k4[h * HC:(h + 1) * HC, h * REL:(h + 1) * REL],
                             w["rel_kT"]).then_inc(rest_in, 16)
            for h in range(H):
                sp.dma_start(rel_v8[h * REL:(h + 1) * REL, h * HC:(h + 1) * HC],
                             w["rel_v"]).then_inc(rest_in, 16)

            def load_band(n):
                for g in range(P // QUAD):
                    base = g * QUAD * ROW + n * HPT * BAND
                    src = rel_scratch[base:base + QUAD * (ROW - 1)].rearrange("(r c) -> r c", c=ROW - 1)
                    src = src[:, 0:HPT * BAND].rearrange("r (h w) -> r h w", w=BAND)
                    sp.dma_start(band[g * QUAD:(g + 1) * QUAD, n % 2, :, g * QUAD:g * QUAD + BAND],
                                 src).then_inc(band_loaded[n % 2], 16)

            def windows(r):
                wait(sp, near_loaded, r * 64)
                for n in range(GROUPS):
                    if n == (AT_LN3 + 4) // HPT + 1 and not (isinstance(r, int) and r == 0):
                        store(x3_dram, x3, x3_ready, x3_stored, r - 1, CT)
                    sp.wait_ge(probs_ready, r * STEPS + (n + 1) * HPT)
                    for g in range(P // QUAD):
                        src = probs[g * QUAD:(g + 1) * QUAD, (n % 2) * HPT * PROW:(n % 2 + 1) * HPT * PROW]
                        at = (n % QT_N) * P + g * QUAD
                        src = src.rearrange("r (h c) -> r h c", c=PROW)[:, :, at:at + BAND]
                        dst = prob_scratch[g * QUAD * ROW:(g + 1) * QUAD * ROW]
                        dst = dst.rearrange("(r s w) -> r s w", r=QUAD, w=BAND)[:, n * HPT:(n + 1) * HPT, :]
                        sp.dma_start(dst, src).then_inc(near_written[n % 2], 16)
                    if n + 2 < GROUPS:
                        if band_on_pe(r + 1):
                            sp.wait_ge(s_filled, r * S_JOBS + S_SCORE + (n + 1) * HPT)
                        else:
                            sp.wait_ge(added_ready, r * STEPS + (n + 1) * HPT)
                        load_band(n + 2)

            def near_back(r):
                sp.wait_ge(near_written[0], (r + 1) * (GROUPS // 2) * 64)
                sp.wait_ge(near_written[1], (r + 1) * (GROUPS // 2) * 64)
                for g in range(P // QUAD):
                    base = g * QUAD * ROW
                    src = prob_scratch[base:base + QUAD * (ROW + 1)].rearrange("(r c) -> r c", c=ROW + 1)
                    n = ROW - QUAD + 1
                    sp.dma_start(near[g * QUAD:(g + 1) * QUAD, :, :].rearrange("r s w -> r (s w)")[:, 0:n],
                                 src[:, 0:n]).then_inc(near_loaded, 16)

            def relative(b):
                sp.wait_ge(t_emptied, t_job(b, "REL")[1] + 1)
                wait(sp, band_loaded[0], b * (GROUPS // 2) * 64)
                wait(sp, band_loaded[1], b * (GROUPS // 2) * 64)
                sp.dma_start(rel_scratch[0:P * ROW].rearrange("(p n) -> p n", p=P),
                             rel_pad[:].rearrange("p s w -> p (s w)")).then_inc(rel_written, 16)
                sp.wait_ge(rel_written, b * 16 + 16)
                sp.sem_inc(gate, 1)
                load_band(0)
                load_band(1)

            def store(dram, tile, ready, stored, r, per_round=1):
                sp.wait_ge(ready, (r + 1) * per_round)
                sp.sem_inc(gate, 1)
                sp.dma_start(dram[bass.ds(r * S, S), :].rearrange("(t p) n -> p t n", p=P),
                             tile[:]).then_inc(stored, 16)

            def round_(b):
                windows(b - 1)
                near_back(b - 1)
                if not (isinstance(b, int) and b == B):
                    relative(b)
                store(x2_dram, x2, x2_ready, x2_stored, b - 1)

            relative(0)
            round_(1)
            with sp.Fori(2, B - 1) as b:
                round_(b)
            round_(B - 1)
            round_(B)
            store(x3_dram, x3, x3_ready, x3_stored, B - 1, CT)
            sp.wait_ge(x2_stored, B * 16)
            sp.wait_ge(x3_stored, B * 16)

        @block.gpsimd
        def _(pool):
            pool.dma_start(x_in[:], w["x"][0].rearrange("(t p) n -> p t n", p=P)).then_inc(x_loaded, 16)

            def after(ins):
                ins.then_inc(consts, 1)
            nc.gpsimd.memset(ident[:], 0.0)
            nc.gpsimd.drain()
            after(nc.gpsimd.affine_select(out=ident[:], in_=ident[:], compare_op=ALU.not_equal, fill=1.0,
                                          base=0, pattern=[[-1, P]], channel_multiplier=1))
            after(nc.gpsimd.memset(rel_k4[:], 0.0))
            after(nc.gpsimd.memset(rel_v8[:], 0.0))
            after(nc.gpsimd.memset(half[:], -0.5))
            after(nc.gpsimd.memset(zeros[:], 0.0))
            after(nc.gpsimd.memset(rel_pad[:], 0.0))
            after(nc.gpsimd.memset(band[:], 0.0))
            after(nc.gpsimd.memset(probs[:], 0.0))


            def power(moments, rs, which, b):
                pool.wait_ge(var_ready[which], b + 1)
                nc.gpsimd.tensor_tensor(rs[:], moments[:, :, 1], half[:], ALU.pow).then_inc(rstd_ready[which], 1)

            def load_x(b):
                wait(pool, xn_ready, b * TT)
                wait(pool, xbo_ready, b)
                nc.gpsimd.sem_inc(gate, 1)
                pool.dma_start(x_in[:], w["x"][b].rearrange("(t p) n -> p t n", p=P)).then_inc(x_loaded, 16)

            def load_c(b):
                wait(pool, mask_used, b)
                nc.gpsimd.sem_inc(gate, 1)
                pool.dma_start(mask_in[:], w["mask"][b].partition_broadcast(P)).then_inc(mask_loaded, 16)
                wait(pool, ckv_done, b)
                nc.gpsimd.sem_inc(gate, 1)
                pool.dma_start(c_in[:], w["ctx"][b].rearrange("(t p) n -> p t n", p=P)).then_inc(c_loaded, 16)

            def keep_causal(b, t):
                wait(pool, exps_ready, b * TT)
                pool.wait_ge(a_emptied, a_job(b, "RAW", t) + 1)
                nc.gpsimd.sem_inc(gate, 1)
                nc.gpsimd.affine_select(out=causal[:, t, :], in_=raw[:, t, :], compare_op=ALU.is_ge,
                                        fill=NEG, base=t * P, pattern=[[-1, S]],
                                        channel_multiplier=1).then_inc(causal_ready, 1)

            def add_bo(b):
                wait(pool, att_emptied, b * TT)
                pool.wait_ge(x_loaded, b * 16 + 16)
                nc.gpsimd.sem_inc(gate, 1)
                for t in range(TT):
                    ins = nc.gpsimd.tensor_tensor(x_bo[:, t, :], x_in[:, t, :], b_o[:], ALU.add)
                ins.then_inc(xbo_ready, 1)

            def steps(b, beside):
                r = b - 1
                pool.wait_ge(mask_used, b)
                for s in range(STEPS):
                    group, g = divmod(s, HPT)
                    lo, hi, first = window(group)
                    if g == 0:
                        pool.wait_ge(band_loaded[group % 2], (r * (GROUPS // 2) + group // 2 + 1) * 64)
                    wait(pool, s_emptied, r * S_JOBS + S_SCORE + max(s - 1, 0))
                    nc.gpsimd.sem_inc(gate, 1)
                    if g < 2 and group > 0:
                        old_lo, old_hi, _ = window(group - 1)
                        if lo > old_lo:
                            old_hi = min(old_hi, lo)
                        nc.gpsimd.tensor_copy(added[:, s % 2, old_lo:old_hi], mask_add[:, old_lo:old_hi])
                    nc.gpsimd.tensor_tensor(added[:, s % 2, lo:hi], mask_add[:, lo:hi],
                                            band[:, group % 2, g, lo - first:hi - first],
                                            ALU.add).then_inc(added_ready, 1)
                    beside(s)

            def attend(b, s):
                if not (isinstance(b, int) and b == B - 1):
                    if s == AT_LN + TT:
                        power(mom, rstd, 0, b + 1)
                    if 0 <= s - AT_RAW - 2 < TT:
                        keep_causal(b + 1, s - AT_RAW - 2)
                if s == AT_LN2 + TT:
                    power(mom2, rstd2, 1, b)

            def norm_x2(b, s):
                if s == AT_LN3 + TT and not (isinstance(b, int) and b < 2):
                    power(mom3, rstd3, 2, b - 2)

            def beside(b, s):
                attend(b, s)
                norm_x2(b, s)

            def next_loads(b, load=True):
                add_bo(b + 1)
                if load:
                    load_x(b + 2)
                load_c(b + 1)

            def round_(b, load=True):
                steps(b, lambda s: beside(b, s))
                next_loads(b, load)

            load_c(0)
            pool.wait_ge(consts, N_CONSTS)
            power(mom, rstd, 0, 0)
            for t in range(TT):
                keep_causal(0, t)
            pool.wait_ge(rest_in, 16 * N_REST_DMAS)
            add_bo(0)
            load_x(1)
            for s in range(STEPS + 2):
                beside(0, s)
            next_loads(0)
            round_(1)
            with pool.Fori(2, B - 2) as b:
                round_(b)
            round_(B - 2, load=False)
            for s in range(STEPS):
                beside(B - 1, s)
            norm_x2(B, AT_LN3 + TT)
            power(mom3, rstd3, 2, B - 1)

        @block.tensor
        def _(pe):
            pe.wait_ge(consts, N_CONSTS)
            def product(out, lhs, rhs, k_tiles):
                for k in range(k_tiles):
                    ins = nc.tensor.matmul(out, lhs(k), rhs(k), start=(k == 0), stop=(k == k_tiles - 1))
                return ins

            def t_open(b, kind, n=0):
                bank, before = t_job(b, kind, n)
                wait(pe, t_emptied, before - 1)
                return t_bank[bank]

            def t_evacuated(b, kind, n):
                pe.wait_ge(t_emptied, t_job(b, kind, n)[1] + 1)

            def a_open(b, kind, n):
                before = a_job(b, kind, n)
                wait(pe, a_emptied, before - 1)
                return a_bank[n % 2]

            def a_evacuated(b, kind, n):
                pe.wait_ge(a_emptied, a_job(b, kind, n) + 1)

            def attend_first(b, s):
                if s == AT_XN:
                    for t in range(TT):
                        bank = a_open(b, "XN", t)
                        pe.wait_ge(xn_ready, b * TT + t + 1)
                        for k in range(KD):
                            ins = nc.tensor.transpose(bank[:, k * P:(k + 1) * P], xn[:, t, k * P:(k + 1) * P],
                                                      ident[:])
                        ins.then_inc(a_filled, 1)
                for kind, at, wt in (("Q", AT_Q, w_q), ("K", AT_K, w_k)):
                    if s in (at, at + 2):
                        m2 = (s - at) // 2
                        a_evacuated(b, "XN", TT - 1)
                        bank = a_open(b, kind, m2)
                        for j in range(2):
                            m = 2 * m2 + j
                            ins = product(bank[:, j * S:(j + 1) * S], lambda k: wt[:, k, m * P:(m + 1) * P],
                                          lambda k: xn_t[:, k, :], KD)
                        ins.then_inc(a_filled, 1)
                if 0 <= s - AT_RAW < TT:
                    t = s - AT_RAW
                    a_evacuated(b, "K", KD // 2 - 1)
                    bank = a_open(b, "RAW", t)
                    product(bank[:, 0:S], lambda k: q_t[:, k, t * P:(t + 1) * P], lambda k: k_t[:, k, :],
                            KD).then_inc(a_filled, 1)
                if 0 <= s - AT_V < TT:
                    t = s - AT_V
                    wait(pe, att_emptied, b * TT)
                    bank = a_open(b, "V", t)
                    product(bank[:, 0:D], lambda k: xn_t[:, k, t * P:(t + 1) * P], lambda k: w_v[:, k, :],
                            KD).then_inc(a_filled, 1)

            def attend_second(b, s):
                if s in AT_CK:
                    o = AT_CK.index(s)
                    if o == 0:
                        pe.wait_ge(c_loaded, 16 * b + 16)
                    bank = t_open(b, "CK", o)
                    product(bank[:, 0:L], lambda k: cw_k[:, k, o * P:(o + 1) * P], lambda k: c_in[:, k, :],
                            CT).then_inc(t_filled, 1)
                if s in AT_CQ:
                    o = AT_CQ.index(s)
                    if o == 0:
                        pe.wait_ge(qn_ready, (b + 1) * TT)
                    bank = t_open(b, "CQ", o)
                    product(bank[:, 0:L], lambda k: cw_q[:, k, o * P:(o + 1) * P], lambda k: qn[:, k, :],
                            CT).then_inc(t_filled, 1)
                if s == AT_WT:
                    for t in range(TT):
                        bank = a_open(b, "WT", t)
                        pe.wait_ge(mix_ready, b * TT + t + 1)
                        for k in range(TT):
                            ins = nc.tensor.transpose(bank[:, k * P:(k + 1) * P], mix[:, t, k * P:(k + 1) * P],
                                                      ident[:])
                        ins.then_inc(a_filled, 1)
                if 0 <= s - AT_OT < 2:
                    m2 = s - AT_OT
                    a_evacuated(b, "WT", TT - 1)
                    bank = a_open(b, "OT", m2)
                    for j in range(2):
                        m = 2 * m2 + j
                        ins = product(bank[:, j * S:(j + 1) * S], lambda k: v[:, k, m * P:(m + 1) * P],
                                      lambda k: mix_t[:, k, :], TT)
                    ins.then_inc(a_filled, 1)
                if 0 <= s - AT_ATT < TT:
                    t = s - AT_ATT
                    a_evacuated(b, "OT", 1)
                    product(a_bank[t][:, 0:D], lambda k: o_t[:, k, t * P:(t + 1) * P],
                            lambda k: w_o[:, k, :], KD).then_inc(att_filled, 1)

            def score(r, n, band_here):
                group, g = divmod(n, HPT)
                o, t = divmod(group, QT_N)
                wait(pe, s_emptied, r * S_JOBS + max(n - 1, 0))
                bank = s_bank[n % 2]
                ins = nc.tensor.matmul(bank[:, 0:L], cq[g * HC:(g + 1) * HC, o, t * P:(t + 1) * P],
                                       ck[g * HC:(g + 1) * HC, o, :], start=True, stop=not band_here,
                                       skip_group_check=True)
                if band_here:
                    if g == 0:
                        pe.wait_ge(band_loaded[group % 2], (r * (GROUPS // 2) + group // 2 + 1) * 64)
                    lo, hi, first = window(group)
                    ins = nc.tensor.matmul(bank[:, lo:hi], ident[:], band[:, group % 2, g, lo - first:hi - first],
                                           start=False, stop=True, skip_group_check=True)
                ins.then_inc(s_filled, 1)

            def turn(r, n):
                bank = t_open(r + 1, "PT", n)
                pe.wait_ge(probs_ready, r * STEPS + n + 1)
                src = prob_tile(n % PSLOTS)
                for k in range(QT_N):
                    ins = nc.tensor.transpose(bank[:, k * P:(k + 1) * P], src[:, k * P:(k + 1) * P], ident[:])
                ins.then_inc(t_filled, 1)

            def weigh(r, n):
                o, t = divmod(n, QT_N)
                t_evacuated(r + 1, "PT", (n + 1) * HPT - 1)
                for k in range(QT_N):
                    for g in range(HPT):
                        h = o * HPT + g
                        nc.tensor.matmul(acc[g * HC:(g + 1) * HC, o, t * P:(t + 1) * P],
                                         cv[:, k, h * HC:(h + 1) * HC], prob_t[:, n % 2, g, k, :],
                                         start=False, stop=False, skip_group_check=True)

            def steps(b, beside):
                r = b - 1
                wait(pe, acc_emptied, r)
                pe.wait_ge(ck_kept, b)
                for o in range(CT):
                    nc.tensor.matmul(acc[:, o, :], zeros[:, 0:P], zeros[:], start=True, stop=False,
                                     skip_group_check=True)
                for s in range(STEPS + 4):
                    if s < STEPS:
                        score(r, s, band_here=band_on_pe(b))
                    if 3 <= s < STEPS + 3:
                        turn(r, s - 3)
                    if s >= HPT + 3 and (s - 3) % HPT == 0:
                        weigh(r, (s - 3) // HPT - 1)
                    beside(s)

            def project(b):
                def values(s2):
                    bank = t_open(b, "CV", s2)
                    for j in range(2):
                        s = 2 * s2 + j
                        ins = product(bank[:, j * C:(j + 1) * C], lambda k: c_in[:, k, s * P:(s + 1) * P],
                                      lambda k: cw_v[:, k, :], CT)
                    ins.then_inc(t_filled, 1)

                values(0)
                t_evacuated(b, "CQ", CT - 1)
                bank = t_open(b, "REL")
                n = HPT * REL
                for o in range(CT):
                    for t in range(QT_N):
                        at = (o * QT_N + t) * n
                        ins = nc.tensor.matmul(bank[:, at:at + n], cq[:, o, t * P:(t + 1) * P], rel_k4[:],
                                               start=True, stop=True)
                ins.then_inc(t_filled, 1)
                values(1)

            def finish(b):
                r = b - 1
                bank = t_open(b, "PB")
                pe.wait_ge(near_packed, r + 1)
                for t in range(QT_N):
                    ins = nc.tensor.transpose(bank[0:H * REL, t * P:(t + 1) * P],
                                              near_c[:, t, :, :].rearrange("p h j -> p (h j)"), ident[:])
                ins.then_inc(t_filled, 1)
                t_evacuated(b, "PB", 0)
                for o in range(CT):
                    ins = nc.tensor.matmul(acc[:, o, :], rel_v8[:, o * P:(o + 1) * P], near_t[:],
                                           start=False, stop=True, skip_group_check=True)
                ins.then_inc(acc_done, 1)
                pe.wait_ge(acc_emptied, r + 1)
                for o in range(CT):
                    wait(pe, s_emptied, r * S_JOBS + S_OUT + o - 1)
                    product(s_bank[(S_OUT + o) % 2][:, 0:L], lambda k: cw_o[:, k, o * P:(o + 1) * P],
                            lambda k: cn_t[:, k, :], CT).then_inc(s_filled, 1)

            def beside(b, s):
                attend_second(b, s)
                if not (isinstance(b, int) and b == B - 1):
                    attend_first(b + 1, s)

            def round_(b):
                steps(b, lambda s: beside(b, s))
                project(b)
                finish(b)

            for s in range(STEPS):
                if s == AT_Q:
                    pe.wait_ge(first_in, 16 * N_FIRST_DMAS)
                if s == AT_V:
                    pe.wait_ge(rest_in, 16 * N_REST_DMAS)
                attend_first(0, s)
            for s in range(STEPS + 2):
                beside(0, s)
            project(0)
            round_(1)
            with pe.Fori(2, B - 1) as b:
                round_(b)
            round_(B - 1)
            steps(B, lambda s: None)
            finish(B)

        @block.scalar
        def _(act):
            act.wait_ge(first_in, 16 * N_FIRST_DMAS)
            act.wait_ge(consts, N_CONSTS)
            nc.scalar.mul(cb_qs[:], cb_q[:], XSCALE)
            self_wait(act)
            def t_full(b, kind, n=0):
                bank, before = t_job(b, kind, n)
                act.wait_ge(t_filled, before + 1)
                return t_bank[bank]

            def a_full(b, kind, n):
                act.wait_ge(a_filled, a_job(b, kind, n) + 1)
                return a_bank[n % 2]

            def attend_first(b, s):
                if s == AT_XN:
                    for t in range(TT):
                        bank = a_full(b, "XN", t)
                        nc.scalar.copy(xn_t[:, :, t * P:(t + 1) * P],
                                       bank[:].rearrange("p (k n) -> p k n", k=KD)).then_inc(a_emptied, 1)
                for kind, at, dst, bias in (("Q", AT_Q, q_t, b_q), ("K", AT_K, k_t, b_k)):
                    if s in (at, at + 2):
                        m2 = (s - at) // 2
                        bank = a_full(b, kind, m2)
                        for j in range(2):
                            m = 2 * m2 + j
                            ins = nc.scalar.activation(dst[:, m, :], bank[:, j * S:(j + 1) * S], ACT.Identity,
                                                       bias=bias[:, m:m + 1])
                        ins.then_inc(a_emptied, 1)
                if 0 <= s - AT_RAW < TT:
                    t = s - AT_RAW
                    bank = a_full(b, "RAW", t)
                    nc.scalar.mul(raw[:, t, :], bank[:, 0:S], SCALE).then_inc(a_emptied, 1)
                if 0 <= s - AT_V < TT:
                    t = s - AT_V
                    bank = a_full(b, "V", t)
                    nc.scalar.copy(v[:, t, :], bank[:, 0:D]).then_inc(a_emptied, 1)

            def attend_second(b, s):
                for o, at in enumerate(AT_CK):
                    if s == at - (0 if isinstance(b, int) and b == 0 else 1):
                        bank = t_full(b, "CK", o)
                        nc.scalar.activation(ck_next[:, o, :], bank[:, 0:L], ACT.Identity,
                                             bias=cb_k[:, o:o + 1]).then_inc(t_emptied, 1)
                for o, at in enumerate(AT_CQ):
                    if s == at - (0 if isinstance(b, int) and b == 0 else 1):
                        bank = t_full(b, "CQ", o)
                        nc.scalar.activation(cq[:, o, :], bank[:, 0:L], ACT.Identity, bias=cb_qs[:, o:o + 1],
                                             scale=XSCALE).then_inc(t_emptied, 1)
                if s in (AT_TOP + 4, AT_TOP + 6):
                    t = (s - AT_TOP - 4) // 2
                    act.wait_ge(nmax_ready, b * TT + t + 1)
                    nc.scalar.activation(e_w[:, t, :], causal[:, t, :], ACT.Exp, bias=nmax[:, t, 0:1],
                                         accum_out=sums[:, t, 0:1])
                    nc.scalar.activation(e_c[:, t, :], csum[:, t, :], ACT.Exp, bias=nmax[:, t, 1:2],
                                         scale=1.0 / COMP, accum_out=sums[:, t, 1:2])
                if s == AT_SPARSE + 1:
                    for t in range(TT):
                        act.wait_ge(sparse_ready, b * TT + t + 1)
                        nc.scalar.activation(e_s[:, t, :], left[:, t, :], ACT.Exp, bias=nmax[:, t, 2:3],
                                             accum_out=sums[:, t, 2:3]).then_inc(exps_ready, 1)
                if s == AT_WT:
                    for t in range(TT):
                        bank = a_full(b, "WT", t)
                        nc.scalar.copy(mix_t[:, :, t * P:(t + 1) * P],
                                       bank[:, 0:S].rearrange("p (k n) -> p k n", k=TT)).then_inc(a_emptied, 1)
                if 0 <= s - AT_OT < 2:
                    m2 = s - AT_OT
                    bank = a_full(b, "OT", m2)
                    for j in range(2):
                        m = 2 * m2 + j
                        ins = nc.scalar.activation(o_t[:, m, :], bank[:, j * S:(j + 1) * S], ACT.Identity,
                                                   bias=b_v[:, m:m + 1])
                    ins.then_inc(a_emptied, 1)

            def steps(b, beside):
                r = b - 1
                for s in range(STEPS + 4):
                    if s < STEPS:
                        group = s // HPT
                        act.wait_ge(s_emptied, r * S_JOBS + S_SCORE + s + 1)
                        if s % HPT == 0:
                            wait(act, near_written[group % 2], (r * (GROUPS // 2) + group // 2) * 64)
                        nc.scalar.activation(prob_tile(s % PSLOTS), scores[:, s % 2, :], ACT.Exp,
                                             bias=nmx[:, s:s + 1], scale=-1.0,
                                             accum_out=lsum[:, s:s + 1]).then_inc(exp_done, 1)
                    if 2 <= s < STEPS + 2:
                        group, g = divmod(s - 2, HPT)
                        bank = t_full(b, "PT", s - 2)
                        nc.scalar.copy(prob_t[:, group % 2, g, :, :].rearrange("p k q -> p (k q)"),
                                       bank[:]).then_inc(t_emptied, 1)
                    beside(s)
                    if s == 1:
                        wait(act, x2_ready, b - 1)
                        act.wait_ge(qn_ready, b * TT)
                        nc.scalar.copy(x1_prev[:], x1[:]).then_inc(x1_kept, 1)

            def keep_keys(b):
                act.wait_ge(t_emptied, t_job(b, "CK", CT - 1)[1] + 1)
                nc.scalar.copy(ck[:], ck_next[:]).then_inc(ck_kept, 1)

            def project(b):

                def values(s2):
                    bank = t_full(b, "CV", s2)
                    ins = nc.scalar.copy(cv[:, 2 * s2:2 * s2 + 2, :], bank[:].rearrange("p (s c) -> p s c", s=2))
                    ins.then_inc(t_emptied, 1)

                values(0)
                bank = t_full(b, "REL")
                wait(act, rel_written, b * 16)
                nc.scalar.copy(rel_pad[:, :, 0:REL],
                               bank[:, 0:STEPS * REL].rearrange("p (s j) -> p s j", j=REL)).then_inc(t_emptied, 1)
                values(1)
                act.sem_inc(ckv_done, 1)

            def finish(b):
                bank = t_full(b, "PB")
                nc.scalar.copy(near_t[:], bank[0:H * REL, :]).then_inc(t_emptied, 1)
                act.wait_ge(acc_done, b)
                for o in range(CT):
                    ins = nc.scalar.activation(cn_t[:, o, :], acc[:, o, :], ACT.Identity, bias=cb_v[:, o:o + 1])
                ins.then_inc(acc_emptied, 1)

            def beside(b, s):
                attend_second(b, s)
                if not (isinstance(b, int) and b == B - 1):
                    attend_first(b + 1, s)

            def round_(b):
                steps(b, lambda s: beside(b, s))
                keep_keys(b)
                project(b)
                finish(b)

            for s in range(STEPS):
                attend_first(0, s)
            for s in range(STEPS + 2):
                beside(0, s)
            keep_keys(0)
            project(0)
            round_(1)
            with act.Fori(2, B - 1) as b:
                round_(b)
            round_(B - 1)
            steps(B, lambda s: None)
            finish(B)

        @block.vector
        def _(dve):
            for j, share in enumerate((3.0, 3.0 * COMP, 3.0)):
                nc.vector.memset(shares[:, j:j + 1], share)
            self_wait(dve)
            def normalise(dst, src, moments, rs, ready, tiles=range(TT)):
                for t in tiles:
                    nc.vector.tensor_scalar(dst[:, t, :], src[:, t, :], moments[:, t, 0:1],
                                            rs[:, t:t + 1], ALU.subtract, ALU.mult).then_inc(ready, 1)

            def attend_first(b, s):
                if 0 <= s - AT_LN < TT:
                    if s == AT_LN:
                        dve.wait_ge(x_loaded, 16 * b + 16)
                    layer_norm_stats(nc, dve, x_in, stats, mom, TT, var_ready[0], only=s - AT_LN)
                if 0 <= s - AT_LN - 3 < TT:
                    dve.wait_ge(rstd_ready[0], b + 1)
                    normalise(xn, x_in, mom, rstd, xn_ready, [s - AT_LN - 3])
                if 0 <= s - AT_MAX < TT:
                    t = s - AT_MAX
                    dve.wait_ge(a_emptied, a_job(b, "RAW", t) + 1)
                    nc.vector.tensor_reduce(csum[:, t, :], raw[:, t, :].rearrange("p (s c) -> p s c", c=COMP),
                                            AX.X, ALU.add)
                    self_wait(dve)
                    nc.vector.tensor_reduce(nmax[:, t, 1:2], csum[:, t, :], AX.X, ALU.max, negate=True)
                    self_wait(dve)
                    nc.vector.tensor_scalar(nmax[:, t, 1:2], nmax[:, t, 1:2], 1.0 / COMP, None, ALU.mult)
                    dve.wait_ge(causal_ready, b * TT + t + 1)
                    nc.vector.tensor_reduce(nmax[:, t, 0:1], causal[:, t, :], AX.X, ALU.max,
                                            negate=True).then_inc(nmax_ready, 1)

            def attend_second(b, s):
                if AT_TOP <= s < AT_SPARSE:
                    turn, t = divmod(s - AT_TOP, TT)
                    src = raw if turn == 0 else left
                    nc.vector.max(best[:, t, :], src[:, t, :])
                    self_wait(dve)
                    if turn == 0:
                        nc.vector.tensor_scalar(nmax[:, t, 2:3], best[:, t, 0:1], 0.0, -1.0, ALU.max, ALU.mult)
                    nc.vector.match_replace(left[:, t, :], best[:, t, :], src[:, t, :], NEG)
                    self_wait(dve)
                if s == AT_SPARSE:
                    for t in range(TT):
                        nc.vector.scalar_tensor_tensor(out=left[:, t, :], in0=left[:, t, :], scalar=NEG,
                                                       in1=raw[:, t, :], op0=ALU.is_equal,
                                                       op1=ALU.mult).then_inc(sparse_ready, 1)
                if s == AT_MIX:
                    for t in range(TT):
                        dve.wait_ge(exps_ready, b * TT + t + 1)
                        nc.vector.tensor_tensor(rsum[:, t, :], sums[:, t, :], shares[:], ALU.mult)
                    self_wait(dve)
                    for t in range(TT):
                        nc.vector.reciprocal(rsum[:, t, :], rsum[:, t, :])
                    self_wait(dve)
                    for t in range(TT):
                        nc.vector.tensor_scalar(mix[:, t, :], e_w[:, t, :], rsum[:, t, 0:1], None, ALU.mult)
                    self_wait(dve)
                if s == AT_MIX + 1:
                    for t in range(TT):
                        nc.vector.scalar_tensor_tensor(out=mix[:, t, :], in0=e_s[:, t, :],
                                                       scalar=rsum[:, t, 2:3], in1=mix[:, t, :],
                                                       op0=ALU.mult, op1=ALU.add)
                    self_wait(dve)
                if s == AT_MIX + 2:
                    for t in range(TT):
                        groups = mix[:, t, :].rearrange("p (s c) -> p s c", c=COMP)
                        nc.vector.scalar_tensor_tensor(
                            out=groups, in0=e_c[:, t, :].unsqueeze(2).to_broadcast([P, S // COMP, COMP]),
                            scalar=rsum[:, t, 1:2], in1=groups, op0=ALU.mult,
                            op1=ALU.add).then_inc(mix_ready, 1)
                if 0 <= s - AT_LN2 < TT:
                    t = s - AT_LN2
                    if t == 0:
                        dve.wait_ge(xbo_ready, b + 1)
                        wait(dve, x1_kept, b)
                    dve.wait_ge(att_filled, b * TT + t + 1)
                    nc.vector.tensor_tensor(x1[:, t, :], a_bank[t][:, 0:D], x_bo[:, t, :],
                                            ALU.add).then_inc(att_emptied, 1)
                    self_wait(dve)
                    layer_norm_stats(nc, dve, x1, stats2, mom2, TT, var_ready[1], only=t)
                if s == AT_LN2 + 3:
                    dve.wait_ge(rstd_ready[1], b + 1)
                    normalise(qn, x1, mom2, rstd2, qn_ready)

            def steps(b, beside):
                r = b - 1
                dve.wait_ge(mask_used, b)
                for s in range(STEPS + 1):
                    if s < STEPS:
                        dve.wait_ge(s_filled, r * S_JOBS + S_SCORE + s + 1)
                        if not band_on_pe(b):
                            dve.wait_ge(added_ready, r * STEPS + s + 1)
                        wait(dve, exp_done, r * STEPS + max(s - 1, 0))
                        dve.sem_inc(gate, 1)
                        nc.vector.tensor_tensor_reduce(
                            out=scores[:, s % 2, :], in0=s_bank[(S_SCORE + s) % 2][:, 0:L],
                            in1=mask_add[:] if band_on_pe(b) else added[:, s % 2, :],
                            scale=-1.0, scalar=-NEG, op0=ALU.add, op1=ALU.min,
                            accum_out=nmx[:, s:s + 1]).then_inc(s_emptied, 1)
                    if 1 <= s <= STEPS:
                        n = s - 1
                        dve.wait_ge(exp_done, r * STEPS + n + 1)
                        nc.vector.reciprocal(linv[:, n:n + 1], lsum[:, n:n + 1])
                        self_wait(dve)
                        nc.vector.tensor_scalar(prob_tile(n % PSLOTS), prob_tile(n % PSLOTS), linv[:, n:n + 1],
                                                None, ALU.mult).then_inc(probs_ready, 1)
                    if 0 <= s - AT_LN3 < TT and not (isinstance(b, int) and b == 1):
                        layer_norm_stats(nc, dve, x2, stats3, mom3, TT, var_ready[2], only=s - AT_LN3)
                    if s == AT_LN3 + 3 and not (isinstance(b, int) and b == 1):
                        normalise_x2(b - 2)
                    beside(s)

            def normalise_x2(r):
                dve.wait_ge(rstd_ready[2], r + 1)
                wait(dve, x3_stored, 16 * r)
                normalise(x3, x2, mom3, rstd3, x3_ready)

            def masks(b):
                self_wait(dve)
                dve.wait_ge(mask_loaded, 16 * b + 16)
                for tile in (mask_add[:], added[:, 0, :], added[:, 1, :]):
                    ins = nc.vector.tensor_scalar(tile, mask_in[:], 0.0, NEG, ALU.is_equal, ALU.mult)
                ins.then_inc(mask_used, 1)

            def finish(b):
                r = b - 1
                dve.wait_ge(near_loaded, r * 64 + 64)
                for o in range(CT):
                    ins = nc.vector.tensor_copy(
                        near_c[:, :, o * HPT:(o + 1) * HPT, :],
                        near[:].rearrange("p (o t h) w -> p o t h w", o=CT, h=HPT)[:, o, :, :, 0:REL])
                ins.then_inc(near_packed, 1)
                wait(dve, x2_stored, 16 * r)
                for o in range(CT):
                    dve.wait_ge(s_filled, r * S_JOBS + S_OUT + o + 1)
                    nc.vector.scalar_tensor_tensor(out=x2[:, o, :], in0=s_bank[(S_OUT + o) % 2][:, 0:L],
                                                   scalar=cb_o[:, o:o + 1], in1=x1_prev[:, o, :], op0=ALU.add,
                                                   op1=ALU.add).then_inc(s_emptied, 1)
                dve.wait_ge(s_emptied, (r + 1) * S_JOBS)
                dve.sem_inc(x2_ready, 1)

            def beside(b, s):
                attend_second(b, s)
                if not (isinstance(b, int) and b == B - 1):
                    attend_first(b + 1, s)

            def round_(b):
                steps(b, lambda s: beside(b, s))
                masks(b)
                finish(b)

            for s in range(STEPS):
                attend_first(0, s)
            dve.wait_ge(first_in, 16 * N_FIRST_DMAS)
            for s in range(STEPS + 2):
                beside(0, s)
            masks(0)
            round_(1)
            round_(2)
            with dve.Fori(3, B - 1) as b:
                round_(b)
            round_(B - 1)
            steps(B, lambda s: None)
            finish(B)
            layer_norm_stats(nc, dve, x2, stats3, mom3, TT, var_ready[2])
            normalise_x2(B - 1)


def expert_pass(nc, w, x2_dram, x3_dram, out):
    N, D = x2_dram.shape
    ROUNDS = N // P
    KD = D // P
    HEADS, KEYS = 8, P
    PH = 2 * HEADS
    DK = w["ffn_Wq"].shape[0] // PH
    KT = DK // P
    E = w["in_a"].shape[0]
    F = w["ffn_W_inT"].shape[1]
    KF = F // P
    SIMS = PH * KEYS
    CHUNKS = SIMS // BANK
    PER = BANK // KEYS
    HALVES = F // BANK
    SLOTS = HEADS
    VE_HEADS = range(6)
    PE_HEADS = range(6, HEADS)
    assert KEYS * KEYS >= E and DK % P == 0

    with ExitStack() as ctx:
        def sb(name, shape, dt=F32):
            return ctx.enter_context(nc.sbuf_tensor(name, shape, dt))

        def pb(name, shape):
            return ctx.enter_context(nc.psum_tensor(name, shape, F32))

        def sem(name):
            return ctx.enter_context(nc.semaphore(name))

        ident = sb("ident_f", [P, P])
        fold = sb("fold", [P, KD, SIMS])
        w_in = sb("w_in", [P, KD, F])
        w_out = sb("w_out", [P, KF, D])
        xn_pe = sb("xn_pe", [P, D])
        xn_ve = sb("xn_ve", [P, D])
        x_res = sb("x_res", [P, D])
        xn_t = sb("xn_tf", [P, KD, P])
        xn_kept = sb("xn_kept", [P, KD, P])
        sims = sb("sims", [P, SIMS])
        top = sb("top", [P, PH, 8])
        place = sb("place", [P, PH, 8], U32)
        row_f = sb("row_f", [P, HEADS])
        rows = sb("rows", [P, HEADS], U32)
        rows_now = sb("rows_now", [P, 2, HEADS], U32)
        score = sb("score", [P, HEADS])
        gates = sb("gates", [P, HEADS])
        gates_1 = sb("gates_1", [P, HEADS])
        gates_2 = sb("gates_2", [P, HEADS])
        lin = sb("lin", [P, HEADS])
        lout = sb("lout", [P, HEADS])
        in_a = sb("in_a_rows", [P, HEADS, D])
        in_b = sb("in_b_rows", [P, HEADS, F])
        out_a = sb("out_a_rows", [P, HEADS, F])
        out_b = sb("out_b_rows", [P, HEADS, D])
        wq_in = out_a[:].rearrange("p g (k n) -> p g k n", k=KT)
        keys_in = out_b[:, :, 0:KT * KEYS].rearrange("p g (k n) -> p g k n", k=KT)
        diag = sb("diag", [P, len(PE_HEADS), P])
        hid = sb("hid", [P, F])
        hid_t = sb("hid_t", [P, KF, P])
        res = sb("res", [P, D])

        x_bank = pb("x_bank", [P, BANK])
        l_bank = [pb(f"l_bank{i}", [P, BANK]) for i in range(2)]
        h_bank = [pb(f"h_bank{i}", [P, BANK]) for i in range(KF * P // BANK)]
        hid_ps = pb("hid_ps", [P, F])
        out_ps = pb("out_ps", [P, D])

        ident_ready = sem("ident_ready")
        ident_zeroed = sem("ident_zeroed")
        w_loaded = sem("w_loaded")
        wq_loaded = [sem(f"wq_loaded{i}") for i in range(SLOTS)]
        fold_filled = sem("fold_filled")
        fold_emptied = sem("fold_emptied")
        xpe_loaded = sem("xpe_loaded")
        xve_loaded = sem("xve_loaded")
        xres_loaded = sem("xres_loaded")
        xt_filled = sem("xt_filled")
        xt_emptied = sem("xt_emptied")
        kept = sem("kept")
        sims_filled = sem("sims_filled")
        sims_emptied = sem("sims_emptied")
        picked = sem("picked")
        rows_taken = sem("rows_taken")
        in_a_loaded = [sem(f"in_a_loaded{i}") for i in range(HEADS)]
        in_b_loaded = [sem(f"in_b_loaded{i}") for i in range(HEADS)]
        out_a_loaded = [sem(f"out_a_loaded{i}") for i in range(HEADS)]
        out_b_loaded = [sem(f"out_b_loaded{i}") for i in range(HEADS)]
        in_a_used = sem("in_a_used")
        out_a_used = sem("out_a_used")
        out_b_used = sem("out_b_used")
        lin_ready = sem("lin_ready")
        diag_ready = sem("diag_ready")
        win_done = sem("win_done")
        hid_filled = sem("hid_filled")
        hid_summed = sem("hid_summed")
        gelu_done = sem("gelu_done")
        ht_filled = sem("ht_filled")
        ht_emptied = sem("ht_emptied")
        out_filled = sem("out_filled")
        res_ready = sem("res_ready")
        res_stored = sem("res_stored")
        gate = sem("gate_f")

        def rounds(front, keep, back, eng):
            def beside(r, within):
                keep(r + 1)
                front(r + 2, within)

            def keep_only(within):
                keep(ROUNDS - 1)
                within()

            front(0)
            keep(0)
            front(1)
            back(0, lambda within=nothing: beside(0, within))
            with eng.Fori(1, ROUNDS - 2) as r:
                back(r, lambda within=nothing: beside(r, within))
            back(ROUNDS - 2, lambda within=nothing: keep_only(within))
            back(ROUNDS - 1, lambda within=nothing: within())

        def nothing(*_):
            pass

        block = ctx.enter_context(nc.Block())

        @block.sync
        def _(sp):
            def tokens(dram, r):
                return dram[bass.ds(r * P, P), :]

            def load_front(r):
                wait(sp, xt_filled, r)
                sp.sem_inc(gate, 1)
                sp.dma_start(xn_pe[:], tokens(x3_dram, r)).then_inc(xpe_loaded, 16)

            def load_products(r):
                wait(sp, in_a_used, r * HEADS)
                sp.sem_inc(gate, 1)
                sp.dma_start(xn_ve[:], tokens(x3_dram, r)).then_inc(xve_loaded, 16)

            def load_residual(r):
                wait(sp, res_ready, r)
                sp.sem_inc(gate, 1)
                sp.dma_start(x_res[:], tokens(x2_dram, r)).then_inc(xres_loaded, 16)

            def store(r):
                sp.dma_start(tokens(out, r), res[:]).then_inc(res_stored, 16)

            def round_(r, ahead=True):
                load_products(r + 1)
                if ahead:
                    load_front(r + 3)
                load_residual(r + 1)
                store(r)

            load_front(0)
            load_products(0)
            load_residual(0)
            wq_v = w["ffn_Wq"].rearrange("(g k p) n -> g p k n", k=KT, p=P)
            keys_v = w["ffn_keysT"].rearrange("(g k p) n -> g p k n", k=KT, p=P)
            for g in range(PH):
                wait(sp, fold_filled, g - SLOTS + 1)
                sp.dma_start(wq_in[:, g % SLOTS, :, :], wq_v[g]).then_inc(wq_loaded[g % SLOTS], 16)
                sp.dma_start(keys_in[:, g % SLOTS, :, :], keys_v[g]).then_inc(wq_loaded[g % SLOTS], 16)
            sp.dma_start(w_in[:], w["ffn_W_inT"].rearrange("(k p) n -> p k n", p=P)).then_inc(w_loaded, 16)
            sp.dma_start(w_out[:], w["ffn_W_outT"].rearrange("(k p) n -> p k n", p=P)).then_inc(w_loaded, 16)
            load_front(1)
            load_front(2)
            round_(0)
            with sp.Fori(1, ROUNDS - 3) as r:
                round_(r)
            round_(ROUNDS - 3, ahead=False)
            round_(ROUNDS - 2, ahead=False)
            sp.wait_ge(res_ready, ROUNDS)
            store(ROUNDS - 1)
            sp.wait_ge(res_stored, 16 * ROUNDS)

        @block.gpsimd
        def _(pool):
            nc.gpsimd.memset(ident[:], 0.0).then_inc(ident_zeroed, 1)
            pool.wait_ge(ident_zeroed, 1)
            nc.gpsimd.affine_select(out=ident[:], in_=ident[:], compare_op=ALU.not_equal, fill=1.0,
                                    base=0, pattern=[[-1, P]], channel_multiplier=1).then_inc(ident_ready, 1)

            def gathers(r, odd):
                pool.wait_ge(picked, r + 1)
                nc.gpsimd.sem_inc(gate, 1)
                nc.gpsimd.tensor_copy(rows_now[:, odd, :], rows[:]).then_inc(rows_taken, 1)
                pool.wait_ge(rows_taken, r + 1)
                nc.gpsimd.sem_inc(gate, 1)
                for table, dst, loaded, used in (
                        ("in_a", in_a, in_a_loaded, in_a_used), ("in_b", in_b, in_b_loaded, hid_summed),
                        ("out_a", out_a, out_a_loaded, out_a_used), ("out_b", out_b, out_b_loaded, out_b_used)):
                    if table == "out_a":
                        if isinstance(r, int) and r == 0:
                            pool.wait_ge(fold_filled, PH)
                    order = [*PE_HEADS, *VE_HEADS] if table == "in_a" else range(HEADS)
                    for n, h in enumerate(order):
                        wait(pool, used, r if table == "in_b" else (r - 1) * HEADS + n + 1)
                        nc.gpsimd.sem_inc(gate, 1)
                        nc.gpsimd.indirect_dma_start(
                            dst[:, h, :], None, w[table],
                            bass.IndirectOffsetOnAxis(rows_now[:, odd, h:h + 1], 0)).then_inc(loaded[h], 16)

            gathers(0, 0)
            gathers(1, 1)
            with pool.Fori(1, ROUNDS // 2 - 1) as pair:
                gathers(2 * pair, 0)
                gathers(2 * pair + 1, 1)
            gathers(ROUNDS - 2, 0)
            gathers(ROUNDS - 1, 1)

        @block.tensor
        def _(pe):
            pe.wait_ge(ident_ready, 1)
            for g in range(PH):
                pe.wait_ge(wq_loaded[g % SLOTS], 32 * (g // SLOTS + 1))
                wait(pe, fold_emptied, g - 1)
                for i in range(KD):
                    for k in range(KT):
                        ins = nc.tensor.matmul(l_bank[g % 2][:, i * P:(i + 1) * P],
                                               wq_in[:, g % SLOTS, k, i * P:(i + 1) * P], keys_in[:, g % SLOTS, k, :],
                                               start=(k == 0), stop=(k == KT - 1))
                ins.then_inc(fold_filled, 1)
            pe.wait_ge(fold_emptied, PH)

            def front(r, within=nothing):
                pe.wait_ge(xpe_loaded, 16 * r + 16)
                wait(pe, xt_emptied, r)
                for k in range(KD):
                    ins = nc.tensor.transpose(x_bank[:, k * P:(k + 1) * P], xn_pe[:, k * P:(k + 1) * P], ident[:])
                ins.then_inc(xt_filled, 1)
                pe.wait_ge(xt_emptied, r + 1)
                for c in range(CHUNKS):
                    wait(pe, sims_emptied, CHUNKS * r + c - 1)
                    for k in range(KD):
                        ins = nc.tensor.matmul(l_bank[c % 2][:], xn_t[:, k, :], fold[:, k, c * BANK:(c + 1) * BANK],
                                               start=(k == 0), stop=(k == KD - 1))
                    ins.then_inc(sims_filled, 1)
                    if c == 1:
                        within()

            def back(r, beside):
                if isinstance(r, int) and r == 0:
                    pe.wait_ge(w_loaded, 32)
                pe.wait_ge(kept, r + 1)
                wait(pe, gelu_done, r)
                for n in range(HALVES):
                    for k in range(KD):
                        ins = nc.tensor.matmul(hid_ps[:, n * BANK:(n + 1) * BANK], xn_kept[:, k, :],
                                               w_in[:, k, n * BANK:(n + 1) * BANK],
                                               start=(k == 0), stop=False, skip_group_check=True)
                ins.then_inc(win_done, 1)

                def heads_part():
                    pe.wait_ge(diag_ready, r + 1)
                    for i, h in enumerate(PE_HEADS):
                        pe.wait_ge(in_b_loaded[h], 16 * r + 16)
                        for n in range(HALVES):
                            ins = nc.tensor.matmul(hid_ps[:, n * BANK:(n + 1) * BANK], diag[:, i, :],
                                                   in_b[:, h, n * BANK:(n + 1) * BANK], start=False,
                                                   stop=(h == PE_HEADS[-1]), skip_group_check=True)
                    ins.then_inc(hid_filled, 1)

                beside(heads_part)
                pe.wait_ge(gelu_done, r + 1)
                for j, bank in enumerate(h_bank):
                    wait(pe, ht_emptied, len(h_bank) * r)
                    for k in range(PER):
                        at = (j * PER + k) * P
                        ins = nc.tensor.transpose(bank[:, k * P:(k + 1) * P], hid[:, at:at + P], ident[:])
                    ins.then_inc(ht_filled, 1)
                pe.wait_ge(ht_emptied, len(h_bank) * (r + 1))
                wait(pe, res_ready, r)
                for k in range(KF):
                    ins = nc.tensor.matmul(out_ps[:], hid_t[:, k, :], w_out[:, k, :], start=(k == 0),
                                           stop=(k == KF - 1))
                ins.then_inc(out_filled, 1)

            rounds(front, nothing, back, pe)

        @block.scalar
        def _(act):
            for g in range(PH):
                act.wait_ge(fold_filled, g + 1)
                nc.scalar.copy(fold[:, :, g * KEYS:(g + 1) * KEYS],
                               l_bank[g % 2][:].rearrange("p (i n) -> p i n", i=KD)).then_inc(fold_emptied, 1)

            def keep(r):
                wait(act, win_done, r)
                act.wait_ge(xt_emptied, r + 1)
                nc.scalar.copy(xn_kept[:], xn_t[:]).then_inc(kept, 1)

            def front(r, within=nothing):
                wait(act, kept, r)
                act.wait_ge(xt_filled, r + 1)
                nc.scalar.copy(xn_t[:].rearrange("p k n -> p (k n)"), x_bank[:]).then_inc(xt_emptied, 1)
                wait(act, picked, r)
                for c in range(CHUNKS):
                    act.wait_ge(sims_filled, CHUNKS * r + c + 1)
                    nc.scalar.copy(sims[:, c * BANK:(c + 1) * BANK], l_bank[c % 2][:]).then_inc(sims_emptied, 1)
                    if c == 0:
                        within()

            def back(r, beside):
                def diagonals():
                    wait(act, hid_filled, r)
                    act.wait_ge(lin_ready, r + 1)
                    for i, h in enumerate(PE_HEADS):
                        ins = nc.scalar.activation(diag[:, i, :], ident[:], ACT.Copy, scale=lin[:, h:h + 1])
                    ins.then_inc(diag_ready, 1)

                beside(diagonals)
                wait(act, out_a_used, r * HEADS)
                act.wait_ge(hid_summed, r + 1)
                nc.scalar.activation(hid[:], hid_ps[:], ACT.Gelu).then_inc(gelu_done, 1)
                for j, bank in enumerate(h_bank):
                    act.wait_ge(ht_filled, len(h_bank) * r + j + 1)
                    nc.scalar.copy(hid_t[:, j * PER:(j + 1) * PER, :].rearrange("p k n -> p (k n)"),
                                   bank[:]).then_inc(ht_emptied, 1)

            rounds(front, keep, back, act)

        @block.vector
        def _(dve):
            def front(r, within=nothing):
                for c in range(CHUNKS):
                    dve.wait_ge(sims_emptied, CHUNKS * r + c + 1)
                    dve.sem_inc(gate, 1)
                    pairs = range(c * PER, (c + 1) * PER)
                    for g in pairs:
                        nc.vector.max(top[:, g, :], sims[:, g * KEYS:(g + 1) * KEYS])
                    self_wait(dve)
                    for g in pairs:
                        nc.vector.max_index(place[:, g, :], top[:, g, :], sims[:, g * KEYS:(g + 1) * KEYS])
                    if c == 1:
                        within()
                self_wait(dve)
                nc.vector.scalar_tensor_tensor(out=row_f[:], in0=place[:, 0:HEADS, 0], scalar=float(KEYS),
                                               in1=place[:, HEADS:PH, 0], op0=ALU.mult, op1=ALU.add)
                nc.vector.tensor_tensor(score[:], top[:, 0:HEADS, 0], top[:, HEADS:PH, 0], ALU.add)
                self_wait(dve)
                nc.vector.tensor_scalar(gates_2[:], score[:], 0.0, None, ALU.max)
                wait(dve, rows_taken, r)
                nc.vector.tensor_scalar(rows[:], row_f[:], float(E - 1), None, ALU.min).then_inc(picked, 1)

            def keep(r):
                self_wait(dve)
                nc.vector.tensor_copy(gates_1[:], gates_2[:])
                self_wait(dve)

            def back(r, beside):
                nc.vector.tensor_copy(gates[:], gates_1[:])
                dve.wait_ge(xve_loaded, 16 * r + 16)
                for heads in (PE_HEADS, VE_HEADS):
                    for h in heads:
                        dve.wait_ge(in_a_loaded[h], 16 * r + 16)
                        nc.vector.tensor_tensor_reduce(out=in_a[:, h, :], in0=in_a[:, h, :], in1=xn_ve[:],
                                                       scale=1.0, scalar=0.0, op0=ALU.mult, op1=ALU.add,
                                                       accum_out=lin[:, h:h + 1]).then_inc(in_a_used, 1)
                    self_wait(dve)
                    some = slice(heads[0], heads[-1] + 1)
                    ins = nc.vector.tensor_tensor(lin[:, some], lin[:, some], gates[:, some], ALU.mult)
                    if heads is PE_HEADS:
                        ins.then_inc(lin_ready, 1)
                def heads_part():
                    self_wait(dve)
                    dve.wait_ge(hid_filled, r + 1)
                    for h in VE_HEADS:
                        dve.wait_ge(in_b_loaded[h], 16 * r + 16)
                        nc.vector.scalar_tensor_tensor(out=hid_ps[:], in0=in_b[:, h, :], scalar=lin[:, h:h + 1],
                                                       in1=hid_ps[:], op0=ALU.mult, op1=ALU.add)
                        self_wait(dve)
                    dve.sem_inc(hid_summed, 1)

                beside(heads_part)
                dve.wait_ge(gelu_done, r + 1)
                for h in range(HEADS):
                    dve.wait_ge(out_a_loaded[h], 16 * r + 16)
                    nc.vector.tensor_tensor_reduce(out=out_a[:, h, :], in0=out_a[:, h, :], in1=hid[:], scale=1.0,
                                                   scalar=0.0, op0=ALU.mult, op1=ALU.add,
                                                   accum_out=lout[:, h:h + 1]).then_inc(out_a_used, 1)
                self_wait(dve)
                nc.vector.tensor_tensor(lout[:], lout[:], gates[:], ALU.mult)
                self_wait(dve)
                dve.wait_ge(out_filled, r + 1)
                for h in range(HEADS):
                    dve.wait_ge(out_b_loaded[h], 16 * r + 16)
                    nc.vector.scalar_tensor_tensor(out=out_ps[:], in0=out_b[:, h, :], scalar=lout[:, h:h + 1],
                                                   in1=out_ps[:], op0=ALU.mult, op1=ALU.add).then_inc(out_b_used, 1)
                    self_wait(dve)
                dve.wait_ge(xres_loaded, 16 * r + 16)
                wait(dve, res_stored, 16 * r)
                nc.vector.tensor_tensor(res[:], out_ps[:], x_res[:], ALU.add).then_inc(res_ready, 1)

            rounds(front, keep, back, dve)


def decoder_layer(nc, w, out):
    B, S, D = w["x"].shape
    x2_dram = nc.dram_tensor("x2_scratch", [B * S, D], F32, kind="Internal").ap()
    x3_dram = nc.dram_tensor("x3_scratch", [B * S, D], F32, kind="Internal").ap()
    attention_pass(nc, w, x2_dram, x3_dram)
    expert_pass(nc, w, x2_dram, x3_dram, out.rearrange("b s d -> (b s) d"))


def kernel(**inputs):
    import numpy as np
    import concourse.bacc as bacc
    from concourse.bass_utils import run_bass_kernel_spmd

    def columns(name):
        return inputs[name].reshape(-1, 128).T

    arrays = {"x": inputs["x"], "ctx": inputs["ctx_1024"],
              "mask": inputs["mask_Bx1x1024_ff1"].reshape(inputs["x"].shape[0], -1),
              "attn_bo": inputs["L0_attn_bo"], "rel_k": inputs["L0_xattn_rel_k"],
              "rel_kT": inputs["L0_xattn_rel_k"].T, "rel_v": inputs["L0_xattn_rel_v"],
              "ffn_Wq": inputs["L0_ffn_Wq"],
              "ffn_keysT": np.asarray(inputs["L0_ffn_keys"]).transpose(2, 0, 3, 1).reshape(
                  inputs["L0_ffn_Wq"].shape[0], -1),
              "ffn_W_inT": inputs["L0_ffn_W_in"].T, "ffn_W_outT": inputs["L0_ffn_W_out"].T,
              "in_a": inputs["L0_ffn_in_a"], "in_b": inputs["L0_ffn_in_b"],
              "out_a": inputs["L0_ffn_out_a"], "out_b": inputs["L0_ffn_out_b"]}
    for c in "qkvo":
        arrays[f"attn_W{c}"] = inputs[f"L0_attn_W{c}"]
        arrays[f"xattn_w{c}T"] = inputs[f"L0_xattn_w{c}"].T
        arrays[f"xattn_b{c}"] = columns(f"L0_xattn_b{c}")
        if c != "o":
            arrays[f"attn_b{c}"] = columns(f"L0_attn_b{c}")
    arrays = {f"in_{k}_dram": np.ascontiguousarray(a) for k, a in arrays.items()}

    nc = bacc.Bacc("TRN2", target_bir_lowering=False, num_devices=1)
    w = {k[3:-5]: nc.dram_tensor(k, a.shape, mybir.dt.from_np(a.dtype), kind="ExternalInput").ap()
         for k, a in arrays.items()}
    shape = inputs["x"].shape
    out = nc.dram_tensor("out_0_dram", shape, F32, kind="ExternalOutput").ap()
    decoder_layer(nc, w, out)
    return run_bass_kernel_spmd(nc, [arrays], core_ids=[0]).results[0]["out_0_dram"]
```
